# Optimizing a Trainium2 kernel written in Bass

```python
import numpy as np
import jax
import jax.numpy as jnp

def _softmax(x, axis=-1):
    return jax.nn.softmax(x, axis=axis)

def _gelu(x):
    return jax.nn.gelu(x, approximate=True)

def _silu(x):
    return jax.nn.silu(x)

def _sigmoid(x):
    return jax.nn.sigmoid(x)

def _layernorm(x, axis=-1, eps=1e-05):
    m = jnp.mean(x, axis=axis, keepdims=True)
    v = jnp.var(x, axis=axis, keepdims=True)
    return (x - m) / jnp.sqrt(v + eps)

def _scatter_add(tgt, idx, src, axis=0):
    return tgt.at[idx].add(src)

def _segment_sum(src, seg, n):
    return jax.ops.segment_sum(src, seg, n)
kernel_name = 'mk_gnn_resnorm_d4_gnn_r32_5eeaf3'

def setup_inputs(seed: int=0):
    np.random.seed(seed)
    _w = jnp.asarray

    def _rec_inputs():
        import jax
        import jax.numpy as jnp
        _gk = jax.random.key(seed)
        x = -8.776e-05 + 1 * jax.random.normal(jax.random.fold_in(_gk, 1), (625, 256), jnp.float32)
        src = jax.random.randint(jax.random.fold_in(_gk, 2), (20000,), 0, 625, jnp.int32)
        dst = jnp.minimum((625 * jax.random.uniform(jax.random.fold_in(_gk, 3), (20000,)) ** 2.0).astype(jnp.int32), 19999)
        _o = jnp.argsort(dst, stable=True)
        src = src[_o]
        dst = dst[_o]
        return (x, src, dst)
    x, src, dst = _rec_inputs()

    def _L0_gnn_setup():
        import jax, jax.numpy as jnp
        import numpy as np
        N_NODES = 625
        key = jax.random.key(seed)
        k1, k2, k3, k4 = jax.random.split(key, 4)
        d = 256
        E = 10000
        x = jax.random.normal(k1, (N_NODES, d), dtype=jnp.float32)
        edge_index = jax.random.randint(k2, (2, E), 0, N_NODES, dtype=jnp.int64)
        limit = float(np.sqrt(6.0 / (d + d)))
        W_l = jax.random.uniform(k3, (d, d), dtype=jnp.float32, minval=-limit, maxval=limit)
        W_r = jax.random.uniform(k4, (d, d), dtype=jnp.float32, minval=-limit, maxval=limit)
        b_r = jnp.zeros((d,), dtype=jnp.float32)
        return {'x': x, 'edge_index': edge_index, 'W_l': W_l, 'W_r': W_r, 'b_r': b_r}
    _L0_gnn_all = _L0_gnn_setup()
    _L0_gnn_in = {k: v for k, v in _L0_gnn_all.items() if k in ('W_l', 'W_r', 'b_r')}
    del _L0_gnn_all

    def _L1_gnn_setup():
        import jax, jax.numpy as jnp
        import numpy as np
        N = 50000
        E = 25000
        D = 256
        H = 4
        F = D // H

        def gat_layer(x, src, dst, W, att_src, att_dst, bias):
            n = x.shape[0]
            h = (x @ W).reshape(n, H, F)
            a_src = jnp.sum(h * att_src[None], axis=-1)
            a_dst = jnp.sum(h * att_dst[None], axis=-1)
            e = jax.nn.leaky_relu(a_src[src] + a_dst[dst], 0.2)
            m = jax.ops.segment_max(e, dst, num_segments=n)
            m = jnp.where(jnp.isfinite(m), m, 0.0)
            ex = jnp.exp(e - m[dst])
            denom = jax.ops.segment_sum(ex, dst, num_segments=n)
            alpha = ex / (denom[dst] + 1e-16)
            msg = h[src] * alpha[..., None]
            out = jax.ops.segment_sum(msg, dst, num_segments=n)
            return out.reshape(n, H * F) + bias
        key = jax.random.key(seed)
        ks = jax.random.split(key, 8)
        x = jax.random.normal(ks[0], (N, D), dtype=jnp.float32)
        edge_index = jax.random.randint(ks[1], (2, E), 0, N, dtype=jnp.int32)
        W = jax.random.normal(ks[2], (D, H * F), dtype=jnp.float32) * (1.0 / np.sqrt(D))
        att_src = jax.random.normal(ks[3], (H, F), dtype=jnp.float32) * (1.0 / np.sqrt(F))
        att_dst = jax.random.normal(ks[4], (H, F), dtype=jnp.float32) * (1.0 / np.sqrt(F))
        bias = jnp.zeros((D,), dtype=jnp.float32)
        ln_gamma = jnp.ones((D,), dtype=jnp.float32)
        ln_beta = jnp.zeros((D,), dtype=jnp.float32)
        return {'x': x, 'edge_index': edge_index, 'W': W, 'att_src': att_src, 'att_dst': att_dst, 'bias': bias, 'ln_gamma': ln_gamma, 'ln_beta': ln_beta}
    _L1_gnn_all = _L1_gnn_setup()
    _L1_gnn_in = {k: v for k, v in _L1_gnn_all.items() if k in ('W', 'att_src', 'att_dst', 'bias', 'ln_gamma', 'ln_beta')}
    del _L1_gnn_all

    def _L2_gnn_setup():
        import jax, jax.numpy as jnp
        import numpy as np
        N_NODES = 512
        D_FEAT = 256
        N_EDGES = 8192
        HIDDEN = 512
        D_OUT = 256
        key = jax.random.key(seed)
        ks = jax.random.split(key, 5)
        x = jax.random.normal(ks[0], (N_NODES, D_FEAT), dtype=jnp.float32)
        W1 = jax.random.normal(ks[1], (2 * D_FEAT, HIDDEN), dtype=jnp.float32) * (1.0 / np.sqrt(2 * D_FEAT))
        b1 = jnp.zeros((HIDDEN,), dtype=jnp.float32)
        W2 = jax.random.normal(ks[2], (HIDDEN, D_OUT), dtype=jnp.float32) * (1.0 / np.sqrt(HIDDEN))
        b2 = jnp.zeros((D_OUT,), dtype=jnp.float32)
        nn_index = jax.random.randint(ks[3], (2, N_EDGES), 0, N_NODES, dtype=jnp.int64)
        return {'x': x, 'W1': W1, 'b1': b1, 'W2': W2, 'b2': b2, 'nn_index': nn_index, 'k': 16}
    _L2_gnn_all = _L2_gnn_setup()
    _L2_gnn_in = {k: v for k, v in _L2_gnn_all.items() if k in ('W1', 'b1', 'W2', 'b2')}
    del _L2_gnn_all

    def _L3_gnn_setup():
        import jax, jax.numpy as jnp
        import numpy as np
        N, IN_CH, HEADS, OUT_CH, E = (50000, 256, 4, 64, 25000)
        key = jax.random.key(seed)
        k1, k2, k3, k4, k5 = jax.random.split(key, 5)
        x = jax.random.normal(k1, (N, IN_CH), dtype=jnp.float32)
        edge_index = jax.random.randint(k2, (2, E), 0, N, dtype=jnp.int64)
        bw = float(np.sqrt(6.0 / (IN_CH + HEADS * OUT_CH)))
        ba = float(np.sqrt(6.0 / (HEADS + OUT_CH)))
        weight = jax.random.uniform(k3, (IN_CH, HEADS * OUT_CH), jnp.float32, -bw, bw)
        attn_l = jax.random.uniform(k4, (HEADS, OUT_CH), jnp.float32, -ba, ba)
        attn_r = jax.random.uniform(k5, (HEADS, OUT_CH), jnp.float32, -ba, ba)
        return {'x': x, 'edge_index': edge_index, 'weight': weight, 'attn_l': attn_l, 'attn_r': attn_r}
    _L3_gnn_all = _L3_gnn_setup()
    _L3_gnn_in = {k: v for k, v in _L3_gnn_all.items() if k in ('weight', 'attn_l', 'attn_r')}
    del _L3_gnn_all
    return {'x': x, 'src': src, 'dst': dst, 'L0_gnn_W_l': _L0_gnn_in['W_l'], 'L0_gnn_W_r': _L0_gnn_in['W_r'], 'L0_gnn_b_r': _L0_gnn_in['b_r'], 'L1_gnn_W': _L1_gnn_in['W'], 'L1_gnn_att_src': _L1_gnn_in['att_src'], 'L1_gnn_att_dst': _L1_gnn_in['att_dst'], 'L1_gnn_bias': _L1_gnn_in['bias'], 'L1_gnn_ln_gamma': _L1_gnn_in['ln_gamma'], 'L1_gnn_ln_beta': _L1_gnn_in['ln_beta'], 'L2_gnn_W1': _L2_gnn_in['W1'], 'L2_gnn_b1': _L2_gnn_in['b1'], 'L2_gnn_W2': _L2_gnn_in['W2'], 'L2_gnn_b2': _L2_gnn_in['b2'], 'L3_gnn_weight': _L3_gnn_in['weight'], 'L3_gnn_attn_l': _L3_gnn_in['attn_l'], 'L3_gnn_attn_r': _L3_gnn_in['attn_r']}

def reference(x, src, dst, L0_gnn_W_l, L0_gnn_W_r, L0_gnn_b_r, L1_gnn_W, L1_gnn_att_src, L1_gnn_att_dst, L1_gnn_bias, L1_gnn_ln_gamma, L1_gnn_ln_beta, L2_gnn_W1, L2_gnn_b1, L2_gnn_W2, L2_gnn_b2, L3_gnn_weight, L3_gnn_attn_l, L3_gnn_attn_r):
    import jax
    import jax.numpy as jnp

    def _L0_gnn_ref(x, edge_index, W_l, W_r, b_r):
        import jax, jax.numpy as jnp
        import numpy as np
        N_NODES = 625
        src, dst = (edge_index[0], edge_index[1])
        messages = x[src]
        sums = jax.ops.segment_sum(messages, dst, num_segments=N_NODES)
        counts = jax.ops.segment_sum(jnp.ones_like(dst, dtype=x.dtype), dst, num_segments=N_NODES)
        aggr = sums / jnp.maximum(counts, 1.0)[:, None]
        out = aggr @ W_l.T + x @ W_r.T + b_r
        return out

    def _L1_gnn_ref(x, edge_index, W, att_src, att_dst, bias, ln_gamma, ln_beta):
        import jax, jax.numpy as jnp
        import numpy as np
        N = 50000
        E = 25000
        D = 256
        H = 4
        F = D // H

        def gat_layer(x, src, dst, W, att_src, att_dst, bias):
            n = x.shape[0]
            h = (x @ W).reshape(n, H, F)
            a_src = jnp.sum(h * att_src[None], axis=-1)
            a_dst = jnp.sum(h * att_dst[None], axis=-1)
            e = jax.nn.leaky_relu(a_src[src] + a_dst[dst], 0.2)
            m = jax.ops.segment_max(e, dst, num_segments=n)
            m = jnp.where(jnp.isfinite(m), m, 0.0)
            ex = jnp.exp(e - m[dst])
            denom = jax.ops.segment_sum(ex, dst, num_segments=n)
            alpha = ex / (denom[dst] + 1e-16)
            msg = h[src] * alpha[..., None]
            out = jax.ops.segment_sum(msg, dst, num_segments=n)
            return out.reshape(n, H * F) + bias
        n = x.shape[0]
        loops = jnp.arange(n, dtype=edge_index.dtype)
        src = jnp.concatenate([edge_index[0], loops])
        dst = jnp.concatenate([edge_index[1], loops])
        h = gat_layer(x, src, dst, W, att_src, att_dst, bias)
        y = h + x
        mu = jnp.mean(y, axis=-1, keepdims=True)
        var = jnp.mean((y - mu) ** 2, axis=-1, keepdims=True)
        y = (y - mu) / jnp.sqrt(var + 1e-05) * ln_gamma + ln_beta
        return jax.nn.relu(y)

    def _L2_gnn_ref(x, W1, b1, W2, b2, nn_index, k):
        import jax, jax.numpy as jnp
        import numpy as np
        N_NODES = 512
        D_FEAT = 256
        N_EDGES = 8192
        HIDDEN = 512
        D_OUT = 256
        num_nodes = x.shape[0]
        src = nn_index[0]
        tgt = nn_index[1]
        x_i = x[tgt]
        x_j = x[src]
        feat = jnp.concatenate([x_i, x_j - x_i], axis=-1)
        h = jax.nn.relu(feat @ W1 + b1)
        msg = h @ W2 + b2
        out = jax.ops.segment_sum(msg, tgt, num_segments=num_nodes)
        deg = jax.ops.segment_sum(jnp.ones((msg.shape[0], 1), dtype=msg.dtype), tgt, num_segments=num_nodes)
        return out / (deg + 1e-08)

    def _L3_gnn_ref(x, edge_index, weight, attn_l, attn_r):
        import jax, jax.numpy as jnp
        import numpy as np
        N, IN_CH, HEADS, OUT_CH, E = (50000, 256, 4, 64, 25000)
        heads, out_ch = attn_l.shape
        n = x.shape[0]
        xt = jnp.matmul(x, weight).reshape(-1, heads, out_ch)
        row, col = (edge_index[0], edge_index[1])
        alpha_l = jnp.einsum('ehd,hd->eh', xt[row], attn_l)
        alpha_r = jnp.einsum('ehd,hd->eh', xt[col], attn_r)
        alpha = jax.nn.softmax(jax.nn.leaky_relu(alpha_l + alpha_r, 0.01), axis=1)
        tmp = jnp.einsum('nh,nhd->nd', alpha[:n], xt[col[:n]])
        out = jnp.broadcast_to(tmp[:, None, :], (n, heads, out_ch))
        return out.reshape(n, heads * out_ch)
    edge_index = jnp.stack([src, dst])
    x = _layernorm(x + _L0_gnn_ref(x, edge_index, L0_gnn_W_l, L0_gnn_W_r, L0_gnn_b_r), axis=-1)
    x = _layernorm(x + _L1_gnn_ref(x, edge_index, L1_gnn_W, L1_gnn_att_src, L1_gnn_att_dst, L1_gnn_bias, L1_gnn_ln_gamma, L1_gnn_ln_beta), axis=-1)
    x = _layernorm(x + _L2_gnn_ref(x, L2_gnn_W1, L2_gnn_b1, L2_gnn_W2, L2_gnn_b2, edge_index, 16), axis=-1)
    x = _layernorm(x + _L3_gnn_ref(x, edge_index, L3_gnn_weight, L3_gnn_attn_l, L3_gnn_attn_r), axis=-1)
    return x

_drawn_inputs = setup_inputs


def setup_inputs(seed=0):
    import zlib

    import numpy as np

    out = dict(_drawn_inputs(seed))
    spreads = {'L0_gnn_b_r': (0.0, 0.1),
     'L1_gnn_bias': (0.0, 0.1),
     'L1_gnn_ln_gamma': (1.0, 0.2),
     'L1_gnn_ln_beta': (0.0, 0.1),
     'L2_gnn_b1': (0.0, 0.1),
     'L2_gnn_b2': (0.0, 0.1)}
    factors = {}
    for name, (base, spread) in spreads.items():
        noise = np.random.default_rng([zlib.crc32(name.encode()), seed]).standard_normal(out[name].shape)
        drawn = base * np.exp(spread * noise) if base else spread * noise
        out[name] = jnp.asarray(drawn.astype(out[name].dtype))
    for name, factor in factors.items():
        out[name] = (out[name] * factor).astype(out[name].dtype)
    return out
```

```python
import concourse.bass as bass
from concourse import mybir
from contextlib import ExitStack

N, D, E = 625, 256, 20000
NP = 125
NT = N // NP
H, F = 4, 64
HID = 512
DC = D // 128
ET = 128
TILES = -(-E // ET)
TAIL = E - (TILES - 1) * ET
LOW_TILES = TILES - 128
U = 6
FAST_TURNS = -(-(TILES + NT - 1) // U)
FAST_ITEMS = FAST_TURNS * U
ALL_TURNS = -(-(TILES * NT) // U)
ALL_ITEMS = ALL_TURNS * U
REST_CHUNK = (ALL_ITEMS - FAST_ITEMS) // 2
PAD = 2
NW = 640
SPLIT = 256
WX = D + 2 * H
NEG = -1.0e30
EPS = 1e-5
HEADS = NT * H


def program(nc, x, src, dst, w_l, w_r, b_r, w1g, att_s1, att_d1, bias1, gamma, beta,
            w1, b1, w2, b2, w3g, att_l, att_r, out):
    f32, f16, i32 = mybir.dt.float32, mybir.dt.float16, mybir.dt.int32
    f32r = mybir.dt.float32r
    ALU, ACT, AX = mybir.AluOpType, mybir.ActivationFunctionType, mybir.AxisListType

    ctx = ExitStack()
    with ctx:
        def sb(name, shape, dt):
            return ctx.enter_context(nc.sbuf_tensor(name, shape, dt))

        def sem(name):
            return ctx.enter_context(nc.semaphore(name))

        def sems(name):
            return [sem(f"{name}{k}") for k in range(U)]

        iota16 = sb("iota16", [128, ALL_ITEMS], f16)
        iota1 = sb("iota1", [128, ALL_ITEMS], f16)
        iota32 = sb("iota32", [128, 128], f32)
        ident = sb("ident", [128, 128], f32)
        upto = sb("upto", [128, 128], f32)
        ones = sb("ones", [128, 128], f32)
        zeros = sb("zeros", [128, 512], f16)
        tile_no = sb("tile_no", [128, NT], f16)
        w_lr = sb("w_lr", [128, 2, 2, D], f32)
        w_lrT = sb("w_lrT", [128, DC, 2 * D], f32)
        g1 = sb("g1", [128, DC, WX], f32)
        g3 = sb("g3", [128, DC, WX], f32)
        att = sb("att", [128, 4, D], f32)
        prod = sb("prod", [128, DC, D], f32)
        src_cols = sb("src_cols", [128, DC, H, 128], f32)
        w1_sb = sb("w1_sb", [128, 4, HID], f32)
        w1_dif = sb("w1_dif", [128, DC, HID], f32)
        w2_sb = sb("w2_sb", [128, 4, D], f32)
        rows = sb("rows", [128, 5, D], f32)
        b1_row = sb("b1_row", [128, HID], f32)
        src_i = sb("src_i", [128, 2, ET], i32)
        dst_i = sb("dst_i", [128, 2, ET], i32)
        src16 = sb("src16", [128, 2, ET], f16)
        dst_f = sb("dst_f", [128, 2 * ET], f32)
        dst_tile = sb("dst_tile", [128, 2 * ET], f32)
        has = sb("has", [128, 2 * NT], f32)
        has_sum = sb("has_sum", [128, 2 * NT], f32)
        has_before = sb("has_before", [128, 2 * NT], f32)
        place = sb("place", [128, 2 * NT], f32)
        t_src = sb("t_src", [128, ALL_ITEMS], f32)
        t_dst = sb("t_dst", [128, ALL_ITEMS + U], f32)
        t_tile = sb("t_tile", [1, ALL_ITEMS + 2 * U], i32)
        count = sb("count", [1, 1], i32)
        hot_dst = sb("hot_dst", [128, U, 128], f16)
        adj = sb("adj", [128, NT, NW], f32)
        deg = sb("deg", [128, NT], f32)
        rdeg = sb("rdeg", [128, NT], f32)
        rdeg2 = sb("rdeg2", [128, NT], f32)
        x0 = sb("x0", [128, NT, D], f32)
        x1 = sb("x1", [128, NT, D], f32)
        x2 = sb("x2", [128, NT, D], f32)
        xT = sb("xT", [128, DC, N], f32)
        tmp = sb("tmp", [128, NT, D], f32)
        h_sb = sb("h_sb", [128, NT, WX], f32)
        stats = sb("stats", [128, NT, 6], f32)
        mv = sb("mv", [128, NT, 2], f32)
        std = sb("std", [128, NT], f32)
        rstd = sb("rstd", [128, NT], f32)
        arena = sb("arena", [128, NT * NW + 8 * N + 2 * NT * NP + H * N], f32)
        halves = arena[:, :].bitcast(f16)
        c0 = 2 * NT * REST_CHUNK
        c1 = c0 + NT * 2 * ET
        c2 = c1 + NT * 2 * ET
        pick = halves[:, 0:c0].rearrange("p (q i) -> p q i", q=2 * NT)
        in_tile = halves[:, c0:c1].rearrange("p (b e) -> p b e", b=NT)
        dst_loc = halves[:, c1:c2].rearrange("p (b e) -> p b e", b=NT)
        hot_src = halves[:, c2:c2 + U * NW].rearrange("p (k s) -> p k s", k=U)
        a0 = NT * NW
        mask = arena[:, 0:a0].rearrange("p (b s) -> p b s", b=NT)
        score = arena[:, a0:a0 + 8 * N].rearrange("p (i s) -> p i s", i=8)
        a1 = a0 + 8 * N
        probT = arena[:, a1:a1 + 2 * NT * NP].rearrange("p (i s) -> p i s", i=2)
        a2 = a1 + 2 * NT * NP
        a_row = arena[:, a2:a2 + H * N].rearrange("p (h s) -> p h s", h=H)
        adjT = arena[:, a0:a0 + NT * NT * NP]
        xl0 = a0 + NT * NT * NP
        xl = arena[:, xl0:xl0 + NT * D].rearrange("p (b f) -> p b f", b=NT)
        xr = arena[:, a2:a2 + NT * D].rearrange("p (b f) -> p b f", b=NT)
        top = sb("top", [128, NT, H], f32)
        neg_top = sb("neg_top", [128, NT, H], f32)
        den = sb("den", [128, NT, H], f32)
        rden = sb("rden", [128, NT, H], f32)
        ring = arena[:, 0:U * HID].rearrange("p (i f) -> p i f", i=U)
        p0 = U * HID
        p_sb = arena[:, p0:p0 + NT * HID].rearrange("p (b f) -> p b f", b=NT)
        parts = sb("parts", [128, 2, NT, HID], f32r)
        high = sb("high", [128, 3, SPLIT], f32r)
        low = sb("low", [128, 3, SPLIT], f32r)
        q_sb = sb("q_sb", [128, NT, HID], f32)
        bend = q_sb[:, :, :].rearrange("p b f -> p (b f)")[:, 0:4 * N].rearrange("p (i s) -> p i s", i=4)
        a_dst4 = sb("a_dst4", [128, NT, H], f32)
        hot = sb("hot", [128, U, 128], f32r)
        hotT = sb("hotT", [128, 2, 128], f32r)
        gidx = sb("gidx", [128, U], i32)
        e_dst = sb("e_dst", [128, NT], i32)
        e_src = sb("e_src", [128, NT], i32)
        xt_g = sb("xt_g", [128, NT, WX], f32)
        al_g = sb("al_g", [128, NT, H], f32)
        lg = sb("lg", [128, NT, H], f32)
        lmax = sb("lmax", [128, NT], f32)
        lsum = sb("lsum", [128, NT], f32)
        ps = ctx.enter_context(nc.psum_tensor("ps", [128, 8, 512], f32))
        flat = ps[:, :, :].rearrange("p b f -> p (b f)")

        q_dram = nc.dram_tensor("q_table", (N, HID), f32).ap()
        xt_dram = nc.dram_tensor("xt_table", (N, WX), f32).ap()
        al_dram = nc.dram_tensor("al_table", (N, H), f32).ap()

        src_loaded, dst_loaded, x_loaded = sem("src_loaded"), sem("dst_loaded"), sem("x_loaded")
        lr_loaded, g1_loaded, g3_loaded = sem("lr_loaded"), sem("g1_loaded"), sem("g3_loaded")
        att_loaded, w1_loaded, w2_loaded = sem("att_loaded"), sem("w1_loaded"), sem("w2_loaded")
        rows_loaded, e_loaded = sem("rows_loaded"), sem("e_loaded")
        filled, consts, pool_step = sem("filled"), sem("consts"), sem("pool_step")
        dve_step, act_step = sem("dve_step"), sem("act_step")
        has_ready, pos_done, casts_done, picked = sem("has_ready"), sem("pos_done"), sem("casts_done"), sem("picked")
        listed, list_read = sem("listed"), sem("list_read")
        rest_picked, rest_listed, rest_read = sem("rest_picked"), sem("rest_listed"), sem("rest_read")
        atts_ready, folded, cols_ready = sem("atts_ready"), sem("folded"), sem("cols_ready")
        dif_ready, xr_raw, xr_ready = sem("dif_ready"), sem("xr_raw"), sem("xr_ready")
        wT_done, wT_copied = sem("wT_done"), sem("wT_copied")
        xT_done, xT_copied_a, xT_copied_v = sem("xT_done"), sem("xT_copied_a"), sem("xT_copied_v")
        lin_done, lin_read = sem("lin_done"), sem("lin_read")
        hots_built, hots_used, adj_done = sems("hots_built"), sems("hots_used"), sem("adj_done")
        adj_copied_v, adj_copied_a = sem("adj_copied_v"), sem("adj_copied_a")
        adjT_done, adjT_copied_v, adjT_copied_a = sem("adjT_done"), sem("adjT_copied_v"), sem("adjT_copied_a")
        agg_done, var_ready, std_ready, x_ready = sem("agg_done"), sem("var_ready"), sem("std_ready"), sem("x_ready")
        h_done, h_copied, row_done, row_copied = sem("h_done"), sem("h_copied"), sem("row_done"), sem("row_copied")
        top_ready, leaky, exped, weighted = sem("top_ready"), sem("leaky"), sem("exped"), sem("weighted")
        bent = sem("bent")
        probT_done, probT_a, probT_v = sem("probT_done"), sem("probT_a"), sem("probT_v")
        mixed, mixed_read = sem("mixed"), sem("mixed_read")
        q_done, q_copied, q_stored = sem("q_done"), sem("q_copied"), sem("q_stored")
        p_done, p_added, p_high, parts_ready = sem("p_done"), sem("p_added"), sem("p_high"), sem("parts_ready")
        high_ready, low_ready = sems("high_ready"), sems("low_ready")
        gidx_ready = sem("gidx_ready")
        gathered, hot_built, hot_turned, hotT_ready = sems("gathered"), sems("hot_built"), sems("hot_turned"), sems("hotT_ready")
        p_spread, summed, relued, scattered = sems("p_spread"), sems("summed"), sems("relued"), sems("scattered")
        edges_done, s_copied_a, s_copied_v = sem("edges_done"), sem("s_copied_a"), sem("s_copied_v")
        sT_done, sT_copied_a, sT_copied_v, conv_done = sem("sT_done"), sem("sT_copied_a"), sem("sT_copied_v"), sem("conv_done")
        xt_done, xt_copied, xt_stored, xt_gathered = sem("xt_done"), sem("xt_copied"), sem("xt_stored"), sem("xt_gathered")
        lg_ready, l_exped, result_ready, stored = sem("lg_ready"), sem("l_exped"), sem("result_ready"), sem("stored")

        def nodes(ap):
            return ap.rearrange("(b p) f -> p b f", p=NP)

        def items(turn, k, width=1):
            return bass.ds(U * turn + (k - U), width)

        FULL = 4 * NP

        block = ctx.enter_context(nc.Block())

        @block.sync
        def _(sp):
            edges = (TILES - 1) * ET
            sp.wait_ge(filled, 2)
            for buf, ap, done in ((dst_i, dst, dst_loaded), (src_i, src, src_loaded)):
                sp.dma_start(buf[:, 0, :], ap[0:128 * ET].rearrange("(c e) -> c e", e=ET)).then_inc(done, 16)
                sp.dma_start(buf[0:LOW_TILES - 1, 1, :],
                             ap[128 * ET:edges].rearrange("(c e) -> c e", e=ET)).then_inc(done, 16)
                sp.dma_start(buf[LOW_TILES - 1:LOW_TILES, 1, 0:TAIL],
                             ap[edges:E].rearrange("(c e) -> c e", c=1)).then_inc(done, 16)
            sp.dma_start(g1[:, :, 0:D], w1g.rearrange("(c p) f -> p c f", p=128)).then_inc(g1_loaded, 16)
            for n, ap in enumerate((att_s1, att_d1, att_l, att_r)):
                sp.dma_start(att[:, n, :], ap.rearrange("h f -> (h f)").partition_broadcast(128)).then_inc(att_loaded, 16)
            sp.dma_start(g3[:, :, 0:D], w3g.rearrange("(c p) f -> p c f", p=128)).then_inc(g3_loaded, 16)
            sp.dma_start(w1_sb[:, :, :], w1.rearrange("(c p) f -> p c f", p=128)).then_inc(w1_loaded, 16)
            sp.dma_start(w2_sb[:, :, :], w2.rearrange("(c p) f -> p c f", p=128)).then_inc(w2_loaded, 16)
            sp.dma_start(e_dst[0:NP, :], dst[0:N].rearrange("(b p) -> p b", p=NP), allow_slow_non_contiguous=True).then_inc(e_loaded, 16)
            sp.dma_start(e_src[0:NP, :], src[0:N].rearrange("(b p) -> p b", p=NP), allow_slow_non_contiguous=True).then_inc(e_loaded, 16)
            for b in range(NT):
                sp.wait_ge(q_copied, b + 1)
                sp.dma_start(q_dram[b * NP:(b + 1) * NP, :], q_sb[0:NP, b, :]).then_inc(q_stored, 16)
            sp.wait_ge(xt_copied, NT)
            sp.dma_start(nodes(xt_dram), h_sb[0:NP, :, :]).then_inc(xt_stored, 16)
            sp.dma_start(nodes(al_dram), h_sb[0:NP, :, D:D + H]).then_inc(xt_stored, 16)
            sp.wait_ge(result_ready, 1)
            sp.dma_start(nodes(out), x0[0:NP, :, :]).then_inc(stored, 16)
            sp.wait_ge(stored, 16)
            sp.wait_ge(q_stored, 16 * NT)
            sp.wait_ge(xt_stored, 32)

        @block.gpsimd
        def _(pool):
            nc.gpsimd.memset(dst_i[:, 1, :], -1).then_inc(filled, 1)
            nc.gpsimd.memset(src_i[:, 1, :], 0).then_inc(filled, 1)
            iota = nc.gpsimd.iota
            iota(iota1[:, :], [[1, ALL_ITEMS]], base=1, channel_multiplier=0, allow_small_or_imprecise_dtypes=True)
            iota(iota16[:, :], [[1, ALL_ITEMS]], base=0, channel_multiplier=0, allow_small_or_imprecise_dtypes=True)
            iota(tile_no[:, :], [[1, NT]], base=0, channel_multiplier=0, allow_small_or_imprecise_dtypes=True)
            iota(iota32[:, :], [[1, 128]], base=0, channel_multiplier=0, allow_small_or_imprecise_dtypes=True)
            nc.gpsimd.memset(zeros[:, :], 0.0)
            nc.gpsimd.memset(t_tile[:, :], 0)
            nc.gpsimd.memset(ones[:, :], 1.0)
            nc.gpsimd.memset(upto[:, :], 1.0)
            nc.gpsimd.memset(ident[:, :], 0.0).then_inc(pool_step, 1)
            pool.wait_ge(pool_step, 1)
            nc.gpsimd.affine_select(out=upto[:, :], in_=upto[:, :], compare_op=ALU.is_ge, fill=0.0, base=0,
                                    pattern=[[1, 128]], channel_multiplier=-1)
            nc.gpsimd.affine_select(out=ident[:, :], in_=ident[:, :], compare_op=ALU.not_equal, fill=1.0, base=0,
                                    pattern=[[-1, 128]], channel_multiplier=1).then_inc(consts, 1)
            pool.wait_ge(att_loaded, 64)
            pool.wait_ge(g1_loaded, 16)
            for n in range(4):
                if n == 2:
                    pool.wait_ge(g3_loaded, 16)
                if n:
                    pool.wait_ge(folded, n)
                g = g1 if n < 2 else g3
                nc.gpsimd.tensor_tensor(prod[:, :, :], g[:, :, 0:D], att[:, n, :].unsqueeze(1).to_broadcast([128, DC, D]),
                                        ALU.mult).then_inc(atts_ready, 1)
            nc.gpsimd.tensor_copy(src_cols[:, :, :, :],
                                  g1[:, :, D:D + H].unsqueeze(3).to_broadcast([128, DC, H, 128])).then_inc(cols_ready, 1)
            pool.wait_ge(w1_loaded, 16)
            nc.gpsimd.tensor_tensor(w1_dif[:, :, :], w1_sb[:, 0:2, :], w1_sb[:, 2:4, :], ALU.subtract).then_inc(dif_ready, 1)
            pool.wait_ge(x_loaded, 16)
            pool.wait_ge(rows_loaded, 96)
            nc.gpsimd.tensor_tensor(tmp[0:NP, :, :], x0[0:NP, :, :], rows[0:NP, 0, :].unsqueeze(1).to_broadcast([NP, NT, D]),
                                    ALU.add).then_inc(pool_step, 1)
            pool.wait_ge(pool_step, 2)
            pool.wait_ge(lin_read, 2 * NT)
            nc.gpsimd.tensor_tensor(xr[0:NP, :, :], xr[0:NP, :, :], tmp[0:NP, :, :], ALU.add).then_inc(xr_ready, 1)

            for i in range(HEADS):
                pool.wait_ge(bent, i + 1)
                s = score[0:NP, i % 8, :]
                nc.gpsimd.tensor_tensor(s, s, bend[0:NP, i % 4, :], ALU.add).then_inc(leaky, 1)

            pool.wait_ge(gidx_ready, 1)
            pool.wait_ge(q_stored, 16 * NT)

            def gather(k):
                pool.indirect_dma_start(ring[:, k, :], None, q_dram[:, :],
                                        bass.IndirectOffsetOnAxis(ap=gidx[:, k:k + 1], axis=0)).then_inc(gathered[k], 16)

            def gathers(first, last):
                with pool.Fori(first, last + 1) as before:
                    for k in range(U):
                        pool.wait_ge(q_stored, 16 * NT)
                        pool.wait_ge(scattered[k], before)
                        gather(k)

            for k in range(U):
                gather(k)
            gathers(1, FAST_TURNS - 1)
            n = pool.value_load(count[0:1, 0:1], min_val=0, max_val=ALL_ITEMS)
            with pool.If(n > FAST_ITEMS):
                pool.wait_ge(gidx_ready, 2)
                gathers(FAST_TURNS, ALL_TURNS - 1)
            pool.wait_ge(e_loaded, 32)
            pool.wait_ge(xt_stored, 32)
            for b in range(NT):
                pool.indirect_dma_start(xt_g[0:NP, b, :], None, xt_dram[:, :],
                                        bass.IndirectOffsetOnAxis(ap=e_dst[0:NP, b:b + 1], axis=0)).then_inc(xt_gathered, 16)
                pool.indirect_dma_start(al_g[0:NP, b, :], None, al_dram[:, :],
                                        bass.IndirectOffsetOnAxis(ap=e_src[0:NP, b:b + 1], axis=0)).then_inc(xt_gathered, 16)
            pool.wait_ge(xt_gathered, 32 * NT)

        @block.scalar
        def _(act):
            act.dma_start(x0[0:NP, :, :], nodes(x)).then_inc(x_loaded, 16)
            for n, ap in enumerate((w_l, w_r)):
                act.dma_start(w_lr[:, n, :, :], ap.rearrange("(c p) f -> p c f", p=128)).then_inc(lr_loaded, 16)
            for n, ap in enumerate((b_r, bias1, gamma, beta, b2)):
                act.dma_start(rows[:, n, :], ap.partition_broadcast(128)).then_inc(rows_loaded, 16)
            act.dma_start(b1_row[:, :], b1.partition_broadcast(128)).then_inc(rows_loaded, 16)

            def copy(o, i):
                return nc.scalar.activation(o, i, ACT.Copy)

            def copy_xT(n):
                act.wait_ge(xT_done, 3 * n + 1)
                copy(xT[:, 0, 0:FULL], ps[:, 0, 0:FULL]).then_inc(xT_copied_a, 1)
                act.wait_ge(xT_done, 3 * n + 3)
                copy(xT[:, :, FULL:N], ps[:, 2, 0:2 * NP].rearrange("p (c s) -> p c s", c=DC)).then_inc(xT_copied_a, 1)

            def root(n):
                act.wait_ge(var_ready, n + 1)
                nc.scalar.activation(std[0:NP, :], std[0:NP, :], ACT.Sqrt).then_inc(std_ready, 1)

            copy_xT(0)
            for n in range(2):
                act.wait_ge(wT_done, n + 1)
                copy(w_lrT[:, :, n * D:(n + 1) * D], ps[:, 3 + n, :].rearrange("p (c f) -> p c f", c=DC)).then_inc(wT_copied, 1)
            for b in range(NT):
                act.wait_ge(lin_done, b + 1)
                copy(xl[0:NP, b, :], ps[0:NP, 4 + b % 4, 0:D]).then_inc(lin_read, 1)
                copy(xr[0:NP, b, :], ps[0:NP, 4 + b % 4, D:2 * D]).then_inc(lin_read, 1)
            act.wait_ge(adj_done, 1)
            for b in range(NT):
                copy(adj[0:NP, b, 512:NW], flat[0:NP, 2560 + 128 * b:2560 + 128 * b + 128]).then_inc(adj_copied_a, 1)
            for m in range(1, 7, 2):
                act.wait_ge(adjT_done, m + 1)
                copy(adjT[0:NP, m * FULL:(m + 1) * FULL], ps[0:NP, m, 0:FULL]).then_inc(adjT_copied_a, 1)
            root(0)

            copy_xT(1)
            for b in range(NT):
                act.wait_ge(h_done, b + 1)
                copy(h_sb[0:NP, b, :], ps[0:NP, 3 + b, 0:WX]).then_inc(h_copied, 1)
            for h in range(H):
                act.wait_ge(row_done, h + 1)
                copy(a_row[0:NP, h, :], flat[0:NP, 1024 * (h % 2):1024 * (h % 2) + N]).then_inc(row_copied, 1)

            def probs_out(i):
                act.wait_ge(probT_done, i + 1)
                if i >= 2:
                    act.wait_ge(mixed, i - 1)
                copy(probT[0:NP, i % 2, 0:FULL], ps[0:NP, 4 + 2 * (i % 2), 0:FULL]).then_inc(probT_a, 1)

            def exp(i):
                act.wait_ge(leaky, i + 1)
                s = score[0:NP, i % 8, :]
                nc.scalar.activation(s, s, ACT.Exp, bias=neg_top[0:NP, i // H, i % H:i % H + 1], scale=0.2).then_inc(exped, 1)

            for i in range(HEADS):
                b, h = i // H, i % H
                s = score[0:NP, i % 8, :]
                act.wait_ge(top_ready, b + 1)
                if i >= 4:
                    act.wait_ge(leaky, i - 3)
                nc.scalar.activation(bend[0:NP, i % 4, :], s, ACT.Relu, bias=a_dst4[0:NP, b, h:h + 1], scale=4.0).then_inc(bent, 1)
                if i >= 1:
                    exp(i - 1)
                if i >= 3:
                    probs_out(i - 3)
            exp(HEADS - 1)
            for i in range(HEADS - 3, HEADS):
                probs_out(i)
            root(1)
            root(2)

            copy_xT(2)
            for b in range(NT):
                act.wait_ge(q_done, b + 1)
                copy(q_sb[0:NP, b, :], ps[0:NP, 3 + b, :]).then_inc(q_copied, 1)
            for b in range(NT):
                act.wait_ge(p_added, b + 1)
                copy(parts[0:NP, 0, b, :], p_sb[0:NP, b, :]).then_inc(p_high, 1)

            def turn_hot(g, k):
                k, g = k % U, g + k // U
                act.wait_ge(hot_turned[k], g)
                before = (k - 2) % U
                if not (isinstance(g, int) and (g - (k < 2)) < 1):
                    act.wait_ge(p_spread[before], g - (1 if k < 2 else 0))
                copy(hotT[0:NP, k % 2, :], ps[0:NP, 7, 0:128]).then_inc(hotT_ready[k], 1)

            def relu(g, k):
                act.wait_ge(summed[k], g)
                if not (isinstance(g, int) and g - (k < 3) < 1):
                    act.wait_ge(scattered[(k - 3) % U], g - (1 if k < 3 else 0))
                nc.scalar.activation(high[:, k % 3, :], ring[:, k, 0:SPLIT], ACT.Relu).then_inc(high_ready[k], 1)
                nc.scalar.activation(ring[:, k, SPLIT:HID], ring[:, k, SPLIT:HID], ACT.Relu).then_inc(relued[k], 1)

            def act_turn(g, last=False):
                for k in range(U):
                    if not (last and k + 2 >= U):
                        turn_hot(g, k + 2)
                    relu(g, k)

            def act_turns(first, last):
                turn_hot(first, 0)
                turn_hot(first, 1)
                act_turn(first)
                act.preload_act_table(ACT.Relu)
                with act.Fori(first + 1, last) as g:
                    act_turn(g)
                act_turn(last, last=True)

            act_turns(1, FAST_TURNS)
            n = act.value_load(count[0:1, 0:1], min_val=0, max_val=ALL_ITEMS)
            with act.If(n > FAST_ITEMS):
                act_turns(FAST_TURNS + 1, ALL_TURNS)
            act.wait_ge(edges_done, 1)
            for b in (1, 3):
                copy(q_sb[0:NP, b, :], ps[0:NP, b, :]).then_inc(s_copied_a, 1)
            for c in (1, 3):
                act.wait_ge(sT_done, c + 1)
                copy(p_sb[:, c, 0:FULL], ps[:, c, 0:FULL]).then_inc(sT_copied_a, 1)
            act.wait_ge(sT_done, 5)
            copy(p_sb[:, 4, 0:FULL], ps[:, 4, 0:FULL]).then_inc(sT_copied_a, 1)
            root(3)

            copy_xT(3)
            for b in range(NT):
                act.wait_ge(xt_done, b + 1)
                copy(h_sb[0:NP, b, :], ps[0:NP, 3 + b, 0:WX]).then_inc(xt_copied, 1)
            act.wait_ge(lg_ready, 1)
            nc.scalar.activation(lg[0:NP, :, :], lg[0:NP, :, :], ACT.Exp).then_inc(l_exped, 1)
            root(4)

        @block.vector
        def _(dve):
            steps = [0]

            def step(ins):
                steps[0] += 1
                ins.then_inc(dve_step, 1)

            def settle():
                dve.wait_ge(dve_step, steps[0])

            V = nc.vector
            dve.wait_ge(dst_loaded, 48)
            step(V.tensor_copy(dst_f[:, :], dst_i[:, :, :].rearrange("p k e -> p (k e)")))
            settle()
            step(V.tensor_scalar(dst_tile[:, :], dst_f[:, :], 0.0, None, ALU.is_ge))
            for j in range(1, NT):
                settle()
                step(V.scalar_tensor_tensor(dst_tile[:, :], dst_f[:, :], float(NP * j), dst_tile[:, :], ALU.is_ge, ALU.add))
            settle()
            for b in range(NT):
                step(V.tensor_scalar(in_tile[:, b, :], dst_tile[:, :], float(b + 1), None, ALU.is_equal))
            settle()
            step(V.reduce_max(has[:, :], in_tile[:, :, :].rearrange("p b (k e) -> p (b k) e", k=2), AX.X))
            dve.wait_ge(consts, 1)
            settle()
            step(V.tensor_tensor_scan(has_sum[:, :], ones[:, 0:2 * NT], has[:, :], 0.0, ALU.mult, ALU.add))
            settle()
            V.tensor_tensor(has_before[:, :], has_sum[:, :], has[:, :], ALU.subtract).then_inc(has_ready, 1)
            for b in range(NT):
                V.tensor_scalar(dst_loc[:, b, :], dst_f[:, :], float(1 - NP * b), None, ALU.add)
            dve.wait_ge(src_loaded, 48)
            V.tensor_copy(src16[:, :, :], src_i[:, :, :]).then_inc(casts_done, 1)
            dve.wait_ge(pos_done, 1)
            step(V.tensor_tensor(place[:, :], ps[:, 0, 0:2 * NT], has[:, :], ALU.mult))
            step(V.tensor_copy(count[0:1, :], ps[0:1, 0, 2 * NT:2 * NT + 1]))
            settle()
            for q in range(2 * NT):
                V.tensor_scalar(pick[:, q, 0:FAST_ITEMS], iota1[:, 0:FAST_ITEMS], place[:, q:q + 1], None,
                                ALU.is_equal).then_inc(picked, 1)

            def read_list(lo, w, done):
                V.tensor_copy(t_src[:, lo:lo + w], ps[:, 0, 0:w])
                V.tensor_scalar(t_dst[:, lo:lo + w], ps[:, 1, 0:w], 1.0, None, ALU.subtract)
                V.tensor_copy(t_tile[0:1, PAD + lo:PAD + lo + w], ps[0:1, 2, 0:w]).then_inc(done, 1)

            dve.wait_ge(listed, 1)
            read_list(0, FAST_ITEMS, list_read)
            dve.wait_ge(list_read, 1)
            n = dve.value_load(count[0:1, 0:1], min_val=0, max_val=ALL_ITEMS)
            with dve.If(n > FAST_ITEMS):
                for r in range(2):
                    lo = FAST_ITEMS + r * REST_CHUNK
                    for q in range(2 * NT):
                        V.tensor_scalar(pick[:, q, :], iota1[:, lo:lo + REST_CHUNK], place[:, q:q + 1], None,
                                        ALU.is_equal).then_inc(rest_picked, 1)
                    dve.wait_ge(rest_listed, r + 1)
                    read_list(lo, REST_CHUNK, rest_read)
                    dve.wait_ge(rest_read, r + 1)

            def copy_xT(n):
                dve.wait_ge(xT_done, 3 * n + 2)
                V.tensor_copy(xT[:, 1, 0:FULL], ps[:, 1, 0:FULL]).then_inc(xT_copied_v, 1)

            copy_xT(0)

            def hots(g, first=False):
                for k in range(U):
                    if not first:
                        dve.wait_ge(hots_used[k], g - 1)
                    V.tensor_scalar(hot_src[:, k, :], iota16[:, 0:NW], t_src[:, items(g, k)], None, ALU.is_equal)
                    V.tensor_scalar(hot_dst[:, k, :], iota16[:, 0:128], t_dst[:, items(g, k)], None,
                                    ALU.is_equal).then_inc(hots_built[k], 1)

            hots(1, first=True)
            with dve.Fori(2, FAST_TURNS + 1) as g:
                hots(g)
            with dve.If(n > FAST_ITEMS):
                with dve.Fori(FAST_TURNS + 1, ALL_TURNS + 1) as g:
                    hots(g)
            for n_att in range(4):
                g, at = (g1, D + H * n_att) if n_att < 2 else (g3, D + H * (n_att - 2))
                dve.wait_ge(atts_ready, n_att + 1)
                V.tensor_reduce(g[:, :, at:at + H], prod[:, :, :].rearrange("p c (h f) -> p c h f", h=H), AX.X,
                                ALU.add).then_inc(folded, 1)
            dve.wait_ge(adj_done, 1)
            for b in range(NT):
                V.tensor_copy(adj[0:NP, b, 0:512], ps[0:NP, b, :]).then_inc(adj_copied_v, 1)
            dve.wait_ge(adj_copied_v, NT)
            dve.wait_ge(adj_copied_a, NT)
            step(V.tensor_reduce(deg[0:NP, :], adj[0:NP, :, :], AX.X, ALU.add))
            settle()
            step(V.tensor_scalar(rdeg[0:NP, :], deg[0:NP, :], 1.0, None, ALU.max))
            step(V.tensor_scalar(rdeg2[0:NP, :], deg[0:NP, :], 1e-8, None, ALU.add))
            settle()
            step(V.reciprocal(rdeg[0:NP, :], rdeg[0:NP, :]))
            step(V.reciprocal(rdeg2[0:NP, :], rdeg2[0:NP, :]))
            for m in range(0, 7, 2):
                w = min(FULL, NT * NT * NP - m * FULL)
                dve.wait_ge(adjT_done, m + 1)
                V.tensor_copy(adjT[0:NP, m * FULL:m * FULL + w], ps[0:NP, m, 0:w]).then_inc(adjT_copied_v, 1)
            dve.wait_ge(adjT_done, 7)
            for b in range(NT):
                blk = adj[0:NP, b, b * NP:(b + 1) * NP]
                step(V.tensor_tensor(blk, blk, ident[0:NP, 0:NP], ALU.add))
            settle()
            step(V.tensor_scalar(mask[0:NP, :, :], adj[0:NP, :, :], 0.0, NEG, ALU.is_equal, ALU.mult))

            norms = [0]

            def layer_norm(o, i):
                for b in range(NT):
                    step(V.bn_stats(stats[0:NP, b, :], i[0:NP, b, :]))
                settle()
                for b in range(NT):
                    step(V.bn_aggr(mv[0:NP, b, :], stats[0:NP, b, :]))
                settle()
                V.tensor_scalar(std[0:NP, :], mv[0:NP, :, 1], EPS, None, ALU.add).then_inc(var_ready, 1)
                norms[0] += 1
                dve.wait_ge(std_ready, norms[0])
                step(V.reciprocal(rstd[0:NP, :], std[0:NP, :]))
                settle()
                for b in range(NT):
                    last = V.tensor_scalar(o[0:NP, b, :], i[0:NP, b, :], mv[0:NP, b, 0:1], rstd[0:NP, b:b + 1],
                                           ALU.subtract, ALU.mult)
                return last

            def row(n):
                return rows[0:NP, n, :].unsqueeze(1).to_broadcast([NP, NT, D])

            dve.wait_ge(xr_ready, 1)
            for b in range(NT):
                dve.wait_ge(agg_done, b + 1)
                step(V.scalar_tensor_tensor(tmp[0:NP, b, :], ps[0:NP, b, 0:D], rdeg[0:NP, b:b + 1], xr[0:NP, b, :],
                                            ALU.mult, ALU.add))
            settle()
            layer_norm(x1, tmp).then_inc(x_ready, 1)

            copy_xT(1)

            def best(b):
                for h in range(H):
                    dve.wait_ge(row_copied, h + 1)
                    if b >= 2:
                        dve.wait_ge(probT_done, H * (b - 2) + h + 1)
                    step(V.tensor_tensor_reduce(out=score[0:NP, (H * b + h) % 8, :], in0=mask[0:NP, b, 0:N],
                                                in1=a_row[0:NP, h, :], scale=1.0, scalar=-3.0e38, op0=ALU.add,
                                                op1=ALU.max, accum_out=top[0:NP, b, h:h + 1]))
                dve.wait_ge(h_copied, b + 1)
                settle()
                step(V.tensor_tensor(top[0:NP, b, :], top[0:NP, b, :], h_sb[0:NP, b, D + H:D + 2 * H], ALU.add))
                settle()
                step(V.scalar_tensor_tensor(top[0:NP, b, :], top[0:NP, b, :], 0.2, top[0:NP, b, :], ALU.mult, ALU.max))
                settle()
                V.tensor_scalar(a_dst4[0:NP, b, :], h_sb[0:NP, b, D + H:D + 2 * H], 4.0, None, ALU.mult)
                V.scalar_tensor_tensor(neg_top[0:NP, b, :], h_sb[0:NP, b, D + H:D + 2 * H], 0.2, top[0:NP, b, :],
                                       ALU.mult, ALU.subtract).then_inc(top_ready, 1)

            def probs_out(i):
                dve.wait_ge(probT_done, i + 1)
                if i >= 2:
                    dve.wait_ge(mixed, i - 1)
                V.tensor_copy(probT[0:NP, i % 2, FULL:N], ps[0:NP, 5 + 2 * (i % 2), 0:NP]).then_inc(probT_v, 1)

            def heads_out(b):
                dve.wait_ge(weighted, H * (b + 1))
                step(V.tensor_scalar(rden[0:NP, b, :], den[0:NP, b, :], 1e-16, None, ALU.add))
                settle()
                step(V.reciprocal(rden[0:NP, b, :], rden[0:NP, b, :]))
                settle()
                dve.wait_ge(mixed, H * (b + 1))
                V.tensor_tensor(tmp[0:NP, b, :].rearrange("p (h f) -> p h f", h=H),
                                ps[0:NP, b % 4, 0:D].rearrange("p (h f) -> p h f", h=H),
                                rden[0:NP, b, :].unsqueeze(2).to_broadcast([NP, H, F]), ALU.mult).then_inc(mixed_read, 1)

            best(0)
            for b in range(NT):
                if b + 1 < NT:
                    best(b + 1)
                for h in range(H):
                    i = H * b + h
                    dve.wait_ge(exped, i + 1)
                    V.tensor_tensor_reduce(out=score[0:NP, i % 8, :], in0=score[0:NP, i % 8, :], in1=adj[0:NP, b, 0:N],
                                           scale=1.0, scalar=0.0, op0=ALU.mult, op1=ALU.add,
                                           accum_out=den[0:NP, b, h:h + 1]).then_inc(weighted, 1)
                    if i >= 1:
                        probs_out(i - 1)
                if b >= 1:
                    heads_out(b - 1)
            probs_out(HEADS - 1)
            heads_out(NT - 1)
            dve.wait_ge(mixed_read, NT)
            step(V.tensor_tensor(tmp[0:NP, :, :], tmp[0:NP, :, :], row(1), ALU.add))
            settle()
            step(V.tensor_tensor(tmp[0:NP, :, :], tmp[0:NP, :, :], x1[0:NP, :, :], ALU.add))
            settle()
            step(layer_norm(tmp, tmp))
            settle()
            step(V.tensor_tensor(tmp[0:NP, :, :], tmp[0:NP, :, :], row(2), ALU.mult))
            settle()
            step(V.tensor_tensor(tmp[0:NP, :, :], tmp[0:NP, :, :], row(3), ALU.add))
            settle()
            step(V.scalar_tensor_tensor(tmp[0:NP, :, :], tmp[0:NP, :, :], 0.0, x1[0:NP, :, :], ALU.max, ALU.add))
            settle()
            layer_norm(x2, tmp).then_inc(x_ready, 1)

            V.tensor_copy(gidx[:, :], t_src[:, 0:U]).then_inc(gidx_ready, 1)
            copy_xT(2)
            for b in range(NT):
                dve.wait_ge(p_done, b + 1)
                V.tensor_tensor(p_sb[0:NP, b, :], ps[0:NP, (b + 1) % 2, :], b1_row[0:NP, :], ALU.add).then_inc(p_added, 1)
                dve.wait_ge(p_high, b + 1)
                V.tensor_tensor(parts[0:NP, 1, b, :], p_sb[0:NP, b, :], parts[0:NP, 0, b, :].bitcast(f32), ALU.subtract).then_inc(parts_ready, 1)

            def build_hot(g, k):
                column = items(g, k)
                k, g = k % U, g + k // U
                if not (isinstance(g, int) and g < 2):
                    dve.wait_ge(scattered[k], g - 1)
                V.tensor_scalar(hot[:, k, :], iota32[:, :], t_dst[:, column], None, ALU.is_equal).then_inc(hot_built[k], 1)

            def add_p(g, k, index=True):
                dve.wait_ge(gathered[k], 16 * g)
                if index:
                    V.tensor_scalar(gidx[:, k:k + 1], t_src[:, items(g, k + U)], 0.0, None, ALU.add)
                dve.wait_ge(p_spread[k], g)
                V.tensor_tensor(ring[:, k, :], ring[:, k, :], ps[:, 5 + k % 2, :], ALU.add).then_inc(summed[k], 1)

            def rest(g, k):
                k, g = k % U, g + k // U
                dve.wait_ge(high_ready[k], g)
                V.scalar_tensor_tensor(low[:, k % 3, :], ring[:, k, 0:SPLIT], 0.0, high[:, k % 3, :].bitcast(f32),
                                       ALU.max, ALU.subtract).then_inc(low_ready[k], 1)

            def dve_turn(g, first=False, last=False, index=True):
                for k in range(U):
                    if not (last and k + 3 >= U):
                        build_hot(g, k + 3)
                    add_p(g, k, index)
                    if not (first and k < 1):
                        rest(g, k - 1)
                if last:
                    rest(g, U - 1)

            def dve_turns(first, last, index_last):
                for k in range(3):
                    build_hot(first, k)
                dve_turn(first, first=True)
                with dve.Fori(first + 1, last) as g:
                    dve_turn(g)
                dve_turn(last, last=True, index=index_last)

            dve_turns(1, FAST_TURNS, False)
            n = dve.value_load(count[0:1, 0:1], min_val=0, max_val=ALL_ITEMS)
            with dve.If(n > FAST_ITEMS):
                V.tensor_copy(gidx[:, :], t_src[:, FAST_ITEMS:FAST_ITEMS + U]).then_inc(gidx_ready, 1)
                dve_turns(FAST_TURNS + 1, ALL_TURNS, False)
            dve.wait_ge(edges_done, 1)
            for b in (0, 2, 4):
                V.tensor_copy(q_sb[0:NP, b, :], ps[0:NP, b, :]).then_inc(s_copied_v, 1)
            for c in (0, 2):
                dve.wait_ge(sT_done, c + 1)
                V.tensor_copy(p_sb[:, c, 0:FULL], ps[:, c, 0:FULL]).then_inc(sT_copied_v, 1)
            for b in range(NT):
                step(V.scalar_tensor_tensor(tmp[0:NP, b, :], rows[0:NP, 4, :], deg[0:NP, b:b + 1], x2[0:NP, b, :],
                                            ALU.mult, ALU.bypass))
            settle()
            for b in range(NT):
                dve.wait_ge(conv_done, b + 1)
                step(V.tensor_tensor(tmp[0:NP, b, :], tmp[0:NP, b, :], ps[0:NP, (5 + b) % 8, 0:D], ALU.add))
            settle()
            for b in range(NT):
                step(V.scalar_tensor_tensor(tmp[0:NP, b, :], tmp[0:NP, b, :], rdeg2[0:NP, b:b + 1], x2[0:NP, b, :],
                                            ALU.mult, ALU.add))
            settle()
            layer_norm(x1, tmp).then_inc(x_ready, 1)

            copy_xT(3)
            dve.wait_ge(xt_gathered, 32 * NT)
            al = lg[0:NP, :, :]
            step(V.tensor_tensor(al, al_g[0:NP, :, :], xt_g[0:NP, :, D + H:D + 2 * H], ALU.add))
            settle()
            step(V.scalar_tensor_tensor(al, al, 0.01, al, ALU.mult, ALU.max))
            settle()
            step(V.tensor_reduce(lmax[0:NP, :], al, AX.X, ALU.max))
            settle()
            V.tensor_tensor(al, al, lmax[0:NP, :].unsqueeze(2).to_broadcast([NP, NT, H]), ALU.subtract).then_inc(lg_ready, 1)
            dve.wait_ge(l_exped, 1)
            step(V.tensor_reduce(lsum[0:NP, :], al, AX.X, ALU.add))
            settle()
            step(V.reciprocal(lsum[0:NP, :], lsum[0:NP, :]))
            settle()
            step(V.tensor_tensor(al, al, lsum[0:NP, :].unsqueeze(2).to_broadcast([NP, NT, H]), ALU.mult))
            settle()
            for b in range(NT):
                step(V.tensor_tensor(tmp[0:NP, b, :].rearrange("p (h f) -> p h f", h=H),
                                     xt_g[0:NP, b, 0:D].rearrange("p (h f) -> p h f", h=H),
                                     lg[0:NP, b, :].unsqueeze(2).to_broadcast([NP, H, F]), ALU.mult))
            settle()
            step(V.tensor_reduce(xl[0:NP, :, 0:F], tmp[0:NP, :, :].rearrange("p b (h f) -> p b f h", h=H), AX.X, ALU.add))
            settle()
            for b in range(NT):
                step(V.tensor_tensor(tmp[0:NP, b, :].rearrange("p (h f) -> p h f", h=H),
                                     x1[0:NP, b, :].rearrange("p (h f) -> p h f", h=H),
                                     xl[0:NP, b, 0:F].unsqueeze(1).to_broadcast([NP, H, F]), ALU.add))
            settle()
            layer_norm(x0, tmp).then_inc(result_ready, 1)

        @block.tensor
        def _(pe):
            def mm(o, a, b, start, stop):
                return nc.tensor.matmul(o, a, b, start=start, stop=stop, skip_group_check=True)

            def turn(n, xs):
                for c in range(DC):
                    for b in range(NT - 1):
                        last = nc.tensor.transpose(ps[:, c, b * NP:(b + 1) * NP], xs[0:NP, b, c * 128:(c + 1) * 128],
                                                   ident[0:NP, 0:NP])
                    last.then_inc(xT_done, 1)
                for c in range(DC):
                    last = nc.tensor.transpose(ps[:, 2, c * NP:(c + 1) * NP], xs[0:NP, NT - 1, c * 128:(c + 1) * 128],
                                               ident[0:NP, 0:NP])
                last.then_inc(xT_done, 1)

            def turned(n):
                pe.wait_ge(xT_copied_a, 2 * n + 2)
                pe.wait_ge(xT_copied_v, n + 1)

            pe.wait_ge(consts, 1)
            pe.wait_ge(has_ready, 1)
            mm(ps[:, 0, 0:2 * NT], upto[:, :], has[:, :], True, False)
            mm(ps[:, 0, 0:2 * NT], ones[:, :], has_before[:, :], False, True)
            mm(ps[:, 0, 2 * NT:2 * NT + 1], ones[:, :], has_sum[:, 2 * NT - 1:2 * NT], True, True).then_inc(pos_done, 1)

            def make_list(w, sem_in, base, done):
                pe.wait_ge(sem_in, base)
                for q in range(2 * NT):
                    b, kt = q // 2, q % 2
                    one = pick[:, q, 0:w]
                    mm(ps[:, 0, 0:w], src16[:, kt, :], one, q == 0, q == 2 * NT - 1)
                    mm(ps[:, 1, 0:w], dst_loc[:, b, kt * ET:(kt + 1) * ET], one, q == 0, q == 2 * NT - 1)
                    last = mm(ps[0:1, 2, 0:w], tile_no[:, b:b + 1], one, q == 0, q == 2 * NT - 1)
                last.then_inc(done, 1)

            pe.wait_ge(casts_done, 1)
            make_list(FAST_ITEMS, picked, 2 * NT, listed)
            pe.wait_ge(list_read, 1)
            n_items = pe.value_load(count[0:1, 0:1], min_val=0, max_val=ALL_ITEMS)
            with pe.If(n_items > FAST_ITEMS):
                for r in range(2):
                    make_list(REST_CHUNK, rest_picked, 2 * NT * (r + 1), rest_listed)
                    pe.wait_ge(rest_read, r + 1)
            pe.wait_ge(x_loaded, 16)
            turn(0, x0)
            pe.wait_ge(lr_loaded, 32)
            for n in range(2):
                for c in range(DC):
                    for o in range(DC):
                        at = c * D + o * 128
                        last = nc.tensor.transpose(ps[:, 3 + n, at:at + 128], w_lr[:, n, o, c * 128:(c + 1) * 128], ident[:, :])
                last.then_inc(wT_done, 1)
            turned(0)
            pe.wait_ge(wT_copied, 2)
            for b in range(NT):
                if b == NT - 1:
                    pe.wait_ge(lin_read, 2)
                for c in range(DC):
                    last = mm(ps[0:NP, 4 + b % 4, :], xT[:, c, b * NP:(b + 1) * NP], w_lrT[:, c, :], c == 0, c == DC - 1)
                last.then_inc(lin_done, 1)
            pe.wait_ge(lin_read, 2 * NT)
            for k in range(7):
                mm(ps[:, k, :], zeros[:, 0:128], zeros[:, :], True, True)

            def tiles_of(g, lo, width):
                _, values = nc.values_load_multi_w_load_instructions(
                    t_tile[0:1, bass.ds(U * g + (lo - U), width)], engines=[mybir.EngineType.PE], min_val=0, max_val=NT - 1,
                    skip_runtime_bounds_check_because="a node tile's number: one of 0 to NT - 1, or 0 where no item is")
                return values

            def adjacency(g):
                tiles = tiles_of(g, PAD, U)
                for k in range(U):
                    pe.wait_ge(hots_built[k], g)
                    mm(ps[:, bass.ds(tiles[k], 1), :], hot_dst[:, k, :], hot_src[:, k, 0:512], False, True)
                    mm(flat[:, bass.ds(tiles[k] * 128 + 2560, 128)], hot_dst[:, k, :], hot_src[:, k, 512:NW],
                       False, True).then_inc(hots_used[k], 1)

            with pe.Fori(1, FAST_TURNS + 1) as g:
                adjacency(g)
            with pe.If(n_items > FAST_ITEMS):
                with pe.Fori(FAST_TURNS + 1, ALL_TURNS + 1) as g:
                    adjacency(g)
            mm(ps[:, 6, :], zeros[:, 0:128], zeros[:, :], False, True).then_inc(adj_done, 1)
            pe.wait_ge(adj_copied_v, NT)
            pe.wait_ge(adj_copied_a, NT)
            for n in range(NT * NT):
                s, d = n // NT, n % NT
                last = nc.tensor.transpose(ps[0:NP, n // 4, (n % 4) * NP:(n % 4 + 1) * NP], adj[0:NP, d, s * NP:(s + 1) * NP],
                                           ident[0:NP, 0:NP])
                if n % 4 == 3 or n == NT * NT - 1:
                    last.then_inc(adjT_done, 1)
            pe.wait_ge(adjT_copied_v, 4)
            pe.wait_ge(adjT_copied_a, 3)
            for b in range(NT):
                for s in range(NT):
                    at = (s * NT + b) * NP
                    last = mm(ps[0:NP, b, 0:D], adjT[0:NP, at:at + NP], xl[0:NP, s, :], s == 0, s == NT - 1)
                last.then_inc(agg_done, 1)
            pe.wait_ge(x_ready, 1)
            turn(1, x1)
            pe.wait_ge(folded, 4)
            turned(1)

            def project(g, done):
                for b in range(NT):
                    for c in range(DC):
                        last = mm(ps[0:NP, 3 + b, 0:WX], xT[:, c, b * NP:(b + 1) * NP], g[:, c, :], c == 0, c == DC - 1)
                    last.then_inc(done, 1)

            project(g1, h_done)
            pe.wait_ge(cols_ready, 1)
            for h in range(H):
                if h >= 2:
                    pe.wait_ge(row_copied, h - 1)
                elif h == 1:
                    pe.wait_ge(h_copied, NT)
                for lo, hi in ((0, 512), (512, N)):
                    for c in range(DC):
                        last = mm(flat[:, 1024 * (h % 2) + lo:1024 * (h % 2) + hi], src_cols[:, c, h, :], xT[:, c, lo:hi],
                                  c == 0, c == DC - 1)
                last.then_inc(row_done, 1)
            pe.wait_ge(row_copied, H)

            def mix(i):
                b, h = i // H, i % H
                pe.wait_ge(probT_a, i + 1)
                pe.wait_ge(probT_v, i + 1)
                if b >= 4:
                    pe.wait_ge(mixed_read, b - 3)
                for s in range(NT):
                    last = mm(ps[0:NP, b % 4, h * F:(h + 1) * F], probT[0:NP, i % 2, s * NP:(s + 1) * NP],
                              h_sb[0:NP, s, h * F:(h + 1) * F], s == 0, s == NT - 1)
                last.then_inc(mixed, 1)

            for i in range(HEADS):
                pe.wait_ge(weighted, i + 1)
                if i >= 2:
                    pe.wait_ge(probT_a, i - 1)
                    pe.wait_ge(probT_v, i - 1)
                for s in range(NT):
                    last = nc.tensor.transpose(ps[0:NP, 4 + 2 * (i % 2) + s // 4, (s % 4) * NP:(s % 4 + 1) * NP],
                                               score[0:NP, i % 8, s * NP:(s + 1) * NP], ident[0:NP, 0:NP])
                last.then_inc(probT_done, 1)
                if i >= 1:
                    mix(i - 1)
            mix(HEADS - 1)
            pe.wait_ge(x_ready, 2)
            turn(2, x2)
            turned(2)
            pe.wait_ge(w1_loaded, 16)
            for b in range(NT):
                for c in range(DC):
                    last = mm(ps[0:NP, 3 + b, :], xT[:, c, b * NP:(b + 1) * NP], w1_sb[:, DC + c, :], c == 0, c == DC - 1)
                last.then_inc(q_done, 1)
            pe.wait_ge(dif_ready, 1)
            for b in range(NT):
                if b >= 2:
                    pe.wait_ge(p_added, b - 1)
                for c in range(DC):
                    last = mm(ps[0:NP, (b + 1) % 2, :], xT[:, c, b * NP:(b + 1) * NP], w1_dif[:, c, :], c == 0, c == DC - 1)
                last.then_inc(p_done, 1)
            pe.wait_ge(p_added, NT)
            pe.wait_ge(q_copied, NT)
            for k in range(NT):
                mm(ps[:, k, :], zeros[:, 0:128], zeros[:, :], True, True)
            pe.wait_ge(parts_ready, NT)

            def turn_hot(g, k):
                k, g = k % U, g + k // U
                pe.wait_ge(hot_built[k], g)
                if not (isinstance(g, int) and g - (k < 1) < 1):
                    pe.wait_ge(hotT_ready[(k - 1) % U], g - (1 if k < 1 else 0))
                nc.tensor.transpose(ps[:, 7, 0:128], hot[:, k, :].bitcast(f32), ident[:, :]).then_inc(hot_turned[k], 1)

            def spread_p(g, k, tile):
                k, g = k % U, g + k // U
                pe.wait_ge(hotT_ready[k], g)
                if not (isinstance(g, int) and g - (k < 2) < 1):
                    pe.wait_ge(summed[(k - 2) % U], g - (1 if k < 2 else 0))
                for r in range(2):
                    last = mm(ps[:, 5 + k % 2, :], hotT[0:NP, k % 2, :], parts[0:NP, r, bass.ds(tile, 1), :], r == 0, r == 1)
                last.then_inc(p_spread[k], 1)

            def scatter(g, k, tile):
                k, g = k % U, g + k // U
                pe.wait_ge(relued[k], g)
                mm(flat[:, bass.ds(tile * 512 + SPLIT, HID - SPLIT)], hot[:, k, :].bitcast(f32), ring[:, k, SPLIT:HID], False, True)
                pe.wait_ge(low_ready[k], g)
                mm(flat[:, bass.ds(tile * 512, SPLIT)], hot[:, k, :], high[:, k % 3, :], False, True)
                mm(flat[:, bass.ds(tile * 512, SPLIT)], hot[:, k, :], low[:, k % 3, :], False, True).then_inc(scattered[k], 1)

            def pe_turn(g, first=False, last=False):
                tiles = tiles_of(g, 0, PAD + U + 1)
                if first:
                    spread_p(g, 0, tiles[PAD])
                for k in range(U):
                    if not (last and k + 2 >= U):
                        turn_hot(g, k + 2)
                    if not (last and k + 1 >= U):
                        spread_p(g, k + 1, tiles[PAD + k + 1])
                    if not (first and k < 2):
                        scatter(g, k - 2, tiles[k])
                if last:
                    scatter(g, U - 2, tiles[U])
                    scatter(g, U - 1, tiles[U + 1])

            def pe_turns(first, last):
                turn_hot(first, 0)
                turn_hot(first, 1)
                pe_turn(first, first=True)
                with pe.Fori(first + 1, last) as g:
                    pe_turn(g)
                pe_turn(last, last=True)

            pe_turns(1, FAST_TURNS)
            with pe.If(n_items > FAST_ITEMS):
                pe_turns(FAST_TURNS + 1, ALL_TURNS)
            mm(ps[:, 4, :], zeros[:, 0:128], zeros[:, :], False, True).then_inc(edges_done, 1)
            pe.wait_ge(s_copied_a, 2)
            pe.wait_ge(s_copied_v, 3)
            for c in range(4):
                for b in range(4):
                    last = nc.tensor.transpose(ps[:, c, b * NP:(b + 1) * NP], q_sb[0:NP, b, c * 128:(c + 1) * 128],
                                               ident[0:NP, 0:NP])
                last.then_inc(sT_done, 1)
            for c in range(4):
                last = nc.tensor.transpose(ps[:, 4, c * NP:(c + 1) * NP], q_sb[0:NP, 4, c * 128:(c + 1) * 128], ident[0:NP, 0:NP])
            last.then_inc(sT_done, 1)
            pe.wait_ge(w2_loaded, 16)
            pe.wait_ge(sT_copied_a, 3)
            pe.wait_ge(sT_copied_v, 2)
            for b in range(NT):
                for c in range(4):
                    lhs = p_sb[:, c, b * NP:(b + 1) * NP] if b < 4 else p_sb[:, 4, c * NP:(c + 1) * NP]
                    last = mm(ps[0:NP, (5 + b) % 8, 0:D], lhs, w2_sb[:, c, :], c == 0, c == 3)
                last.then_inc(conv_done, 1)
            pe.wait_ge(x_ready, 3)
            turn(3, x1)
            turned(3)
            project(g3, xt_done)


_INS = ['x', 'src', 'dst', 'L0_gnn_W_l', 'L0_gnn_W_r', 'L0_gnn_b_r', 'L1_gnn_W', 'L1_gnn_att_src', 'L1_gnn_att_dst',
        'L1_gnn_bias', 'L1_gnn_ln_gamma', 'L1_gnn_ln_beta', 'L2_gnn_W1', 'L2_gnn_b1', 'L2_gnn_W2', 'L2_gnn_b2',
        'L3_gnn_weight', 'L3_gnn_attn_l', 'L3_gnn_attn_r']


def kernel(**inputs):
    import numpy as _np
    import concourse.bacc as _bacc
    from concourse import mybir as _mybir
    from concourse.bass_utils import run_bass_kernel_spmd as _run

    nc = _bacc.Bacc("TRN2", target_bir_lowering=False, num_devices=1)
    arrays, args = {}, []
    for name in _INS:
        a = _np.ascontiguousarray(inputs[name])
        arrays[f"in_{name}"] = a
        args.append(nc.dram_tensor(f"in_{name}", a.shape, _mybir.dt.from_np(a.dtype), kind="ExternalInput").ap())
    args.append(nc.dram_tensor("out_0", (N, D), _mybir.dt.float32, kind="ExternalOutput").ap())
    program(nc, *args)
    r = _run(nc, [arrays], core_ids=[0])
    return r.results[0]["out_0"]
```

```python
import concourse.bass as bass
from concourse import mybir
from contextlib import ExitStack

N, D, E = 625, 256, 20000
NP = 125
NT = N // NP
H, F = 4, 64
HID = 512
DC = D // 128
ET = 128
TILES = -(-E // ET)
TAIL = E - (TILES - 1) * ET
LOW_TILES = TILES - 128
U = 6
LOADED = 3
HALF = U // 2
GROUP = 6
GROUPS = 3
WIDE = GROUP * GROUPS
DVE_HOTS = 2
FAST_WIDE = -(-(TILES + NT - 1) // WIDE)
FAST_ITEMS = FAST_WIDE * WIDE
FAST_TURNS = FAST_ITEMS // U
ALL_WIDE = -(-(TILES * NT) // WIDE)
ALL_ITEMS = ALL_WIDE * WIDE
ALL_TURNS = ALL_ITEMS // U
REST_CHUNK = (ALL_ITEMS - FAST_ITEMS) // 2
PAD = 2
NW = 640
SPLIT = 256
WX = D + 2 * H
NEG = -1.0e30
EPS = 1e-5
HEADS = NT * H


def program(nc, x, src, dst, w_l, w_r, b_r, w1g, att_s1, att_d1, bias1, gamma, beta,
            w1, b1, w2, b2, w3g, att_l, att_r, out):
    f32, f16, i32 = mybir.dt.float32, mybir.dt.float16, mybir.dt.int32
    f32r = mybir.dt.float32r
    ALU, ACT, AX = mybir.AluOpType, mybir.ActivationFunctionType, mybir.AxisListType

    ctx = ExitStack()
    with ctx:
        def sb(name, shape, dt):
            return ctx.enter_context(nc.sbuf_tensor(name, shape, dt))

        def sem(name):
            return ctx.enter_context(nc.semaphore(name))

        def sems(name):
            return [sem(f"{name}{k}") for k in range(U)]

        def group_sems(name):
            return [sem(f"{name}{k}") for k in range(GROUPS)]

        iota16 = sb("iota16", [128, ALL_ITEMS], f16)
        iota1 = sb("iota1", [128, ALL_ITEMS], f16)
        iota32 = sb("iota32", [128, 128], f32)
        ident = sb("ident", [128, 128], f32)
        ident_r = sb("ident_r", [128, 128], f32r)
        upto = sb("upto", [128, 128], f32)
        ones = sb("ones", [128, 128], f32)
        zeros = sb("zeros", [128, 512], f16)
        tile_no = sb("tile_no", [128, NT], f16)
        w_lr = sb("w_lr", [128, 2, 2, D], f32)
        w_lrT = sb("w_lrT", [128, DC, 2 * D], f32)
        g1 = sb("g1", [128, DC, WX], f32)
        g3 = sb("g3", [128, DC, WX], f32)
        att = sb("att", [128, 4, D], f32)
        w1_sb = sb("w1_sb", [128, 4, HID], f32)
        w1_dif = sb("w1_dif", [128, DC, HID], f32)
        w2_sb = sb("w2_sb", [128, 4, D], f32)
        rows = sb("rows", [128, 5, D], f32)
        b1_row = sb("b1_row", [128, HID], f32)
        src_i = sb("src_i", [128, 2, ET], i32)
        dst_i = sb("dst_i", [128, 2, ET], i32)
        src16 = sb("src16", [128, 2, ET], f16)
        dst_f = sb("dst_f", [128, 2 * ET], f32)
        dst_tile = sb("dst_tile", [128, 2 * ET], f32)
        has = sb("has", [128, 2 * NT], f32)
        has_sum = sb("has_sum", [128, 2 * NT], f32)
        has_before = sb("has_before", [128, 2 * NT], f32)
        place = sb("place", [128, 2 * NT], f32)
        t_src = sb("t_src", [128, ALL_ITEMS], f32)
        t_dst = sb("t_dst", [128, ALL_ITEMS + U], f32)
        t_tile = sb("t_tile", [1, ALL_ITEMS + 2 * U], i32)
        count = sb("count", [1, 1], i32)
        adj = sb("adj", [128, NT, NW], f32)
        deg = sb("deg", [128, NT], f32)
        rdeg = sb("rdeg", [128, NT], f32)
        rdeg2 = sb("rdeg2", [128, NT], f32)
        x0 = sb("x0", [128, NT, D], f32)
        x1 = sb("x1", [128, NT, D], f32)
        x2 = sb("x2", [128, NT, D], f32)
        x1_bias = sb("x1_bias", [128, NT, D], f32)
        xT = sb("xT", [128, DC, N], f32)
        tmp = sb("tmp", [128, NT, D], f32)
        h_sb = sb("h_sb", [128, NT, WX], f32)
        stats = sb("stats", [128, NT, 6], f32)
        mv = sb("mv", [128, NT, 2], f32)
        std = sb("std", [128, NT], f32)
        spare = [x2[:, :, :].rearrange("p b f -> p (b f)")[0:NP, k * N:(k + 1) * N] for k in range(2)]
        rstd = sb("rstd", [128, NT], f32)
        arena = sb("arena", [128, NT * NW + NT * N + 2 * H * N + N], f32)
        halves = arena[:, :].bitcast(f16)
        c0 = 2 * NT * REST_CHUNK
        c1 = c0 + NT * 2 * ET
        c2 = c1 + NT * 2 * ET
        pick = halves[:, 0:c0].rearrange("p (q i) -> p q i", q=2 * NT)
        in_tile = halves[:, c0:c1].rearrange("p (b e) -> p b e", b=NT)
        dst_loc = halves[:, c1:c2].rearrange("p (b e) -> p b e", b=NT)
        c3 = c2 + WIDE * NW
        hot_src = halves[:, c2:c3].rearrange("p (k s) -> p k s", k=WIDE)
        c4 = c3 + WIDE * 128
        hot_dst = halves[:, c3:c4].rearrange("p (k s) -> p k s", k=WIDE)
        apart = halves[:, c4:c4 + WIDE * 128].rearrange("p (k s) -> p k s", k=WIDE)
        a0 = NT * NW
        mask = arena[:, 0:a0].rearrange("p (b s) -> p b s", b=NT)
        adjT = arena[:, a0:a0 + NT * N]
        a1 = a0 + NT * N
        src_row = arena[:, a1:a1 + H * N].rearrange("p (h s) -> p h s", h=H)
        a2 = a1 + H * N
        dst_row = arena[:, a2:a2 + H * N].rearrange("p (h s) -> p h s", h=H)
        a3 = a2 + H * N
        top = sb("top", [128, NT, H], f32)
        down = sb("down", [128, NT, H], f32)
        rden = sb("rden", [128, NT, H], f32)
        ring = arena[:, 0:U * HID].rearrange("p (i f) -> p i f", i=U)
        p0 = U * HID
        p_sb = arena[:, p0:p0 + NT * HID].rearrange("p (b f) -> p b f", b=NT)
        parts = sb("parts", [128, 2, NT, HID], f32r)
        high = sb("high", [128, 3, SPLIT], f32r)
        low = sb("low", [128, 3, SPLIT], f32r)
        whole = sb("whole", [128, 3, HID - SPLIT], f32)
        q_sb = sb("q_sb", [128, NT, HID], f32)
        q_flat = q_sb[:, :, :].rearrange("p b f -> p (b f)")
        score = [q_flat[0:NP, k * N:(k + 1) * N] for k in range(4)] + [arena[0:NP, a3:a3 + N]]
        score += [x0[:, :, :].rearrange("p b f -> p (b f)")[0:NP, k * N:(k + 1) * N] for k in range(2)]
        SLOTS = len(score)
        prod = [q_sb[:, n, :].rearrange("p (c f) -> p c f", c=DC) for n in range(4)]
        h_ones = sb("h_ones", [128, NT, H, F + 1], f32)
        xl, xr = h_ones[:, :, :, :].rearrange("p b h f -> p b (h f)")[:, :, 0:D + 1], x1_bias
        src4 = sb("src4", [128, NT, H], f32)
        src02 = sb("src02", [128, NT, H], f32)
        hot = sb("hot", [128, U, 128], f32r)
        hotT = sb("hotT", [128, 2, 128], f32r)
        gidx = sb("gidx", [128, U], i32)
        e_dst = sb("e_dst", [128, NT], i32)
        e_src = sb("e_src", [128, NT], i32)
        xt_g = arena[:, a2:a2 + NT * WX].rearrange("p (b f) -> p b f", b=NT)
        al_g = sb("al_g", [128, NT, H], f32)
        lg = sb("lg", [128, NT, H], f32)
        lmax = sb("lmax", [128, NT], f32)
        lsum = sb("lsum", [128, NT], f32)
        ps = ctx.enter_context(nc.psum_tensor("ps", [128, 8, 512], f32))
        flat = ps[:, :, :].rearrange("p b f -> p (b f)")

        q_dram = nc.dram_tensor("q_table", (N, HID), f32).ap()
        xt_dram = nc.dram_tensor("xt_table", (N, WX), f32).ap()
        al_dram = nc.dram_tensor("al_table", (N, H), f32).ap()

        src_loaded, dst_loaded, x_loaded = sem("src_loaded"), sem("dst_loaded"), sem("x_loaded")
        lr_loaded, g1_loaded, g3_loaded = sem("lr_loaded"), sem("g1_loaded"), sem("g3_loaded")
        att_loaded, w1_loaded, w2_loaded = sem("att_loaded"), sem("w1_loaded"), sem("w2_loaded")
        rows_loaded, e_loaded = sem("rows_loaded"), sem("e_loaded")
        filled, consts, pool_step = sem("filled"), sem("consts"), sem("pool_step")
        dve_step, act_step = sem("dve_step"), sem("act_step")
        has_ready, pos_done, casts_done, picked = sem("has_ready"), sem("pos_done"), sem("casts_done"), sem("picked")
        listed, list_read = sem("listed"), sem("list_read")
        rest_picked, rest_listed, rest_read = sem("rest_picked"), sem("rest_listed"), sem("rest_read")
        atts_ready, folded = sem("atts_ready"), sem("folded")
        dif_ready, xr_raw, xr_ready = sem("dif_ready"), sem("xr_raw"), sem("xr_ready")
        wT_done, wT_copied = sem("wT_done"), sem("wT_copied")
        xT_done, xT_copied_a, xT_copied_v = sem("xT_done"), sem("xT_copied_a"), sem("xT_copied_v")
        lin_done, lin_read = sem("lin_done"), sem("lin_read")
        src_built, apart_done, dst_built = group_sems("src_built"), group_sems("apart_done"), group_sems("dst_built")
        hots_used, adj_done = group_sems("hots_used"), sem("adj_done")
        adj_copied_v, adj_copied_a = sem("adj_copied_v"), sem("adj_copied_a")
        adjT_done, adjT_copied_v, adjT_copied_a = sem("adjT_done"), sem("adjT_copied_v"), sem("adjT_copied_a")
        agg_done, var_ready, std_ready, x_ready = sem("agg_done"), sem("var_ready"), sem("std_ready"), sem("x_ready")
        h_done, h_copied, row_done, row_copied = sem("h_done"), sem("h_copied"), sem("row_done"), sem("row_copied")
        src_scaled, down_ready = sem("src_scaled"), sem("down_ready")
        bent, leaky, exped, weighted, mixed = sem("bent"), sem("leaky"), sem("exped"), sem("weighted"), sem("mixed")
        bias_added = sem("bias_added")
        sumT_copied, sum_turned, sum_read = sem("sumT_copied"), sem("sum_turned"), sem("sum_read")
        q_done, q_copied, q_stored = sem("q_done"), sem("q_copied"), sem("q_stored")
        p_done, p_added, p_high, parts_ready = sem("p_done"), sem("p_added"), sem("p_high"), sem("parts_ready")
        high_ready, low_ready = sems("high_ready"), sems("low_ready")
        gidx_ready = sem("gidx_ready")
        gathered, hot_turned, hotT_ready = sems("gathered"), sems("hot_turned"), sems("hotT_ready")
        hot_built = [sem(f"hot_built{k}") for k in range(U // 2)]
        next_index = [sem(f"next_index{k}") for k in range(2)]
        p_spread, summed, relued, scattered = sems("p_spread"), sems("summed"), sems("relued"), sems("scattered")
        edges_done, s_copied_a, s_copied_v = sem("edges_done"), sem("s_copied_a"), sem("s_copied_v")
        sT_done, sT_copied_a, sT_copied_v, conv_done = sem("sT_done"), sem("sT_copied_a"), sem("sT_copied_v"), sem("conv_done")
        xt_done, xt_copied, xt_stored, xt_gathered = sem("xt_done"), sem("xt_copied"), sem("xt_stored"), sem("xt_gathered")
        lg_ready, l_exped, result_ready, stored = sem("lg_ready"), sem("l_exped"), sem("result_ready"), sem("stored")

        def nodes(ap):
            return ap.rearrange("(b p) f -> p b f", p=NP)

        def items(turn, k, width=1):
            return bass.ds(U * turn + (k - U), width)

        def row_bank(r):
            return 1024 * (r % H) if r < 2 * H else NT * 512

        def sum_bank(h):
            return (4, 7)[h % 2]

        def wide_item(turn, k):
            return bass.ds(WIDE * turn + (k - WIDE), 1)

        FULL = 4 * NP

        block = ctx.enter_context(nc.Block())

        @block.sync
        def _(sp):
            edges = (TILES - 1) * ET
            for buf, ap, done in ((dst_i, dst, dst_loaded), (src_i, src, src_loaded)):
                sp.dma_start(buf[:, 0, :], ap[0:128 * ET].rearrange("(c e) -> c e", e=ET)).then_inc(done, 16)
                sp.wait_ge(filled, 2)
                sp.dma_start(buf[0:LOW_TILES - 1, 1, :],
                             ap[128 * ET:edges].rearrange("(c e) -> c e", e=ET)).then_inc(done, 16)
                sp.dma_start(buf[LOW_TILES - 1:LOW_TILES, 1, 0:TAIL],
                             ap[edges:E].rearrange("(c e) -> c e", c=1)).then_inc(done, 16)
            sp.dma_start(g1[:, :, 0:D], w1g.rearrange("(c p) f -> p c f", p=128)).then_inc(g1_loaded, 16)
            for n, ap in enumerate((att_s1, att_d1, att_l, att_r)):
                sp.dma_start(att[:, n, :], ap.rearrange("h f -> (h f)").partition_broadcast(128)).then_inc(att_loaded, 16)
            for n, ap in enumerate((b_r, bias1, gamma, beta, b2)):
                sp.dma_start(rows[:, n, :], ap.partition_broadcast(128)).then_inc(rows_loaded, 16)
            sp.dma_start(b1_row[:, :], b1.partition_broadcast(128)).then_inc(rows_loaded, 16)
            sp.dma_start(g3[:, :, 0:D], w3g.rearrange("(c p) f -> p c f", p=128)).then_inc(g3_loaded, 16)
            sp.dma_start(w1_sb[:, :, :], w1.rearrange("(c p) f -> p c f", p=128)).then_inc(w1_loaded, 16)
            sp.dma_start(w2_sb[:, :, :], w2.rearrange("(c p) f -> p c f", p=128)).then_inc(w2_loaded, 16)
            sp.dma_start(e_dst[0:NP, :], dst[0:N].rearrange("(b p) -> p b", p=NP), allow_slow_non_contiguous=True).then_inc(e_loaded, 16)
            sp.dma_start(e_src[0:NP, :], src[0:N].rearrange("(b p) -> p b", p=NP), allow_slow_non_contiguous=True).then_inc(e_loaded, 16)
            for b in range(NT):
                sp.wait_ge(q_copied, b + 1)
                sp.dma_start(q_dram[b * NP:(b + 1) * NP, :], q_sb[0:NP, b, :]).then_inc(q_stored, 16)
            sp.wait_ge(xt_copied, NT)
            sp.dma_start(nodes(xt_dram), h_sb[0:NP, :, :]).then_inc(xt_stored, 16)
            sp.dma_start(nodes(al_dram), h_sb[0:NP, :, D:D + H]).then_inc(xt_stored, 16)
            for b in range(NT):
                sp.wait_ge(result_ready, b + 1)
                sp.dma_start(out[b * NP:(b + 1) * NP, :], x0[0:NP, b, :]).then_inc(stored, 16)
            sp.wait_ge(stored, 16 * NT)
            sp.wait_ge(q_stored, 16 * NT)
            sp.wait_ge(xt_stored, 32)

        @block.gpsimd
        def _(pool):
            nc.gpsimd.memset(dst_i[:, 1, :], -1).then_inc(filled, 1)
            nc.gpsimd.memset(src_i[:, 1, :], 0).then_inc(filled, 1)
            nc.gpsimd.memset(ones[:, :], 1.0)
            nc.gpsimd.memset(upto[:, :], 1.0)
            nc.gpsimd.memset(ident[:, :], 0.0).then_inc(pool_step, 1)
            pool.wait_ge(pool_step, 1)
            nc.gpsimd.affine_select(out=upto[:, :], in_=upto[:, :], compare_op=ALU.is_ge, fill=0.0, base=0,
                                    pattern=[[1, 128]], channel_multiplier=-1)
            nc.gpsimd.affine_select(out=ident[:, :], in_=ident[:, :], compare_op=ALU.not_equal, fill=1.0, base=0,
                                    pattern=[[-1, 128]], channel_multiplier=1).then_inc(consts, 1)
            iota = nc.gpsimd.iota
            iota(iota1[:, :], [[1, ALL_ITEMS]], base=1, channel_multiplier=0, allow_small_or_imprecise_dtypes=True)
            iota(tile_no[:, :], [[1, NT]], base=0, channel_multiplier=0, allow_small_or_imprecise_dtypes=True)
            nc.gpsimd.memset(h_ones[:, :, :, :], 1.0)
            nc.gpsimd.memset(t_tile[:, :], 0)
            nc.gpsimd.memset(zeros[:, :], 0.0)
            iota(iota16[:, :], [[1, ALL_ITEMS]], base=0, channel_multiplier=0, allow_small_or_imprecise_dtypes=True)
            iota(iota32[:, :], [[1, 128]], base=0, channel_multiplier=0, allow_small_or_imprecise_dtypes=True).then_inc(filled, 1)
            pool.wait_ge(att_loaded, 64)
            pool.wait_ge(g1_loaded, 16)
            for n in range(4):
                if n == 2:
                    pool.wait_ge(g3_loaded, 16)
                g = g1 if n < 2 else g3
                nc.gpsimd.tensor_tensor(prod[n], g[:, :, 0:D], att[:, n, :].unsqueeze(1).to_broadcast([128, DC, D]),
                                        ALU.mult).then_inc(atts_ready, 1)
            pool.wait_ge(w1_loaded, 16)
            nc.gpsimd.tensor_tensor(w1_dif[:, :, :], w1_sb[:, 0:2, :], w1_sb[:, 2:4, :], ALU.subtract).then_inc(dif_ready, 1)
            pool.wait_ge(x_loaded, 16)
            pool.wait_ge(rows_loaded, 96)
            nc.gpsimd.tensor_tensor(tmp[0:NP, :, :], x0[0:NP, :, :], rows[0:NP, 0, :].unsqueeze(1).to_broadcast([NP, NT, D]),
                                    ALU.add).then_inc(pool_step, 1)
            pool.wait_ge(pool_step, 2)
            pool.wait_ge(lin_read, 2 * NT)
            nc.gpsimd.tensor_tensor(xr[0:NP, :, :], xr[0:NP, :, :], tmp[0:NP, :, :], ALU.add).then_inc(xr_ready, 1)

            pool.wait_ge(agg_done, NT)
            nc.gpsimd.memset(h_ones[:, :, :, F:F + 1], 1.0)
            pool.wait_ge(x_ready, NT)
            nc.gpsimd.tensor_tensor(x1_bias[0:NP, :, :], x1[0:NP, :, :], rows[0:NP, 1, :].unsqueeze(1).to_broadcast([NP, NT, D]),
                                    ALU.add).then_inc(bias_added, 1)
            for i in range(HEADS):
                h = i // NT
                pool.wait_ge(bent, i + 1)
                pool.wait_ge(row_copied, 2 * H + h + 1)
                w = score[i % SLOTS]
                nc.gpsimd.tensor_tensor(w, w, src_row[0:NP, h, :], ALU.add).then_inc(leaky, 1)

            pool.wait_ge(gidx_ready, 1)
            pool.wait_ge(q_stored, 16 * NT)

            def gather(k):
                pool.indirect_dma_start(ring[:, k, :], None, q_dram[:, :],
                                        bass.IndirectOffsetOnAxis(ap=gidx[:, k:k + 1], axis=0)).then_inc(gathered[k], 16)

            def gathers(first, last):
                with pool.Fori(first, last + 1) as before:
                    for k in range(U):
                        pool.wait_ge(q_stored, 16 * NT)
                        if k % HALF == 0:
                            pool.wait_ge(next_index[k // HALF], before)
                        pool.wait_ge(low_ready[k], before)
                        gather(k)

            for k in range(U):
                gather(k)
            gathers(1, FAST_TURNS - 1)
            n = pool.value_load(count[0:1, 0:1], min_val=0, max_val=ALL_ITEMS)
            with pool.If(n > FAST_ITEMS):
                gathers(FAST_TURNS, ALL_TURNS - 1)
            pool.wait_ge(e_loaded, 32)
            pool.wait_ge(xt_stored, 32)
            for b in range(NT):
                pool.indirect_dma_start(xt_g[0:NP, b, :], None, xt_dram[:, :],
                                        bass.IndirectOffsetOnAxis(ap=e_dst[0:NP, b:b + 1], axis=0)).then_inc(xt_gathered, 16)
                pool.indirect_dma_start(al_g[0:NP, b, :], None, al_dram[:, :],
                                        bass.IndirectOffsetOnAxis(ap=e_src[0:NP, b:b + 1], axis=0)).then_inc(xt_gathered, 16)
            pool.wait_ge(xt_gathered, 32 * NT)

        @block.scalar
        def _(act):
            act.preload_act_table(ACT.Copy)
            act.wait_ge(filled, 2)
            act.dma_start(x0[0:NP, :, :], nodes(x)).then_inc(x_loaded, 16)
            for n, ap in enumerate((w_l, w_r)):
                act.dma_start(w_lr[:, n, :, :], ap.rearrange("(c p) f -> p c f", p=128)).then_inc(lr_loaded, 16)

            def copy(o, i):
                return nc.scalar.activation(o, i, ACT.Copy)

            def copy_xT(n):
                act.wait_ge(xT_done, 3 * n + 1)
                copy(xT[:, 0, 0:FULL], ps[:, 0, 0:FULL]).then_inc(xT_copied_a, 1)
                act.wait_ge(xT_done, 3 * n + 3)
                copy(xT[:, :, FULL:N], ps[:, 2, 0:2 * NP].rearrange("p (c s) -> p c s", c=DC)).then_inc(xT_copied_a, 1)

            def root(n):
                act.wait_ge(var_ready, n + 1)
                nc.scalar.activation(std[0:NP, :], std[0:NP, :], ACT.Sqrt).then_inc(std_ready, 1)

            copy_xT(0)
            copy(xT[:, 1, 0:FULL], ps[:, 1, 0:FULL]).then_inc(xT_copied_v, 1)
            for n in range(2):
                act.wait_ge(wT_done, n + 1)
                copy(w_lrT[:, :, n * D:(n + 1) * D], ps[:, 3 + n, :].rearrange("p (c f) -> p c f", c=DC)).then_inc(wT_copied, 1)
            act.wait_ge(filled, 3)
            def linear_out(b):
                act.wait_ge(lin_done, b + 1)
                copy(xl[0:NP, b, 0:D], ps[0:NP, min(4 + b, 7), 0:D]).then_inc(lin_read, 1)
                copy(xr[0:NP, b, :], ps[0:NP, min(4 + b, 7), D:2 * D]).then_inc(lin_read, 1)

            for b in range(NT - 1):
                linear_out(b)

            def hots(g, first=False):
                for j in range(GROUPS):
                    if not first:
                        act.wait_ge(hots_used[j], g - 1)
                    for k in range(GROUP * j + DVE_HOTS, GROUP * (j + 1)):
                        last = nc.scalar.activation(apart[:, k, :], iota16[:, 0:128], ACT.Abs, bias=t_dst[:, wide_item(g, k)],
                                                    scale=-1.0)
                    last.then_inc(apart_done[j], 1)
                    if j:
                        near(g, j - 1)
                near(g, GROUPS - 1)

            def near(g, j):
                act.wait_ge(apart_done[j], g)
                group = slice(GROUP * j + DVE_HOTS, GROUP * (j + 1))
                nc.scalar.activation(hot_dst[:, group, :], apart[:, group, :], ACT.Relu, bias=ones[:, 0:1],
                                     scale=-1.0).then_inc(dst_built[j], 1)

            act.wait_ge(list_read, 1)
            n = act.value_load(count[0:1, 0:1], min_val=0, max_val=ALL_ITEMS)
            hots(1, first=True)
            act.preload_act_table(ACT.Relu)
            with act.Fori(2, FAST_WIDE + 1) as g:
                hots(g)
            with act.If(n > FAST_ITEMS):
                act.wait_ge(rest_read, 2)
                with act.Fori(FAST_WIDE + 1, ALL_WIDE + 1) as g:
                    hots(g)
            act.wait_ge(adj_done, 1)
            copy(adj[0:NP, :, 512:NW], flat[0:NP, 2560:2560 + 128 * NT].rearrange("p (b s) -> p b s", b=NT)).then_inc(adj_copied_a, 1)
            for b in (1, 3):
                copy(adj[0:NP, b, 0:512], ps[0:NP, b, :]).then_inc(adj_copied_a, 1)
            linear_out(NT - 1)
            for m in range(1, 7, 2):
                act.wait_ge(adjT_done, m + 1)
                copy(adjT[0:NP, m * FULL:(m + 1) * FULL], ps[0:NP, m, 0:FULL]).then_inc(adjT_copied_a, 1)
            root(0)
            act.preload_act_table(ACT.Exp)

            copy_xT(1)
            for b in range(NT):
                act.wait_ge(h_done, b + 1)
                copy(h_sb[0:NP, b, D:WX], ps[0:NP, 3 + b, D:WX]).then_inc(h_copied, 1)
                copy(h_ones[0:NP, b, :, 0:F], ps[0:NP, 3 + b, 0:D].rearrange("p (h f) -> p h f", h=H)).then_inc(h_copied, 1)

            def copy_row(r):
                act.wait_ge(row_done, r + 1)
                row = dst_row[0:NP, r - H, :] if H <= r < 2 * H else src_row[0:NP, r % H, :]
                at = row_bank(r)
                copy(row.rearrange("p (b s) -> p b s", b=NT),
                     flat[0:NP, at:at + NT * 128].rearrange("p (b s) -> p b s", b=NT)[:, :, 0:NP]).then_inc(row_copied, 1)

            for r in range(2 * H):
                copy_row(r)

            def bend(i):
                h, s = i // NT, i % NT
                if i >= SLOTS:
                    act.wait_ge(mixed, i - SLOTS + 1)
                nc.scalar.activation(score[i % SLOTS], dst_row[0:NP, h, :], ACT.Relu, bias=src4[0:NP, s, h:h + 1],
                                     scale=4.0).then_inc(bent, 1)

            def exp(i):
                h, s = i // NT, i % NT
                act.wait_ge(leaky, i + 1)
                nc.scalar.activation(score[i % SLOTS], score[i % SLOTS], ACT.Exp, bias=src02[0:NP, s, h:h + 1],
                                     scale=0.2).then_inc(exped, 1)

            act.wait_ge(row_copied, 2 * H)
            act.wait_ge(src_scaled, 2)

            def copy_sums(h):
                act.wait_ge(mixed, NT * (h + 1))
                if h >= 2:
                    act.wait_ge(sum_turned, h - 1)
                copy(xT[0:F + 1, h % 2, :], flat[0:F + 1, 1024 * (h % 2):1024 * (h % 2) + N]).then_inc(sumT_copied, 1)

            new_row = {0: 0, 2: 1, NT + 3: 2, 2 * NT + 3: 3}
            for i in range(HEADS + 2):
                if i < HEADS:
                    bend(i)
                    if i in new_row:
                        copy_row(2 * H + new_row[i])
                if i >= 2:
                    exp(i - 2)
                if i >= NT + 3 and i % NT == 3:
                    copy_sums(i // NT - 1)
            copy_sums(H - 1)
            root(1)
            root(2)

            copy_xT(2)
            for b in range(NT):
                act.wait_ge(q_done, b + 1)
                copy(q_sb[0:NP, b, :], ps[0:NP, 3 + b, :]).then_inc(q_copied, 1)
            for b in range(NT):
                act.wait_ge(p_added, b + 1)
                copy(parts[0:NP, 0, b, :], p_sb[0:NP, b, :]).then_inc(p_high, 1)

            def turn_hot(g, k):
                k, g = k % U, g + k // U
                act.wait_ge(hot_turned[k], g)
                before = (k - 2) % U
                if not (isinstance(g, int) and (g - (k < 2)) < 1):
                    act.wait_ge(p_spread[before], g - (1 if k < 2 else 0))
                copy(hotT[0:NP, k % 2, :], ps[0:NP, 7, 0:128]).then_inc(hotT_ready[k], 1)

            def relu(g, k):
                act.wait_ge(summed[k], g)
                if not (isinstance(g, int) and g - (k < 3) < 1):
                    act.wait_ge(scattered[(k - 3) % U], g - (1 if k < 3 else 0))
                nc.scalar.activation(whole[:, k % 3, :], ring[:, k, SPLIT:HID], ACT.Relu).then_inc(relued[k], 1)

            def relu_high(g, k):
                nc.scalar.activation(high[:, k % 3, :], ring[:, k, 0:SPLIT], ACT.Relu).then_inc(high_ready[k], 1)

            def act_turn(g, last=False):
                for k in range(U):
                    relu(g, k)
                    if not (last and k + 2 >= U):
                        turn_hot(g, k + 2)
                    relu_high(g, k)

            def act_turns(first, last):
                act.preload_act_table(ACT.Relu)
                turn_hot(first, 0)
                turn_hot(first, 1)
                act_turn(first)
                with act.Fori(first + 1, last) as g:
                    act_turn(g)
                act_turn(last, last=True)

            act_turns(1, FAST_TURNS)
            n = act.value_load(count[0:1, 0:1], min_val=0, max_val=ALL_ITEMS)
            with act.If(n > FAST_ITEMS):
                act_turns(FAST_TURNS + 1, ALL_TURNS)
            act.wait_ge(edges_done, 1)
            for b in (1, 3):
                copy(q_sb[0:NP, b, :], ps[0:NP, b, :]).then_inc(s_copied_a, 1)
            for c in (1, 3):
                act.wait_ge(sT_done, c + 1)
                copy(p_sb[:, c, 0:FULL], ps[:, c, 0:FULL]).then_inc(sT_copied_a, 1)
            act.wait_ge(sT_done, 5)
            copy(p_sb[:, 4, 0:FULL], ps[:, 4, 0:FULL]).then_inc(sT_copied_a, 1)
            root(3)

            copy_xT(3)
            for b in range(NT):
                act.wait_ge(xt_done, b + 1)
                copy(h_sb[0:NP, b, :], ps[0:NP, 3 + b, 0:WX]).then_inc(xt_copied, 1)
            act.wait_ge(lg_ready, 1)
            nc.scalar.activation(lg[0:NP, :, :], lg[0:NP, :, :], ACT.Exp).then_inc(l_exped, 1)
            root(4)

        @block.vector
        def _(dve):
            steps = [0]

            def step(ins):
                steps[0] += 1
                ins.then_inc(dve_step, 1)

            def settle():
                dve.wait_ge(dve_step, steps[0])

            V = nc.vector
            dve.wait_ge(dst_loaded, 48)
            step(V.tensor_copy(dst_f[:, :], dst_i[:, :, :].rearrange("p k e -> p (k e)")))
            settle()
            step(V.tensor_scalar(dst_tile[:, :], dst_f[:, :], 0.0, None, ALU.is_ge))
            for j in range(1, NT):
                settle()
                step(V.scalar_tensor_tensor(dst_tile[:, :], dst_f[:, :], float(NP * j), dst_tile[:, :], ALU.is_ge, ALU.add))
            settle()
            for b in range(NT):
                step(V.tensor_scalar(in_tile[:, b, :], dst_tile[:, :], float(b + 1), None, ALU.is_equal))
            settle()
            step(V.reduce_max(has[:, :], in_tile[:, :, :].rearrange("p b (k e) -> p (b k) e", k=2), AX.X))
            dve.wait_ge(consts, 1)
            settle()
            step(V.tensor_tensor_scan(has_sum[:, :], ones[:, 0:2 * NT], has[:, :], 0.0, ALU.mult, ALU.add))
            settle()
            V.tensor_tensor(has_before[:, :], has_sum[:, :], has[:, :], ALU.subtract).then_inc(has_ready, 1)
            for b in range(NT):
                V.tensor_scalar(dst_loc[:, b, :], dst_f[:, :], float(1 - NP * b), None, ALU.add)
            dve.wait_ge(src_loaded, 48)
            V.tensor_copy(src16[:, :, :], src_i[:, :, :]).then_inc(casts_done, 1)
            dve.wait_ge(pos_done, 1)
            dve.wait_ge(filled, 3)
            step(V.tensor_tensor(place[:, :], ps[:, 7, 0:2 * NT], has[:, :], ALU.mult))
            step(V.tensor_copy(count[0:1, :], ps[0:1, 7, 2 * NT:2 * NT + 1]))
            settle()
            for q in range(2 * NT):
                V.tensor_scalar(pick[:, q, 0:FAST_ITEMS], iota1[:, 0:FAST_ITEMS], place[:, q:q + 1], None,
                                ALU.is_equal).then_inc(picked, 1)
            V.tensor_copy(ident_r[:, :], ident[:, :])
            for n_att in range(4):
                g, at = (g1, D + H * n_att) if n_att < 2 else (g3, D + H * (n_att - 2))
                dve.wait_ge(atts_ready, n_att + 1)
                V.tensor_reduce(g[:, :, at:at + H], prod[n_att].rearrange("p c (h f) -> p c h f", h=H), AX.X,
                                ALU.add).then_inc(folded, 1)

            def read_list(lo, w, done):
                V.tensor_copy(t_src[:, lo:lo + w], ps[:, 0, 0:w])
                V.tensor_scalar(t_dst[:, lo:lo + w], ps[:, 1, 0:w], 1.0, None, ALU.subtract)
                V.tensor_copy(t_tile[0:1, PAD + lo:PAD + lo + w], ps[0:1, 2, 0:w]).then_inc(done, 1)

            dve.wait_ge(listed, 1)
            read_list(0, FAST_ITEMS, list_read)
            dve.wait_ge(list_read, 1)
            n = dve.value_load(count[0:1, 0:1], min_val=0, max_val=ALL_ITEMS)
            with dve.If(n > FAST_ITEMS):
                for r in range(2):
                    lo = FAST_ITEMS + r * REST_CHUNK
                    for q in range(2 * NT):
                        V.tensor_scalar(pick[:, q, :], iota1[:, lo:lo + REST_CHUNK], place[:, q:q + 1], None,
                                        ALU.is_equal).then_inc(rest_picked, 1)
                    dve.wait_ge(rest_listed, r + 1)
                    read_list(lo, REST_CHUNK, rest_read)
                    dve.wait_ge(rest_read, r + 1)

            def copy_xT(n):
                dve.wait_ge(xT_done, 3 * n + 2)
                V.tensor_copy(xT[:, 1, 0:FULL], ps[:, 1, 0:FULL]).then_inc(xT_copied_v, 1)


            def hots(g, first=False):
                for j in range(GROUPS):
                    if not first:
                        dve.wait_ge(hots_used[j], g - 1)
                    for k in range(GROUP * j, GROUP * (j + 1)):
                        if k < GROUP * j + DVE_HOTS:
                            V.tensor_scalar(hot_dst[:, k, :], iota16[:, 0:128], t_dst[:, wide_item(g, k)], None, ALU.is_equal)
                        last = V.tensor_scalar(hot_src[:, k, :], iota16[:, 0:NW], t_src[:, wide_item(g, k)], None, ALU.is_equal)
                    last.then_inc(src_built[j], 1)

            hots(1, first=True)
            with dve.Fori(2, FAST_WIDE + 1) as g:
                hots(g)
            with dve.If(n > FAST_ITEMS):
                with dve.Fori(FAST_WIDE + 1, ALL_WIDE + 1) as g:
                    hots(g)
            dve.wait_ge(adj_done, 1)
            for b in (0, 2, 4):
                V.tensor_copy(adj[0:NP, b, 0:512], ps[0:NP, b, :]).then_inc(adj_copied_v, 1)
            for m in range(0, 7, 2):
                w = min(FULL, NT * NT * NP - m * FULL)
                dve.wait_ge(adjT_done, m + 1)
                V.tensor_copy(adjT[0:NP, m * FULL:m * FULL + w], ps[0:NP, m, 0:w]).then_inc(adjT_copied_v, 1)
            dve.wait_ge(adjT_done, 7)
            for b in range(NT):
                blk = adj[0:NP, b, b * NP:(b + 1) * NP]
                step(V.tensor_tensor(blk, blk, ident[0:NP, 0:NP], ALU.add))
            dve.wait_ge(adj_copied_a, 3)
            settle()
            step(V.tensor_scalar(mask[0:NP, :, :], adj[0:NP, :, :], 0.0, NEG, ALU.is_equal, ALU.mult))

            norms = [0]

            def layer_norm(o, i, done=dve_step, begun=False):
                if not begun:
                    for b in range(NT):
                        step(V.bn_stats(stats[0:NP, b, :], i[0:NP, b, :]))
                settle()
                for b in range(NT):
                    step(V.bn_aggr(mv[0:NP, b, :], stats[0:NP, b, :]))
                settle()
                V.tensor_scalar(std[0:NP, :], mv[0:NP, :, 1], EPS, None, ALU.add).then_inc(var_ready, 1)
                norms[0] += 1
                dve.wait_ge(std_ready, norms[0])
                step(V.reciprocal(rstd[0:NP, :], std[0:NP, :]))
                settle()
                for b in range(NT):
                    V.tensor_scalar(o[0:NP, b, :], i[0:NP, b, :], mv[0:NP, b, 0:1], rstd[0:NP, b:b + 1],
                                    ALU.subtract, ALU.mult).then_inc(done, 1)
                if done is dve_step:
                    steps[0] += NT

            def row(n):
                return rows[0:NP, n, :].unsqueeze(1).to_broadcast([NP, NT, D])

            dve.wait_ge(xr_ready, 1)
            for b in range(NT):
                dve.wait_ge(agg_done, b + 1)
                step(V.tensor_scalar(rdeg[0:NP, b:b + 1], ps[0:NP, b, D:D + 1], 1.0, None, ALU.max))
                V.tensor_copy(deg[0:NP, b:b + 1], ps[0:NP, b, D:D + 1])
                settle()
                step(V.reciprocal(rdeg[0:NP, b:b + 1], rdeg[0:NP, b:b + 1]))
                settle()
                step(V.scalar_tensor_tensor(tmp[0:NP, b, :], ps[0:NP, b, 0:D], rdeg[0:NP, b:b + 1], xr[0:NP, b, :],
                                            ALU.mult, ALU.add))
                settle()
                step(V.bn_stats(stats[0:NP, b, :], tmp[0:NP, b, :]))
            layer_norm(x1, tmp, x_ready, begun=True)
            step(V.tensor_scalar(rdeg2[0:NP, :], deg[0:NP, :], 1e-8, None, ALU.add))
            settle()
            step(V.reciprocal(rdeg2[0:NP, :], rdeg2[0:NP, :]))

            copy_xT(1)

            for b in range(NT):
                at = (b * NT + b) * NP
                step(V.tensor_tensor(adjT[0:NP, at:at + NP], adjT[0:NP, at:at + NP], ident[0:NP, 0:NP], ALU.add))
            dve.wait_ge(h_copied, 2 * NT)
            V.tensor_scalar(src4[0:NP, :, :], h_sb[0:NP, :, D:D + H], 4.0, None, ALU.mult).then_inc(src_scaled, 1)
            V.tensor_scalar(src02[0:NP, :, :], h_sb[0:NP, :, D:D + H], 0.2, None, ALU.mult).then_inc(src_scaled, 1)
            last_steps = []

            def best(h, b):
                if b == 0:
                    dve.wait_ge(row_copied, h + 1)
                if len(last_steps) >= len(spare):
                    dve.wait_ge(dve_step, last_steps[-len(spare)])
                step(V.tensor_tensor_reduce(out=spare[len(last_steps) % len(spare)], in0=mask[0:NP, b, 0:N],
                                            in1=src_row[0:NP, h, :], scale=1.0, scalar=-3.0e38, op0=ALU.add,
                                            op1=ALU.max, accum_out=top[0:NP, b, h:h + 1]))
                last_steps.append(steps[0])

            def down_of(h):
                a_dst = h_sb[0:NP, :, D + H + h]
                settle()
                step(V.tensor_tensor(top[0:NP, :, h], top[0:NP, :, h], a_dst, ALU.add))
                settle()
                step(V.scalar_tensor_tensor(top[0:NP, :, h], top[0:NP, :, h], 0.2, top[0:NP, :, h], ALU.mult, ALU.max))
                settle()
                V.scalar_tensor_tensor(down[0:NP, :, h], top[0:NP, :, h], -5.0, a_dst, ALU.mult, ALU.add).then_inc(down_ready, 1)

            def weigh(i):
                s = i % NT
                dve.wait_ge(exped, i + 1)
                V.scalar_tensor_tensor(score[i % SLOTS], score[i % SLOTS], 1.0, adjT[0:NP, s * N:(s + 1) * N],
                                       ALU.min, ALU.mult).then_inc(weighted, 1)

            def take_sums(h):
                dve.wait_ge(sum_turned, h + 1)
                sums = ps[0:NP, sum_bank(h), 0:NT * (F + 1)].rearrange("p (b f) -> p b f", b=NT)
                step(V.tensor_scalar(rden[0:NP, :, h], sums[:, :, F], 1e-16, None, ALU.add))
                settle()
                step(V.reciprocal(rden[0:NP, :, h], rden[0:NP, :, h]))
                settle()
                V.tensor_tensor(tmp[0:NP, :, h * F:(h + 1) * F], sums[:, :, 0:F],
                                rden[0:NP, :, h].unsqueeze(2).to_broadcast([NP, NT, F]), ALU.mult).then_inc(sum_read, 1)

            settle()
            for h in range(2):
                for b in range(NT):
                    best(h, b)
                down_of(h)
            for h in range(H):
                for s in range(NT):
                    weigh(NT * h + s)
                    if h + 2 < H:
                        best(h + 2, s)
                    if h >= 1 and s == NT - 1:
                        take_sums(h - 1)
                if h + 2 < H:
                    down_of(h + 2)
            take_sums(H - 1)
            dve.wait_ge(sum_read, H)
            dve.wait_ge(bias_added, 1)
            step(V.tensor_tensor(tmp[0:NP, :, :], tmp[0:NP, :, :], x1_bias[0:NP, :, :], ALU.add))
            settle()
            layer_norm(tmp, tmp)
            settle()
            step(V.tensor_tensor(tmp[0:NP, :, :], tmp[0:NP, :, :], row(2), ALU.mult))
            settle()
            step(V.tensor_tensor(tmp[0:NP, :, :], tmp[0:NP, :, :], row(3), ALU.add))
            settle()
            step(V.scalar_tensor_tensor(tmp[0:NP, :, :], tmp[0:NP, :, :], 0.0, x1[0:NP, :, :], ALU.max, ALU.add))
            settle()
            layer_norm(x2, tmp, x_ready)

            V.tensor_copy(gidx[:, :], t_src[:, 0:U]).then_inc(gidx_ready, 1)
            copy_xT(2)
            for b in range(NT + 1):
                if b < NT:
                    dve.wait_ge(p_done, b + 1)
                    V.tensor_tensor(p_sb[0:NP, b, :], ps[0:NP, (b + 1) % 2, :], b1_row[0:NP, :], ALU.add).then_inc(p_added, 1)
                b -= 1
                if b < 0:
                    continue
                dve.wait_ge(p_high, b + 1)
                V.tensor_tensor(parts[0:NP, 1, b, :], p_sb[0:NP, b, :], parts[0:NP, 0, b, :].bitcast(f32), ALU.subtract).then_inc(parts_ready, 1)

            def build_hots(g, k):
                column = items(g, k, 2)
                k, g = k % U, g + k // U
                if not (isinstance(g, int) and g < 2):
                    for slot in (k, k + 1):
                        dve.wait_ge(scattered[slot], g - 1)
                V.tensor_tensor(hot[:, k:k + 2, :], iota32[:, :].unsqueeze(1).to_broadcast([128, 2, 128]),
                                t_dst[:, column].unsqueeze(2).to_broadcast([128, 2, 128]), ALU.is_equal).then_inc(hot_built[k // 2], 1)

            def add_p(g, k, index=True):
                dve.wait_ge(gathered[k], 16 * g)
                if index and k % HALF == HALF - 1:
                    lo = k + 1 - HALF
                    V.tensor_scalar(gidx[:, lo:k + 1], t_src[:, items(g, lo + U, HALF)], 0.0, None,
                                    ALU.add).then_inc(next_index[k // HALF], 1)
                dve.wait_ge(p_spread[k], g)
                V.tensor_tensor(ring[:, k, :], ring[:, k, :], ps[:, 5 + k % 2, :], ALU.add).then_inc(summed[k], 1)

            def rest(g, k):
                k, g = k % U, g + k // U
                dve.wait_ge(high_ready[k], g)
                V.scalar_tensor_tensor(low[:, k % 3, :], ring[:, k, 0:SPLIT], 0.0, high[:, k % 3, :].bitcast(f32),
                                       ALU.max, ALU.subtract).then_inc(low_ready[k], 1)

            def dve_turn(g, first=False, last=False, index=True):
                for k in range(U):
                    if k % 2 == 0 and not (last and k + 2 >= U):
                        build_hots(g, k + 2)
                    add_p(g, k, index)
                    if not (first and k < 1):
                        rest(g, k - 1)
                if last:
                    rest(g, U - 1)

            def dve_turns(first, last, index_last):
                build_hots(first, 0)
                dve_turn(first, first=True)
                with dve.Fori(first + 1, last) as g:
                    dve_turn(g)
                dve_turn(last, last=True, index=index_last)

            dve_turns(1, FAST_TURNS, False)
            n = dve.value_load(count[0:1, 0:1], min_val=0, max_val=ALL_ITEMS)
            with dve.If(n > FAST_ITEMS):
                for half in range(2):
                    lo = half * HALF
                    V.tensor_copy(gidx[:, lo:lo + HALF], t_src[:, FAST_ITEMS + lo:FAST_ITEMS + lo + HALF]).then_inc(next_index[half], 1)
                dve_turns(FAST_TURNS + 1, ALL_TURNS, False)
            dve.wait_ge(edges_done, 1)
            for b in (0, 2, 4):
                V.tensor_copy(q_sb[0:NP, b, :], ps[0:NP, b, :]).then_inc(s_copied_v, 1)
            for c in (0, 2):
                dve.wait_ge(sT_done, c + 1)
                V.tensor_copy(p_sb[:, c, 0:FULL], ps[:, c, 0:FULL]).then_inc(sT_copied_v, 1)
            for b in range(NT):
                step(V.scalar_tensor_tensor(tmp[0:NP, b, :], rows[0:NP, 4, :], deg[0:NP, b:b + 1], x2[0:NP, b, :],
                                            ALU.mult, ALU.bypass))
            settle()
            for b in range(NT):
                dve.wait_ge(conv_done, b + 1)
                step(V.tensor_tensor(tmp[0:NP, b, :], tmp[0:NP, b, :], ps[0:NP, (5 + b) % 8, 0:D], ALU.add))
            settle()
            for b in range(NT):
                step(V.scalar_tensor_tensor(tmp[0:NP, b, :], tmp[0:NP, b, :], rdeg2[0:NP, b:b + 1], x2[0:NP, b, :],
                                            ALU.mult, ALU.add))
            settle()
            layer_norm(x1, tmp, x_ready)

            copy_xT(3)
            dve.wait_ge(xt_gathered, 32 * NT)
            al = lg[0:NP, :, :]
            step(V.tensor_tensor(al, al_g[0:NP, :, :], xt_g[0:NP, :, D + H:D + 2 * H], ALU.add))
            settle()
            step(V.scalar_tensor_tensor(al, al, 0.01, al, ALU.mult, ALU.max))
            settle()
            step(V.tensor_reduce(lmax[0:NP, :], al, AX.X, ALU.max))
            settle()
            V.tensor_tensor(al, al, lmax[0:NP, :].unsqueeze(2).to_broadcast([NP, NT, H]), ALU.subtract).then_inc(lg_ready, 1)
            dve.wait_ge(l_exped, 1)
            step(V.tensor_reduce(lsum[0:NP, :], al, AX.X, ALU.add))
            settle()
            step(V.reciprocal(lsum[0:NP, :], lsum[0:NP, :]))
            settle()
            step(V.tensor_tensor(al, al, lsum[0:NP, :].unsqueeze(2).to_broadcast([NP, NT, H]), ALU.mult))
            settle()
            for b in range(NT):
                step(V.tensor_tensor(tmp[0:NP, b, :].rearrange("p (h f) -> p h f", h=H),
                                     xt_g[0:NP, b, 0:D].rearrange("p (h f) -> p h f", h=H),
                                     lg[0:NP, b, :].unsqueeze(2).to_broadcast([NP, H, F]), ALU.mult))
            settle()
            step(V.tensor_reduce(x2[0:NP, :, 0:F], tmp[0:NP, :, :].rearrange("p b (h f) -> p b f h", h=H), AX.X, ALU.add))
            settle()
            for b in range(NT):
                step(V.tensor_tensor(tmp[0:NP, b, :].rearrange("p (h f) -> p h f", h=H),
                                     x1[0:NP, b, :].rearrange("p (h f) -> p h f", h=H),
                                     x2[0:NP, b, 0:F].unsqueeze(1).to_broadcast([NP, H, F]), ALU.add))
            settle()
            layer_norm(x0, tmp, result_ready)

        @block.tensor
        def _(pe):
            def mm(o, a, b, start, stop):
                return nc.tensor.matmul(o, a, b, start=start, stop=stop, skip_group_check=True)

            def turn(n, xs):
                for b in range(NT - 1):
                    if n:
                        pe.wait_ge(x_ready, NT * (n - 1) + b + 1)
                    for c in range(DC):
                        last = nc.tensor.transpose(ps[:, c, b * NP:(b + 1) * NP], xs[0:NP, b, c * 128:(c + 1) * 128],
                                                   ident[0:NP, 0:NP])
                        if b == NT - 2:
                            last.then_inc(xT_done, 1)
                if n:
                    pe.wait_ge(x_ready, NT * n)
                for c in range(DC):
                    last = nc.tensor.transpose(ps[:, 2, c * NP:(c + 1) * NP], xs[0:NP, NT - 1, c * 128:(c + 1) * 128],
                                               ident[0:NP, 0:NP])
                last.then_inc(xT_done, 1)

            def turned(n):
                pe.wait_ge(xT_copied_a, 2 * n + 2)
                pe.wait_ge(xT_copied_v, n + 1)

            def make_list(w, sem_in, base, done):
                pe.wait_ge(sem_in, base)
                for q in range(2 * NT):
                    b, kt = q // 2, q % 2
                    one = pick[:, q, 0:w]
                    mm(ps[:, 0, 0:w], src16[:, kt, :], one, q == 0, q == 2 * NT - 1)
                    mm(ps[:, 1, 0:w], dst_loc[:, b, kt * ET:(kt + 1) * ET], one, q == 0, q == 2 * NT - 1)
                    last = mm(ps[0:1, 2, 0:w], tile_no[:, b:b + 1], one, q == 0, q == 2 * NT - 1)
                last.then_inc(done, 1)

            def linear(b):
                for c in range(DC):
                    last = mm(ps[0:NP, min(4 + b, 7), :], xT[:, c, b * NP:(b + 1) * NP], w_lrT[:, c, :], c == 0, c == DC - 1)
                last.then_inc(lin_done, 1)

            pe.wait_ge(consts, 1)
            pe.wait_ge(x_loaded, 16)
            turn(0, x0)
            pe.wait_ge(lr_loaded, 32)
            for n in range(2):
                for c in range(DC):
                    for o in range(DC):
                        at = c * D + o * 128
                        last = nc.tensor.transpose(ps[:, 3 + n, at:at + 128], w_lr[:, n, o, c * 128:(c + 1) * 128], ident[:, :])
                last.then_inc(wT_done, 1)
            turned(0)
            pe.wait_ge(wT_copied, 2)
            linear(0)
            pe.wait_ge(has_ready, 1)
            mm(ps[:, 7, 0:2 * NT], upto[:, :], has[:, :], True, False)
            mm(ps[:, 7, 0:2 * NT], ones[:, :], has_before[:, :], False, True)
            mm(ps[:, 7, 2 * NT:2 * NT + 1], ones[:, :], has_sum[:, 2 * NT - 1:2 * NT], True, True).then_inc(pos_done, 1)
            linear(1)
            pe.wait_ge(casts_done, 1)
            make_list(FAST_ITEMS, picked, 2 * NT, listed)
            linear(2)
            linear(3)
            pe.wait_ge(list_read, 1)
            n_items = pe.value_load(count[0:1, 0:1], min_val=0, max_val=ALL_ITEMS)
            with pe.If(n_items > FAST_ITEMS):
                for r in range(2):
                    make_list(REST_CHUNK, rest_picked, 2 * NT * (r + 1), rest_listed)
                    pe.wait_ge(rest_read, r + 1)
            pe.wait_ge(lin_read, 2 * NT - 2)
            for k in range(7):
                mm(ps[:, k, :], zeros[:, 0:128], zeros[:, :], True, True)

            def tiles_at(at, width):
                _, values = nc.values_load_multi_w_load_instructions(
                    t_tile[0:1, bass.ds(at, width)], engines=[mybir.EngineType.PE], min_val=0, max_val=NT - 1,
                    skip_runtime_bounds_check_because="a node tile's number: one of 0 to NT - 1, or 0 where no item is")
                return values

            def adjacency(g):
                tiles = tiles_at(WIDE * g + (PAD - WIDE), WIDE)
                for j in range(GROUPS):
                    pe.wait_ge(src_built[j], g)
                    pe.wait_ge(dst_built[j], g)
                    for k in range(GROUP * j, GROUP * (j + 1)):
                        mm(ps[:, bass.ds(tiles[k], 1), :], hot_dst[:, k, :], hot_src[:, k, 0:512], False, True)
                        last = mm(flat[:, bass.ds(tiles[k] * 128 + 2560, 128)], hot_dst[:, k, :], hot_src[:, k, 512:NW],
                                  False, True)
                    last.then_inc(hots_used[j], 1)

            with pe.Fori(1, FAST_WIDE + 1) as g:
                adjacency(g)
            with pe.If(n_items > FAST_ITEMS):
                with pe.Fori(FAST_WIDE + 1, ALL_WIDE + 1) as g:
                    adjacency(g)
            mm(ps[:, 6, :], zeros[:, 0:128], zeros[:, :], False, True).then_inc(adj_done, 1)
            linear(NT - 1)
            pe.wait_ge(adj_copied_v, 3)
            pe.wait_ge(adj_copied_a, 3)
            for n in range(NT * NT):
                s, d = n // NT, n % NT
                last = nc.tensor.transpose(ps[0:NP, n // 4, (n % 4) * NP:(n % 4 + 1) * NP], adj[0:NP, d, s * NP:(s + 1) * NP],
                                           ident[0:NP, 0:NP])
                if n % 4 == 3 or n == NT * NT - 1:
                    last.then_inc(adjT_done, 1)
            pe.wait_ge(lin_read, 2 * NT)
            pe.wait_ge(adjT_copied_v, 4)
            pe.wait_ge(adjT_copied_a, 3)
            for b in range(NT):
                for s in range(NT):
                    at = (s * NT + b) * NP
                    last = mm(ps[0:NP, b, 0:D + 1], adjT[0:NP, at:at + NP], xl[0:NP, s, :], s == 0, s == NT - 1)
                last.then_inc(agg_done, 1)
            turn(1, x1)
            pe.wait_ge(folded, 4)
            turned(1)

            def project(g, done):
                for b in range(NT):
                    for c in range(DC):
                        last = mm(ps[0:NP, 3 + b, 0:WX], xT[:, c, b * NP:(b + 1) * NP], g[:, c, :], c == 0, c == DC - 1)
                    last.then_inc(done, 1)

            project(g1, h_done)


            def spread_row(r, columns):
                for b in range(NT):
                    at = row_bank(r) + 128 * b
                    last = mm(flat[0:NP, at:at + NP], columns[0:NP, b, r % H:r % H + 1].to_broadcast([NP, NP]),
                              ident[0:NP, 0:NP], True, True)
                last.then_inc(row_done, 1)

            pe.wait_ge(h_copied, 2 * NT)
            for r in range(H):
                spread_row(r, h_sb[:, :, D:D + H])
            for r in range(H, 2 * H):
                pe.wait_ge(row_copied, r - H + 1)
                spread_row(r, h_sb[:, :, D + H:D + 2 * H])

            def spread_down(h):
                pe.wait_ge(down_ready, h + 1)
                pe.wait_ge(row_copied, 2 * H + h)
                spread_row(2 * H + h, down)

            def turn_sums(h):
                pe.wait_ge(sumT_copied, h + 1)
                if h >= 2:
                    pe.wait_ge(sum_read, h - 1)
                for b in range(NT):
                    last = nc.tensor.transpose(ps[0:NP, sum_bank(h), b * (F + 1):(b + 1) * (F + 1)],
                                               xT[0:F + 1, h % 2, b * NP:(b + 1) * NP], ident[0:F + 1, 0:F + 1])
                last.then_inc(sum_turned, 1)

            spread_down(0)
            for i in range(HEADS):
                h, s = i // NT, i % NT
                if s == 0 and h + 1 < H:
                    spread_down(h + 1)
                if s == 0 and h >= 2:
                    pe.wait_ge(sumT_copied, h - 1)
                if s == 3 and h >= 1:
                    turn_sums(h - 1)
                pe.wait_ge(weighted, i + 1)
                for lo, hi in ((0, 512), (512, N)):
                    at = 1024 * (h % 2)
                    last = mm(flat[0:F + 1, at + lo:at + hi], h_ones[0:NP, s, h, :], score[i % SLOTS][:, lo:hi],
                              s == 0, s == NT - 1)
                last.then_inc(mixed, 1)
            turn_sums(H - 1)
            turn(2, x2)
            turned(2)
            pe.wait_ge(w1_loaded, 16)
            for b in range(NT):
                for c in range(DC):
                    last = mm(ps[0:NP, 3 + b, :], xT[:, c, b * NP:(b + 1) * NP], w1_sb[:, DC + c, :], c == 0, c == DC - 1)
                last.then_inc(q_done, 1)
            pe.wait_ge(dif_ready, 1)
            for b in range(NT):
                if b >= 2:
                    pe.wait_ge(p_added, b - 1)
                for c in range(DC):
                    last = mm(ps[0:NP, (b + 1) % 2, :], xT[:, c, b * NP:(b + 1) * NP], w1_dif[:, c, :], c == 0, c == DC - 1)
                last.then_inc(p_done, 1)
            pe.wait_ge(p_added, NT)
            pe.wait_ge(q_copied, NT)
            for k in range(NT):
                mm(ps[:, k, :], zeros[:, 0:128], zeros[:, :], True, True)
            pe.wait_ge(parts_ready, NT)

            def turn_hot(g, k):
                k, g = k % U, g + k // U
                if k % 2 == 0:
                    pe.wait_ge(hot_built[k // 2], g)
                if not (isinstance(g, int) and g - (k < 1) < 1):
                    pe.wait_ge(hotT_ready[(k - 1) % U], g - (1 if k < 1 else 0))
                nc.tensor.transpose(ps[:, 7, 0:128].bitcast(f32r), hot[:, k, :], ident_r[:, :]).then_inc(hot_turned[k], 1)

            def spread_p(g, k, tile):
                k, g = k % U, g + k // U
                pe.wait_ge(hotT_ready[k], g)
                if not (isinstance(g, int) and g - (k < 2) < 1):
                    pe.wait_ge(summed[(k - 2) % U], g - (1 if k < 2 else 0))
                for r in range(2):
                    last = mm(ps[:, 5 + k % 2, :], hotT[0:NP, k % 2, :], parts[0:NP, r, bass.ds(tile, 1), :], r == 0, r == 1)
                last.then_inc(p_spread[k], 1)

            def scatter(g, k, tile):
                k, g = k % U, g + k // U
                pe.wait_ge(relued[k], g)
                mm(flat[:, bass.ds(tile * 512 + SPLIT, HID - SPLIT)], hot[:, k, :].bitcast(f32), whole[:, k % 3, :], False, True)
                pe.wait_ge(low_ready[k], g)
                mm(flat[:, bass.ds(tile * 512, SPLIT)], hot[:, k, :], high[:, k % 3, :], False, True)
                mm(flat[:, bass.ds(tile * 512, SPLIT)], hot[:, k, :], low[:, k % 3, :], False, True).then_inc(scattered[k], 1)

            def pe_turn(g, first=False, last=False, tiles=None):
                tiles = tiles or tiles_at(U * g - U, PAD + U + 1)
                if first:
                    spread_p(g, 0, tiles[PAD])
                for k in range(U):
                    if not (first and k < 2):
                        scatter(g, k - 2, tiles[k])
                    if not (last and k + 1 >= U):
                        spread_p(g, k + 1, tiles[PAD + k + 1])
                    if not (last and k + 2 >= U):
                        turn_hot(g, k + 2)
                if last:
                    scatter(g, U - 2, tiles[U])
                    scatter(g, U - 1, tiles[U + 1])

            def pe_turns(first, last):
                turn_hot(first, 0)
                turn_hot(first, 1)
                pe_turn(first, first=True)
                start = first + 1 + (last - first - 1) % LOADED
                for g in range(first + 1, start):
                    pe_turn(g)
                with pe.Fori(start, last, LOADED) as g:
                    tiles = tiles_at(U * g - U, PAD + LOADED * U + 1)
                    for j in range(LOADED):
                        pe_turn(g + j, tiles=tiles[U * j:])
                pe_turn(last, last=True)

            pe_turns(1, FAST_TURNS)
            with pe.If(n_items > FAST_ITEMS):
                pe_turns(FAST_TURNS + 1, ALL_TURNS)
            mm(ps[:, 4, :], zeros[:, 0:128], zeros[:, :], False, True).then_inc(edges_done, 1)
            pe.wait_ge(s_copied_a, 2)
            pe.wait_ge(s_copied_v, 3)
            for c in range(4):
                for b in range(4):
                    last = nc.tensor.transpose(ps[:, c, b * NP:(b + 1) * NP], q_sb[0:NP, b, c * 128:(c + 1) * 128],
                                               ident[0:NP, 0:NP])
                last.then_inc(sT_done, 1)
            for c in range(4):
                last = nc.tensor.transpose(ps[:, 4, c * NP:(c + 1) * NP], q_sb[0:NP, 4, c * 128:(c + 1) * 128], ident[0:NP, 0:NP])
            last.then_inc(sT_done, 1)
            pe.wait_ge(w2_loaded, 16)
            pe.wait_ge(sT_copied_a, 3)
            pe.wait_ge(sT_copied_v, 2)
            for b in range(NT):
                for c in range(4):
                    lhs = p_sb[:, c, b * NP:(b + 1) * NP] if b < 4 else p_sb[:, 4, c * NP:(c + 1) * NP]
                    last = mm(ps[0:NP, (5 + b) % 8, 0:D], lhs, w2_sb[:, c, :], c == 0, c == 3)
                last.then_inc(conv_done, 1)
            turn(3, x1)
            turned(3)
            project(g3, xt_done)


_INS = ['x', 'src', 'dst', 'L0_gnn_W_l', 'L0_gnn_W_r', 'L0_gnn_b_r', 'L1_gnn_W', 'L1_gnn_att_src', 'L1_gnn_att_dst',
        'L1_gnn_bias', 'L1_gnn_ln_gamma', 'L1_gnn_ln_beta', 'L2_gnn_W1', 'L2_gnn_b1', 'L2_gnn_W2', 'L2_gnn_b2',
        'L3_gnn_weight', 'L3_gnn_attn_l', 'L3_gnn_attn_r']


def kernel(**inputs):
    import numpy as _np
    import concourse.bacc as _bacc
    from concourse import mybir as _mybir
    from concourse.bass_utils import run_bass_kernel_spmd as _run

    nc = _bacc.Bacc("TRN2", target_bir_lowering=False, num_devices=1)
    arrays, args = {}, []
    for name in _INS:
        a = _np.ascontiguousarray(inputs[name])
        arrays[f"in_{name}"] = a
        args.append(nc.dram_tensor(f"in_{name}", a.shape, _mybir.dt.from_np(a.dtype), kind="ExternalInput").ap())
    args.append(nc.dram_tensor("out_0", (N, D), _mybir.dt.float32, kind="ExternalOutput").ap())
    program(nc, *args)
    r = _run(nc, [arrays], core_ids=[0])
    return r.results[0]["out_0"]
```

```python
import concourse.bass as bass
from concourse import mybir
from contextlib import ExitStack

N, D, E = 625, 256, 20000
NP = 125
NT = N // NP
H, F = 4, 64
HID = 512
DC = D // 128
ET = 128
TILES = -(-E // ET)
TAIL = E - (TILES - 1) * ET
LOW_TILES = TILES - 128
U = 6
TOGETHER = 4
HALF = U // 2
GROUP = 6
GROUPS = 3
WIDE = GROUP * GROUPS
DVE_HOTS = 2
FAST_WIDE = -(-(TILES + NT - 1) // WIDE)
FAST_ITEMS = FAST_WIDE * WIDE
FAST_TURNS = FAST_ITEMS // U
ALL_WIDE = -(-(TILES * NT) // WIDE)
ALL_ITEMS = ALL_WIDE * WIDE
ALL_TURNS = ALL_ITEMS // U
REST_CHUNK = (ALL_ITEMS - FAST_ITEMS) // 2
PAD = 2
NW = 640
SPLIT = 256
WX = D + 2 * H
NEG = -1.0e30
EPS = 1e-5
AHEAD = 2
HEADS = NT * H


def program(nc, x, src, dst, w_l, w_r, b_r, w1g, att_s1, att_d1, bias1, gamma, beta,
            w1, b1, w2, b2, w3g, att_l, att_r, out):
    f32, f16, i32 = mybir.dt.float32, mybir.dt.float16, mybir.dt.int32
    f32r = mybir.dt.float32r
    ALU, ACT, AX = mybir.AluOpType, mybir.ActivationFunctionType, mybir.AxisListType

    ctx = ExitStack()
    with ctx:
        def sb(name, shape, dt):
            return ctx.enter_context(nc.sbuf_tensor(name, shape, dt))

        def sem(name):
            return ctx.enter_context(nc.semaphore(name))

        def sems(name):
            return [sem(f"{name}{k}") for k in range(U)]

        def group_sems(name):
            return [sem(f"{name}{k}") for k in range(GROUPS)]

        iota16 = sb("iota16", [128, ALL_ITEMS], f16)
        iota1 = sb("iota1", [128, ALL_ITEMS], f16)
        iota32 = sb("iota32", [128, 128], f32)
        ident = sb("ident", [128, 128], f32)
        ident_r = sb("ident_r", [128, 128], f32r)
        upto = sb("upto", [128, 128], f32)
        ones = sb("ones", [128, 128], f32)
        zeros = sb("zeros", [128, 512], f16)
        tile_no = sb("tile_no", [128, NT], f16)
        w_lr = sb("w_lr", [128, 2, 2, D], f32)
        w_lrT = sb("w_lrT", [128, DC, 2 * D], f32)
        g1 = sb("g1", [128, DC, WX], f32)
        g3 = sb("g3", [128, DC, WX], f32)
        att = sb("att", [128, 4, D], f32)
        w1_sb = sb("w1_sb", [128, 4, HID], f32)
        w1_dif = sb("w1_dif", [128, DC, HID], f32)
        w2_sb = sb("w2_sb", [128, 4, D], f32)
        rows = sb("rows", [128, 5, D], f32)
        b1_row = sb("b1_row", [128, HID], f32)
        src_i = sb("src_i", [128, 2, ET], i32)
        dst_i = sb("dst_i", [128, 2, ET], i32)
        src16 = sb("src16", [128, 2, ET], f16)
        dst_f = sb("dst_f", [128, 2 * ET], f32)
        from_tile = sb("from_tile", [128, 2 * NT + 2], f32)
        in_some = sb("in_some", [128, 2 * NT], f32)
        has = sb("has", [128, 2 * NT], f32)
        has_sum = sb("has_sum", [128, 2 * NT], f32)
        has_before = sb("has_before", [128, 2 * NT], f32)
        place = sb("place", [128, 2 * NT], f32)
        t_src = sb("t_src", [128, ALL_ITEMS + TOGETHER * U], f32)
        t_dst = sb("t_dst", [128, ALL_ITEMS + TOGETHER * U], f32)
        t_tile = sb("t_tile", [1, ALL_ITEMS + (TOGETHER + 1) * U], i32)
        count = sb("count", [1, 1], i32)
        adj = sb("adj", [128, NT, NW], f32)
        deg = sb("deg", [128, NT], f32)
        rdeg = sb("rdeg", [128, NT], f32)
        rdeg2 = sb("rdeg2", [128, NT], f32)
        x0 = sb("x0", [128, NT, D], f32)
        x1 = sb("x1", [128, NT, D], f32)
        x2 = sb("x2", [128, NT, D], f32)
        x1_bias = sb("x1_bias", [128, NT, D], f32)
        x2_b2 = x1_bias
        share = sb("share", [128, NT], f32)
        xT = sb("xT", [128, DC, N], f32)
        tmp = sb("tmp", [128, NT, D], f32)
        h_sb = sb("h_sb", [128, NT, WX], f32)
        stats = sb("stats", [128, NT, 6], f32)
        mv = sb("mv", [128, NT, 2], f32)
        std = sb("std", [128, NT], f32)
        spare = [x2[:, :, :].rearrange("p b f -> p (b f)")[0:NP, k * N:(k + 1) * N] for k in range(2)]
        rstd = sb("rstd", [128, NT], f32)
        arena = sb("arena", [128, NT * NW + NT * N + 2 * H * N + N], f32)
        halves = arena[:, :].bitcast(f16)
        c0 = 2 * NT * REST_CHUNK
        c1 = c0 + 2 * (2 * NT * ET)
        c2 = c1 + NT * 2 * ET
        pick = halves[:, 0:c0].rearrange("p (q i) -> p q i", q=2 * NT)
        compared = arena[:, c0 // 2:c0 // 2 + 2 * NT * ET].rearrange("p (q e) -> p q e", q=2 * NT)
        dst_loc = halves[:, c1:c2].rearrange("p (b e) -> p b e", b=NT)
        c3 = c2 + WIDE * NW
        hot_src = halves[:, c2:c3].rearrange("p (k s) -> p k s", k=WIDE)
        c4 = c3 + WIDE * 128
        hot_dst = halves[:, c3:c4].rearrange("p (k s) -> p k s", k=WIDE)
        apart = halves[:, c4:c4 + WIDE * 128].rearrange("p (k s) -> p k s", k=WIDE)
        a0 = NT * NW
        mask = arena[:, 0:a0].rearrange("p (b s) -> p b s", b=NT)
        adjT = arena[:, a0:a0 + NT * N]
        a1 = a0 + NT * N
        src_row = arena[:, a1:a1 + H * N].rearrange("p (h s) -> p h s", h=H)
        a2 = a1 + H * N
        dst_row = arena[:, a2:a2 + H * N].rearrange("p (h s) -> p h s", h=H)
        a3 = a2 + H * N
        top = sb("top", [128, NT, H], f32)
        down = sb("down", [128, NT, H], f32)
        rden = sb("rden", [128, NT, H], f32)
        ring = arena[:, 0:U * HID].rearrange("p (i f) -> p i f", i=U)
        p0 = U * HID
        p_sb = arena[:, p0:p0 + NT * HID].rearrange("p (b f) -> p b f", b=NT)
        sT = arena[:, 0:NT * 4 * NP].rearrange("p (b s) -> p b s", b=NT)
        parts = sb("parts", [128, 2, NT, HID], f32r)
        rounded = sb("rounded", [128, 6, SPLIT], f32r)
        high, low = rounded[:, 0:3, :], rounded[:, 3:6, :]
        whole = sb("whole", [128, 3, HID - SPLIT], f32)
        q_sb = sb("q_sb", [128, NT, HID], f32)
        q_flat = q_sb[:, :, :].rearrange("p b f -> p (b f)")
        score = [q_flat[0:NP, k * N:(k + 1) * N] for k in range(4)] + [arena[0:NP, a3:a3 + N]]
        score += [x0[:, :, :].rearrange("p b f -> p (b f)")[0:NP, k * N:(k + 1) * N] for k in range(2)]
        SLOTS = len(score)
        prod = [q_sb[:, n, :].rearrange("p (c f) -> p c f", c=DC) for n in range(4)]
        h_ones = sb("h_ones", [128, NT, H, F + 1], f32)
        xl, xr = h_ones[:, :, :, :].rearrange("p b h f -> p b (h f)")[:, :, 0:D + 1], x1_bias
        src4 = sb("src4", [128, NT, H], f32)
        src02 = sb("src02", [128, NT, H], f32)
        hot = sb("hot", [128, U, 128], f32r)
        hotT = sb("hotT", [128, 2, 128], f32r)
        gidx = sb("gidx", [128, U], i32)
        e_src = sb("e_src", [128, NT], i32)
        node_no = sb("node_no", [128, NT], f32)
        dst_row_i = arena[:, a2:a2 + N].bitcast(i32)
        dst_row_f = arena[:, a2 + N:a2 + 2 * N]
        flat_parts = parts[:, :, :, :].rearrange("p r b f -> p (r b f)")
        e_hot = flat_parts[:, 0:NT * N].rearrange("p (b e) -> p b e", b=NT)
        xt_high = flat_parts[:, NT * N:NT * (N + WX)].rearrange("p (b f) -> p b f", b=NT)
        xt_low = rounded[:, :, :].rearrange("p k f -> p (k f)")[:, 0:NT * WX].rearrange("p (b f) -> p b f", b=NT)
        al_sb = sb("al_sb", [128, NT, H], f32)
        al_g = sb("al_g", [128, NT, H], f32)
        lg = sb("lg", [128, NT, H], f32)
        lmax = sb("lmax", [128, NT], f32)
        lsum = sb("lsum", [128, NT], f32)
        ps = ctx.enter_context(nc.psum_tensor("ps", [128, 8, 512], f32))
        flat = ps[:, :, :].rearrange("p b f -> p (b f)")

        q_dram = nc.dram_tensor("q_table", (N, HID), f32).ap()
        al_dram = nc.dram_tensor("al_table", (N, H), f32).ap()

        src_loaded, dst_loaded, x_loaded = sem("src_loaded"), sem("dst_loaded"), sem("x_loaded")
        lr_loaded, g1_loaded, g3_loaded = sem("lr_loaded"), sem("g1_loaded"), sem("g3_loaded")
        att_loaded, w1_loaded, w2_loaded = sem("att_loaded"), sem("w1_loaded"), sem("w2_loaded")
        rows_loaded, e_loaded = sem("rows_loaded"), sem("e_loaded")
        filled, consts, pool_step = sem("filled"), sem("consts"), sem("pool_step")
        dve_step, al_copied = sem("dve_step"), sem("al_copied")
        has_ready, pos_done, casts_done, picked = sem("has_ready"), sem("pos_done"), sem("casts_done"), sem("picked")
        listed, list_read = sem("listed"), sem("list_read")
        rest_picked, rest_listed, rest_read = sem("rest_picked"), sem("rest_listed"), sem("rest_read")
        atts_ready, folded = sem("atts_ready"), sem("folded")
        dif_ready, xr_ready = sem("dif_ready"), sem("xr_ready")
        wT_done, wT_copied = sem("wT_done"), sem("wT_copied")
        xT_done, xT_copied_a, xT_copied_v = sem("xT_done"), sem("xT_copied_a"), sem("xT_copied_v")
        lin_done, lin_read = sem("lin_done"), sem("lin_read")
        src_built, apart_done, dst_built = group_sems("src_built"), group_sems("apart_done"), group_sems("dst_built")
        hots_used, adj_done = group_sems("hots_used"), sem("adj_done")
        adj_copied_v, adj_copied_a = sem("adj_copied_v"), sem("adj_copied_a")
        adjT_done, adjT_copied_v, adjT_copied_a = sem("adjT_done"), sem("adjT_copied_v"), sem("adjT_copied_a")
        agg_done, var_ready, std_ready, x_ready = sem("agg_done"), sem("var_ready"), sem("std_ready"), sem("x_ready")
        h_done, h_copied, row_done, row_copied = sem("h_done"), sem("h_copied"), sem("row_done"), sem("row_copied")
        src_scaled, down_ready = sem("src_scaled"), sem("down_ready")
        bent, leaky, exped, weighted, mixed = sem("bent"), sem("leaky"), sem("exped"), sem("weighted"), sem("mixed")
        bias_added = sem("bias_added")
        sumT_copied, sum_turned, sum_read = sem("sumT_copied"), sem("sum_turned"), sem("sum_read")
        q_done, q_copied, q_stored = sem("q_done"), sem("q_copied"), sem("q_stored")
        p_done, p_added, p_high, parts_ready = sem("p_done"), sem("p_added"), sem("p_high"), sem("parts_ready")
        high_ready, low_ready = sems("high_ready"), sems("low_ready")
        gidx_ready = sem("gidx_ready")
        gathered, hot_turned, hotT_ready = sems("gathered"), sems("hot_turned"), sems("hotT_ready")
        hot_built = [sem(f"hot_built{k}") for k in range(U // 2)]
        next_index = [sem(f"next_index{k}") for k in range(2)]
        p_spread, summed, relued, scattered = sems("p_spread"), sems("summed"), sems("relued"), sems("scattered")
        edges_done, s_copied_a, s_copied_v = sem("edges_done"), sem("s_copied_a"), sem("s_copied_v")
        sT_done, sT_copied_a, sT_copied_v, conv_done = sem("sT_done"), sem("sT_copied_a"), sem("sT_copied_v"), sem("conv_done")
        xt_done, xt_rounded, xt_split, xt_spread = sem("xt_done"), sem("xt_rounded"), sem("xt_split"), sem("xt_spread")
        al_stored, al_gathered = sem("al_stored"), sem("al_gathered")
        lg_ready, l_exped, result_ready, stored = sem("lg_ready"), sem("l_exped"), sem("result_ready"), sem("stored")

        def nodes(ap):
            return ap.rearrange("(b p) f -> p b f", p=NP)

        def items(turn, k, width=1):
            return bass.ds(U * turn + (k - U), width)

        def row_bank(r):
            return 1024 * (r % H) if r < 2 * H else NT * 512

        def sT_bank(b):
            return 5 + b % 3

        def sum_bank(h):
            return (4, 7)[h % 2]

        def loop_start(first, last):
            return first + 1 + (last - first - 1) % TOGETHER

        def wide_item(turn, k):
            return bass.ds(WIDE * turn + (k - WIDE), 1)

        FULL = 4 * NP

        block = ctx.enter_context(nc.Block())

        @block.sync
        def _(sp):
            edges = (TILES - 1) * ET
            for buf, ap, done in ((dst_i, dst, dst_loaded), (src_i, src, src_loaded)):
                sp.dma_start(buf[:, 0, :], ap[0:128 * ET].rearrange("(c e) -> c e", e=ET)).then_inc(done, 16)
                sp.wait_ge(filled, 2)
                sp.dma_start(buf[0:LOW_TILES - 1, 1, :],
                             ap[128 * ET:edges].rearrange("(c e) -> c e", e=ET)).then_inc(done, 16)
                sp.dma_start(buf[LOW_TILES - 1:LOW_TILES, 1, 0:TAIL],
                             ap[edges:E].rearrange("(c e) -> c e", c=1)).then_inc(done, 16)
            sp.dma_start(g1[:, :, 0:D], w1g.rearrange("(c p) f -> p c f", p=128)).then_inc(g1_loaded, 16)
            for n, ap in enumerate((att_s1, att_d1, att_l, att_r)):
                sp.dma_start(att[:, n, :], ap.rearrange("h f -> (h f)").partition_broadcast(128)).then_inc(att_loaded, 16)
            for n, ap in enumerate((b_r, bias1, gamma, beta, b2)):
                sp.dma_start(rows[:, n, :], ap.partition_broadcast(128)).then_inc(rows_loaded, 16)
            sp.dma_start(b1_row[:, :], b1.partition_broadcast(128)).then_inc(rows_loaded, 16)
            sp.dma_start(g3[:, :, 0:D], w3g.rearrange("(c p) f -> p c f", p=128)).then_inc(g3_loaded, 16)
            sp.dma_start(w1_sb[:, :, :], w1.rearrange("(c p) f -> p c f", p=128)).then_inc(w1_loaded, 16)
            sp.dma_start(w2_sb[:, :, :], w2.rearrange("(c p) f -> p c f", p=128)).then_inc(w2_loaded, 16)
            sp.dma_start(e_src[0:NP, :], src[0:N].rearrange("(b p) -> p b", p=NP), allow_slow_non_contiguous=True).then_inc(e_loaded, 16)
            for b in range(NT):
                sp.wait_ge(q_copied, b + 1)
                sp.dma_start(q_dram[b * NP:(b + 1) * NP, :], q_sb[0:NP, b, :]).then_inc(q_stored, 16)
            sp.dma_start(dst_row_i, dst[0:N].partition_broadcast(128)).then_inc(e_loaded, 16)
            sp.wait_ge(al_copied, NT)
            sp.dma_start(nodes(al_dram), al_sb[0:NP, :, :]).then_inc(al_stored, 16)
            for b in range(NT):
                sp.wait_ge(result_ready, b + 1)
                sp.dma_start(out[b * NP:(b + 1) * NP, :], x0[0:NP, b, :]).then_inc(stored, 16)
            sp.wait_ge(stored, 16 * NT)
            sp.wait_ge(q_stored, 16 * NT)
            sp.wait_ge(al_stored, 16)

        @block.gpsimd
        def _(pool):
            nc.gpsimd.memset(dst_i[:, 1, :], -1).then_inc(filled, 1)
            nc.gpsimd.memset(src_i[:, 1, :], 0).then_inc(filled, 1)
            nc.gpsimd.memset(zeros[:, :], 0.0)
            nc.gpsimd.memset(ones[:, :], 1.0)
            nc.gpsimd.memset(upto[:, :], 1.0)
            nc.gpsimd.memset(ident[:, :], 0.0).then_inc(pool_step, 1)
            pool.wait_ge(pool_step, 1)
            nc.gpsimd.affine_select(out=upto[:, :], in_=upto[:, :], compare_op=ALU.is_ge, fill=0.0, base=0,
                                    pattern=[[1, 128]], channel_multiplier=-1)
            nc.gpsimd.affine_select(out=ident[:, :], in_=ident[:, :], compare_op=ALU.not_equal, fill=1.0, base=0,
                                    pattern=[[-1, 128]], channel_multiplier=1).then_inc(consts, 1)
            iota = nc.gpsimd.iota
            iota(iota1[:, :], [[1, ALL_ITEMS]], base=1, channel_multiplier=0, allow_small_or_imprecise_dtypes=True)
            iota(node_no[:, :], [[NP, NT]], base=0, channel_multiplier=1, allow_small_or_imprecise_dtypes=True)
            iota(tile_no[:, :], [[1, NT]], base=0, channel_multiplier=0, allow_small_or_imprecise_dtypes=True)
            nc.gpsimd.memset(h_ones[:, :, :, :], 1.0)
            nc.gpsimd.memset(t_tile[:, :], 0)
            iota(iota16[:, :], [[1, ALL_ITEMS]], base=0, channel_multiplier=0, allow_small_or_imprecise_dtypes=True)
            iota(iota32[:, :], [[1, 128]], base=0, channel_multiplier=0, allow_small_or_imprecise_dtypes=True).then_inc(filled, 1)
            pool.wait_ge(att_loaded, 64)
            pool.wait_ge(g1_loaded, 16)
            for n in range(4):
                if n == 2:
                    pool.wait_ge(g3_loaded, 16)
                g = g1 if n < 2 else g3
                nc.gpsimd.tensor_tensor(prod[n], g[:, :, 0:D], att[:, n, :].unsqueeze(1).to_broadcast([128, DC, D]),
                                        ALU.mult).then_inc(atts_ready, 1)
            pool.wait_ge(w1_loaded, 16)
            nc.gpsimd.tensor_tensor(w1_dif[:, :, :], w1_sb[:, 0:2, :], w1_sb[:, 2:4, :], ALU.subtract).then_inc(dif_ready, 1)
            pool.wait_ge(x_loaded, 16)
            pool.wait_ge(rows_loaded, 96)
            nc.gpsimd.tensor_tensor(tmp[0:NP, :, :], x0[0:NP, :, :], rows[0:NP, 0, :].unsqueeze(1).to_broadcast([NP, NT, D]),
                                    ALU.add).then_inc(pool_step, 1)
            pool.wait_ge(pool_step, 2)
            pool.wait_ge(lin_read, 2 * NT)
            nc.gpsimd.tensor_tensor(xr[0:NP, :, :], xr[0:NP, :, :], tmp[0:NP, :, :], ALU.add).then_inc(xr_ready, 1)

            pool.wait_ge(agg_done, NT)
            nc.gpsimd.memset(h_ones[:, :, :, F:F + 1], 1.0)
            pool.wait_ge(x_ready, NT)
            nc.gpsimd.tensor_tensor(x1_bias[0:NP, :, :], x1[0:NP, :, :], rows[0:NP, 1, :].unsqueeze(1).to_broadcast([NP, NT, D]),
                                    ALU.add).then_inc(bias_added, 1)
            for i in range(HEADS):
                h = i // NT
                pool.wait_ge(bent, i + 1)
                pool.wait_ge(row_copied, 2 * H + h + 1)
                w = score[i % SLOTS]
                nc.gpsimd.tensor_tensor(w, w, src_row[0:NP, h, :], ALU.add).then_inc(leaky, 1)

            pool.wait_ge(gidx_ready, 1)
            pool.wait_ge(q_stored, 16 * NT)

            def gather(k):
                pool.indirect_dma_start(ring[:, k, :], None, q_dram[:, :],
                                        bass.IndirectOffsetOnAxis(ap=gidx[:, k:k + 1], axis=0)).then_inc(gathered[k], 16)

            def gathers(first, last):
                with pool.Fori(first, last + 1) as before:
                    for k in range(U):
                        pool.wait_ge(q_stored, 16 * NT)
                        if k % HALF == 0:
                            pool.wait_ge(next_index[k // HALF], before)
                        pool.wait_ge(low_ready[k], before)
                        gather(k)

            for k in range(U):
                gather(k)
            gathers(1, FAST_TURNS - 1)
            n = pool.value_load(count[0:1, 0:1], min_val=0, max_val=ALL_ITEMS)
            with pool.If(n > FAST_ITEMS):
                gathers(FAST_TURNS, ALL_TURNS - 1)
            pool.wait_ge(e_loaded, 32)
            nc.gpsimd.tensor_copy(dst_row_f, dst_row_i).then_inc(pool_step, 1)
            pool.wait_ge(pool_step, 3)
            pool.wait_ge(edges_done, 1)
            for b in range(NT):
                nc.gpsimd.tensor_scalar(e_hot[:, b, :], dst_row_f, node_no[:, b:b + 1], None, ALU.is_equal).then_inc(pool_step, 1)
            pool.wait_ge(al_stored, 16)
            for b in range(NT):
                pool.indirect_dma_start(al_g[0:NP, b, :], None, al_dram[:, :],
                                        bass.IndirectOffsetOnAxis(ap=e_src[0:NP, b:b + 1], axis=0)).then_inc(al_gathered, 16)
            pool.wait_ge(al_gathered, 16 * NT)

        @block.scalar
        def _(act):
            act.preload_act_table(ACT.Copy)
            act.wait_ge(filled, 2)
            act.dma_start(x0[0:NP, :, :], nodes(x)).then_inc(x_loaded, 16)
            for n, ap in enumerate((w_l, w_r)):
                act.dma_start(w_lr[:, n, :, :], ap.rearrange("(c p) f -> p c f", p=128)).then_inc(lr_loaded, 16)

            def copy(o, i):
                return nc.scalar.activation(o, i, ACT.Copy)

            def copy_xT(n):
                act.wait_ge(xT_done, 3 * n + 1)
                copy(xT[:, 0, 0:FULL], ps[:, 0, 0:FULL]).then_inc(xT_copied_a, 1)
                act.wait_ge(xT_done, 3 * n + 3)
                copy(xT[:, :, FULL:N], ps[:, 2, 0:2 * NP].rearrange("p (c s) -> p c s", c=DC)).then_inc(xT_copied_a, 1)

            def root(n):
                act.wait_ge(var_ready, n + 1)
                nc.scalar.activation(std[0:NP, :], std[0:NP, :], ACT.Sqrt).then_inc(std_ready, 1)

            copy_xT(0)
            copy(xT[:, 1, 0:FULL], ps[:, 1, 0:FULL]).then_inc(xT_copied_v, 1)
            for n in range(2):
                act.wait_ge(wT_done, n + 1)
                copy(w_lrT[:, :, n * D:(n + 1) * D], ps[:, 3 + n, :].rearrange("p (c f) -> p c f", c=DC)).then_inc(wT_copied, 1)
            act.wait_ge(filled, 3)
            def linear_out(b):
                act.wait_ge(lin_done, b + 1)
                copy(xl[0:NP, b, 0:D], ps[0:NP, min(4 + b, 7), 0:D]).then_inc(lin_read, 1)
                copy(xr[0:NP, b, :], ps[0:NP, min(4 + b, 7), D:2 * D]).then_inc(lin_read, 1)

            for b in range(NT - 2):
                linear_out(b)

            def hots(g, first=False):
                for j in range(GROUPS):
                    if not first:
                        act.wait_ge(hots_used[j], g - 1)
                    for k in range(GROUP * j + DVE_HOTS, GROUP * (j + 1)):
                        last = nc.scalar.activation(apart[:, k, :], iota16[:, 0:128], ACT.Abs, bias=t_dst[:, wide_item(g, k)],
                                                    scale=-1.0)
                    last.then_inc(apart_done[j], 1)
                    if j:
                        near(g, j - 1)
                near(g, GROUPS - 1)

            def near(g, j):
                act.wait_ge(apart_done[j], g)
                group = slice(GROUP * j + DVE_HOTS, GROUP * (j + 1))
                nc.scalar.activation(hot_dst[:, group, :], apart[:, group, :], ACT.Relu, bias=ones[:, 0:1],
                                     scale=-1.0).then_inc(dst_built[j], 1)

            act.wait_ge(list_read, 1)
            n = act.value_load(count[0:1, 0:1], min_val=0, max_val=ALL_ITEMS)
            hots(1, first=True)
            linear_out(NT - 2)
            act.preload_act_table(ACT.Relu)
            with act.Fori(2, FAST_WIDE + 1) as g:
                hots(g)
            with act.If(n > FAST_ITEMS):
                act.wait_ge(rest_read, 2)
                with act.Fori(FAST_WIDE + 1, ALL_WIDE + 1) as g:
                    hots(g)
            act.wait_ge(adj_done, 1)
            copy(adj[0:NP, :, 512:NW], flat[0:NP, 2560:2560 + 128 * NT].rearrange("p (b s) -> p b s", b=NT)).then_inc(adj_copied_a, 1)
            for b in (1, 3):
                copy(adj[0:NP, b, 0:512], ps[0:NP, b, :]).then_inc(adj_copied_a, 1)
            linear_out(NT - 1)
            for m in range(1, 7, 2):
                act.wait_ge(adjT_done, m + 1)
                copy(adjT[0:NP, m * FULL:(m + 1) * FULL], ps[0:NP, m, 0:FULL]).then_inc(adjT_copied_a, 1)
            root(0)
            act.preload_act_table(ACT.Exp)

            copy_xT(1)
            for b in range(NT):
                act.wait_ge(h_done, b + 1)
                copy(h_sb[0:NP, b, D:WX], ps[0:NP, 3 + b, D:WX]).then_inc(h_copied, 1)
                copy(h_ones[0:NP, b, :, 0:F], ps[0:NP, 3 + b, 0:D].rearrange("p (h f) -> p h f", h=H)).then_inc(h_copied, 1)

            def copy_row(r):
                act.wait_ge(row_done, r + 1)
                row = dst_row[0:NP, r - H, :] if H <= r < 2 * H else src_row[0:NP, r % H, :]
                at = row_bank(r)
                copy(row.rearrange("p (b s) -> p b s", b=NT),
                     flat[0:NP, at:at + NT * 128].rearrange("p (b s) -> p b s", b=NT)[:, :, 0:NP]).then_inc(row_copied, 1)

            for r in range(2 * H):
                copy_row(r)

            def bend(i):
                h, s = i // NT, i % NT
                if i >= SLOTS:
                    act.wait_ge(mixed, i - SLOTS + 1)
                nc.scalar.activation(score[i % SLOTS], dst_row[0:NP, h, :], ACT.Relu, bias=src4[0:NP, s, h:h + 1],
                                     scale=4.0).then_inc(bent, 1)

            def exp(i):
                h, s = i // NT, i % NT
                act.wait_ge(leaky, i + 1)
                nc.scalar.activation(score[i % SLOTS], score[i % SLOTS], ACT.Exp, bias=src02[0:NP, s, h:h + 1],
                                     scale=0.2).then_inc(exped, 1)

            act.wait_ge(row_copied, 2 * H)
            act.wait_ge(src_scaled, 2)

            def copy_sums(h):
                act.wait_ge(mixed, NT * (h + 1))
                if h >= 2:
                    act.wait_ge(sum_turned, h - 1)
                copy(xT[0:F + 1, h % 2, :], flat[0:F + 1, 1024 * (h % 2):1024 * (h % 2) + N]).then_inc(sumT_copied, 1)

            new_row = {0: 0, 2: 1, 10: 2, 15: 3}
            for i in range(HEADS + 2):
                if i < HEADS:
                    bend(i)
                    if i in new_row:
                        copy_row(2 * H + new_row[i])
                if i >= 2:
                    exp(i - 2)
                if i >= NT + 3 and i % NT == 3:
                    copy_sums(i // NT - 1)
            copy_sums(H - 1)
            root(1)
            root(2)

            copy_xT(2)
            for b in range(NT):
                act.wait_ge(q_done, b + 1)
                copy(q_sb[0:NP, b, :], ps[0:NP, 3 + b, :]).then_inc(q_copied, 1)
            for b in range(NT):
                act.wait_ge(p_added, b + 1)
                copy(parts[0:NP, 0, b, :], p_sb[0:NP, b, :]).then_inc(p_high, 1)

            def turn_hot(g, k):
                k, g = k % U, g + k // U
                act.wait_ge(hot_turned[k], g)
                before = (k - 2) % U
                if not (isinstance(g, int) and (g - (k < 2)) < 1):
                    act.wait_ge(p_spread[before], g - (1 if k < 2 else 0))
                copy(hotT[0:NP, k % 2, :], ps[0:NP, 7, 0:128]).then_inc(hotT_ready[k], 1)

            def relu(g, k):
                act.wait_ge(summed[k], g)
                if not (isinstance(g, int) and g - (k < 3) < 1):
                    act.wait_ge(scattered[(k - 3) % U], g - (1 if k < 3 else 0))
                nc.scalar.activation(whole[:, k % 3, :], ring[:, k, SPLIT:HID], ACT.Relu).then_inc(relued[k], 1)

            def relu_high(g, k):
                nc.scalar.activation(high[:, k % 3, :], ring[:, k, 0:SPLIT], ACT.Relu).then_inc(high_ready[k], 1)

            def act_turn(g, last=False):
                for k in range(U):
                    relu(g, k)
                    if not (last and k + 2 >= U):
                        turn_hot(g, k + 2)
                    relu_high(g, k)

            def act_turns(first, last):
                act.preload_act_table(ACT.Relu)
                turn_hot(first, 0)
                turn_hot(first, 1)
                act_turn(first)
                start = loop_start(first, last)
                for g in range(first + 1, start):
                    act_turn(g)
                with act.Fori(start, last, TOGETHER) as g:
                    for j in range(TOGETHER):
                        act_turn(g + j)
                act_turn(last, last=True)

            act_turns(1, FAST_TURNS)
            n = act.value_load(count[0:1, 0:1], min_val=0, max_val=ALL_ITEMS)
            with act.If(n > FAST_ITEMS):
                act_turns(FAST_TURNS + 1, ALL_TURNS)
            act.wait_ge(edges_done, 1)
            for b in (1, 3):
                copy(q_sb[0:NP, b, :], ps[0:NP, b, :]).then_inc(s_copied_a, 1)
                act.wait_ge(sT_done, b)
                copy(sT[:, b - 1, :], ps[:, sT_bank(b - 1), 0:4 * NP]).then_inc(sT_copied_a, 1)
            act.wait_ge(sT_done, NT)
            copy(sT[:, NT - 1, :], ps[:, sT_bank(NT - 1), 0:4 * NP]).then_inc(sT_copied_a, 1)
            root(3)

            copy_xT(3)
            for b in range(NT):
                act.wait_ge(xt_done, b + 1)
                copy(al_sb[0:NP, b, :], ps[0:NP, 3 + b, D:D + H]).then_inc(al_copied, 1)
                copy(xt_high[0:NP, b, :], ps[0:NP, 3 + b, 0:WX]).then_inc(xt_rounded, 1)
            act.wait_ge(lg_ready, 1)
            nc.scalar.activation(lg[0:NP, :, :], lg[0:NP, :, :], ACT.Exp).then_inc(l_exped, 1)
            root(4)

        @block.vector
        def _(dve):
            steps = [0]

            def step(ins):
                steps[0] += 1
                ins.then_inc(dve_step, 1)

            def settle():
                dve.wait_ge(dve_step, steps[0])

            V = nc.vector
            dve.wait_ge(dst_loaded, 48)
            step(V.tensor_copy(dst_f[:, :], dst_i[:, :, :].rearrange("p k e -> p (k e)")))
            settle()
            step(V.memset(from_tile[:, 2 * NT:], 0.0))
            dve.wait_ge(consts, 1)
            settle()
            for q in range(2 * NT):
                b, k = q // 2, q % 2
                step(V.tensor_scalar(compared[:, q, :], dst_f[:, k * ET:(k + 1) * ET], float(NP * b), None, ALU.is_ge, ALU.add,
                                     accum_out=from_tile[:, q:q + 1]))
            settle()
            step(V.tensor_tensor(in_some[:, :], from_tile[:, 0:2 * NT], from_tile[:, 2:2 * NT + 2], ALU.subtract))
            settle()
            step(V.tensor_scalar(has[:, :], in_some[:, :], 0.5, None, ALU.is_ge))
            dve.wait_ge(consts, 1)
            settle()
            step(V.tensor_tensor_scan(has_sum[:, :], ones[:, 0:2 * NT], has[:, :], 0.0, ALU.mult, ALU.add))
            settle()
            V.tensor_tensor(has_before[:, :], has_sum[:, :], has[:, :], ALU.subtract).then_inc(has_ready, 1)
            for b in range(NT):
                V.tensor_scalar(dst_loc[:, b, :], dst_f[:, :], float(1 - NP * b), None, ALU.add)
            dve.wait_ge(src_loaded, 48)
            V.tensor_copy(src16[:, :, :], src_i[:, :, :]).then_inc(casts_done, 1)
            dve.wait_ge(pos_done, 1)
            dve.wait_ge(filled, 3)
            step(V.tensor_tensor(place[:, :], ps[:, 7, 0:2 * NT], has[:, :], ALU.mult))
            step(V.tensor_copy(count[0:1, :], ps[0:1, 7, 2 * NT:2 * NT + 1]))
            settle()
            for q in range(2 * NT):
                V.tensor_scalar(pick[:, q, 0:FAST_ITEMS], iota1[:, 0:FAST_ITEMS], place[:, q:q + 1], None,
                                ALU.is_equal).then_inc(picked, 1)
            V.tensor_copy(ident_r[:, :], ident[:, :])
            for n_att in range(4):
                g, at = (g1, D + H * n_att) if n_att < 2 else (g3, D + H * (n_att - 2))
                dve.wait_ge(atts_ready, n_att + 1)
                V.tensor_reduce(g[:, :, at:at + H], prod[n_att].rearrange("p c (h f) -> p c h f", h=H), AX.X,
                                ALU.add).then_inc(folded, 1)

            def read_list(lo, w, done):
                V.tensor_copy(t_src[:, lo:lo + w], ps[:, 0, 0:w])
                V.tensor_scalar(t_dst[:, lo:lo + w], ps[:, 1, 0:w], 1.0, None, ALU.subtract)
                V.tensor_copy(t_tile[0:1, PAD + lo:PAD + lo + w], ps[0:1, 2, 0:w]).then_inc(done, 1)

            dve.wait_ge(listed, 1)
            read_list(0, FAST_ITEMS, list_read)
            dve.wait_ge(list_read, 1)
            n = dve.value_load(count[0:1, 0:1], min_val=0, max_val=ALL_ITEMS)
            with dve.If(n > FAST_ITEMS):
                for r in range(2):
                    lo = FAST_ITEMS + r * REST_CHUNK
                    for q in range(2 * NT):
                        V.tensor_scalar(pick[:, q, :], iota1[:, lo:lo + REST_CHUNK], place[:, q:q + 1], None,
                                        ALU.is_equal).then_inc(rest_picked, 1)
                    dve.wait_ge(rest_listed, r + 1)
                    read_list(lo, REST_CHUNK, rest_read)
                    dve.wait_ge(rest_read, r + 1)

            def copy_xT(n):
                dve.wait_ge(xT_done, 3 * n + 2)
                V.tensor_copy(xT[:, 1, 0:FULL], ps[:, 1, 0:FULL]).then_inc(xT_copied_v, 1)


            def hots(g, first=False):
                for j in range(GROUPS):
                    if not first:
                        dve.wait_ge(hots_used[j], g - 1)
                    for k in range(GROUP * j, GROUP * (j + 1)):
                        if k < GROUP * j + DVE_HOTS:
                            V.tensor_scalar(hot_dst[:, k, :], iota16[:, 0:128], t_dst[:, wide_item(g, k)], None, ALU.is_equal)
                        last = V.tensor_scalar(hot_src[:, k, :], iota16[:, 0:NW], t_src[:, wide_item(g, k)], None, ALU.is_equal)
                    last.then_inc(src_built[j], 1)

            hots(1, first=True)
            with dve.Fori(2, FAST_WIDE + 1) as g:
                hots(g)
            with dve.If(n > FAST_ITEMS):
                with dve.Fori(FAST_WIDE + 1, ALL_WIDE + 1) as g:
                    hots(g)
            dve.wait_ge(adj_done, 1)
            for b in (0, 2, 4):
                V.tensor_copy(adj[0:NP, b, 0:512], ps[0:NP, b, :]).then_inc(adj_copied_v, 1)
            for m in range(0, 7, 2):
                w = min(FULL, NT * NT * NP - m * FULL)
                dve.wait_ge(adjT_done, m + 1)
                V.tensor_copy(adjT[0:NP, m * FULL:m * FULL + w], ps[0:NP, m, 0:w]).then_inc(adjT_copied_v, 1)
            dve.wait_ge(adjT_done, 7)
            for b in range(NT):
                blk = adj[0:NP, b, b * NP:(b + 1) * NP]
                step(V.tensor_tensor(blk, blk, ident[0:NP, 0:NP], ALU.add))
            dve.wait_ge(adj_copied_a, 3)
            settle()
            step(V.tensor_scalar(mask[0:NP, :, :], adj[0:NP, :, :], 0.0, NEG, ALU.is_equal, ALU.mult))

            norms = [0]

            def layer_norm(o, i, done=dve_step, begun=False):
                if not begun:
                    for b in range(NT):
                        step(V.bn_stats(stats[0:NP, b, :], i[0:NP, b, :]))
                settle()
                for b in range(NT):
                    step(V.bn_aggr(mv[0:NP, b, :], stats[0:NP, b, :]))
                settle()
                V.tensor_scalar(std[0:NP, :], mv[0:NP, :, 1], EPS, None, ALU.add).then_inc(var_ready, 1)
                norms[0] += 1
                dve.wait_ge(std_ready, norms[0])
                step(V.reciprocal(rstd[0:NP, :], std[0:NP, :]))
                settle()
                for b in range(NT):
                    V.tensor_scalar(o[0:NP, b, :], i[0:NP, b, :], mv[0:NP, b, 0:1], rstd[0:NP, b:b + 1],
                                    ALU.subtract, ALU.mult).then_inc(done, 1)
                if done is dve_step:
                    steps[0] += NT

            def row(n):
                return rows[0:NP, n, :].unsqueeze(1).to_broadcast([NP, NT, D])

            dve.wait_ge(xr_ready, 1)
            for b in range(NT):
                dve.wait_ge(agg_done, b + 1)
                step(V.tensor_scalar(rdeg[0:NP, b:b + 1], ps[0:NP, b, D:D + 1], 1.0, None, ALU.max))
                V.tensor_copy(deg[0:NP, b:b + 1], ps[0:NP, b, D:D + 1])
                settle()
                step(V.reciprocal(rdeg[0:NP, b:b + 1], rdeg[0:NP, b:b + 1]))
                settle()
                step(V.scalar_tensor_tensor(tmp[0:NP, b, :], ps[0:NP, b, 0:D], rdeg[0:NP, b:b + 1], xr[0:NP, b, :],
                                            ALU.mult, ALU.add))
                settle()
                step(V.bn_stats(stats[0:NP, b, :], tmp[0:NP, b, :]))
            layer_norm(x1, tmp, x_ready, begun=True)
            step(V.tensor_scalar(rdeg2[0:NP, :], deg[0:NP, :], 1e-8, None, ALU.add))
            settle()
            step(V.reciprocal(rdeg2[0:NP, :], rdeg2[0:NP, :]))

            copy_xT(1)

            for b in range(NT):
                at = (b * NT + b) * NP
                step(V.tensor_tensor(adjT[0:NP, at:at + NP], adjT[0:NP, at:at + NP], ident[0:NP, 0:NP], ALU.add))
            dve.wait_ge(h_copied, 2 * NT)
            V.tensor_scalar(src4[0:NP, :, :], h_sb[0:NP, :, D:D + H], 4.0, None, ALU.mult).then_inc(src_scaled, 1)
            V.tensor_scalar(src02[0:NP, :, :], h_sb[0:NP, :, D:D + H], 0.2, None, ALU.mult).then_inc(src_scaled, 1)
            last_steps = []

            def best(h, b):
                if b == 0:
                    dve.wait_ge(row_copied, h + 1)
                if len(last_steps) >= len(spare):
                    dve.wait_ge(dve_step, last_steps[-len(spare)])
                step(V.tensor_tensor_reduce(out=spare[len(last_steps) % len(spare)], in0=mask[0:NP, b, 0:N],
                                            in1=src_row[0:NP, h, :], scale=1.0, scalar=-3.0e38, op0=ALU.add,
                                            op1=ALU.max, accum_out=top[0:NP, b, h:h + 1]))
                last_steps.append(steps[0])

            def down_of(h):
                a_dst = h_sb[0:NP, :, D + H + h]
                settle()
                step(V.tensor_tensor(top[0:NP, :, h], top[0:NP, :, h], a_dst, ALU.add))
                settle()
                step(V.scalar_tensor_tensor(top[0:NP, :, h], top[0:NP, :, h], 0.2, top[0:NP, :, h], ALU.mult, ALU.max))
                settle()
                V.scalar_tensor_tensor(down[0:NP, :, h], top[0:NP, :, h], -5.0, a_dst, ALU.mult, ALU.add).then_inc(down_ready, 1)

            def weigh(i):
                s = i % NT
                dve.wait_ge(exped, i + 1)
                V.scalar_tensor_tensor(score[i % SLOTS], score[i % SLOTS], 1.0, adjT[0:NP, s * N:(s + 1) * N],
                                       ALU.min, ALU.mult).then_inc(weighted, 1)

            def take_sums(h):
                dve.wait_ge(sum_turned, h + 1)
                sums = ps[0:NP, sum_bank(h), 0:NT * (F + 1)].rearrange("p (b f) -> p b f", b=NT)
                step(V.tensor_scalar(rden[0:NP, :, h], sums[:, :, F], 1e-16, None, ALU.add))
                settle()
                step(V.reciprocal(rden[0:NP, :, h], rden[0:NP, :, h]))
                settle()
                head = slice(h * F, (h + 1) * F)
                V.tensor_tensor(tmp[0:NP, :, head], sums[:, :, 0:F],
                                rden[0:NP, :, h].unsqueeze(2).to_broadcast([NP, NT, F]), ALU.mult).then_inc(sum_read, 1)
                dve.wait_ge(sum_read, h + 1)
                step(V.tensor_tensor(tmp[0:NP, :, head], tmp[0:NP, :, head], x1_bias[0:NP, :, head], ALU.add))

            dve.wait_ge(bias_added, 1)
            settle()
            for h in range(AHEAD):
                for b in range(NT):
                    best(h, b)
                down_of(h)
            for h in range(H):
                for s in range(NT):
                    weigh(NT * h + s)
                    if h + AHEAD < H:
                        best(h + AHEAD, s)
                    if h >= 1 and s == NT - 1:
                        take_sums(h - 1)
                if h + AHEAD < H:
                    down_of(h + AHEAD)
            take_sums(H - 1)
            settle()
            layer_norm(tmp, tmp)
            settle()
            step(V.tensor_tensor(tmp[0:NP, :, :], tmp[0:NP, :, :], row(2), ALU.mult))
            settle()
            step(V.tensor_tensor(tmp[0:NP, :, :], tmp[0:NP, :, :], row(3), ALU.add))
            settle()
            step(V.scalar_tensor_tensor(tmp[0:NP, :, :], tmp[0:NP, :, :], 0.0, x1[0:NP, :, :], ALU.max, ALU.add))
            settle()
            layer_norm(x2, tmp, x_ready)

            V.tensor_copy(gidx[:, :], t_src[:, 0:U]).then_inc(gidx_ready, 1)
            copy_xT(2)
            dve.wait_ge(x_ready, 2 * NT)
            step(V.tensor_tensor(share[0:NP, :], deg[0:NP, :], rdeg2[0:NP, :], ALU.mult))
            settle()
            for b in range(NT):
                step(V.scalar_tensor_tensor(x2_b2[0:NP, b, :], rows[0:NP, 4, :], share[0:NP, b:b + 1], x2[0:NP, b, :],
                                            ALU.mult, ALU.add))
            for b in range(NT + 1):
                if b < NT:
                    dve.wait_ge(p_done, b + 1)
                    V.tensor_tensor(p_sb[0:NP, b, :], ps[0:NP, (b + 1) % 2, :], b1_row[0:NP, :], ALU.add).then_inc(p_added, 1)
                b -= 1
                if b < 0:
                    continue
                dve.wait_ge(p_high, b + 1)
                V.tensor_tensor(parts[0:NP, 1, b, :], p_sb[0:NP, b, :], parts[0:NP, 0, b, :].bitcast(f32), ALU.subtract).then_inc(parts_ready, 1)

            def build_hots(g, k):
                column = items(g, k, 2)
                k, g = k % U, g + k // U
                if not (isinstance(g, int) and g < 2):
                    for slot in (k, k + 1):
                        dve.wait_ge(scattered[slot], g - 1)
                V.tensor_tensor(hot[:, k:k + 2, :], iota32[:, :].unsqueeze(1).to_broadcast([128, 2, 128]),
                                t_dst[:, column].unsqueeze(2).to_broadcast([128, 2, 128]), ALU.is_equal).then_inc(hot_built[k // 2], 1)

            def add_p(g, k, index=True):
                dve.wait_ge(gathered[k], 16 * g)
                if index and k % HALF == HALF - 1:
                    lo = k + 1 - HALF
                    V.tensor_scalar(gidx[:, lo:k + 1], t_src[:, items(g, lo + U, HALF)], 0.0, None,
                                    ALU.add).then_inc(next_index[k // HALF], 1)
                dve.wait_ge(p_spread[k], g)
                V.tensor_tensor(ring[:, k, :], ring[:, k, :], ps[:, 5 + k % 2, :], ALU.add).then_inc(summed[k], 1)

            def rest(g, k):
                k, g = k % U, g + k // U
                dve.wait_ge(high_ready[k], g)
                V.scalar_tensor_tensor(low[:, k % 3, :], ring[:, k, 0:SPLIT], 0.0, high[:, k % 3, :].bitcast(f32),
                                       ALU.max, ALU.subtract).then_inc(low_ready[k], 1)

            def dve_turn(g, first=False, last=False, index=True):
                for k in range(U):
                    if k % 2 == 0 and not (last and k + 2 >= U):
                        build_hots(g, k + 2)
                    add_p(g, k, index)
                    if not (first and k < 1):
                        rest(g, k - 1)
                if last:
                    rest(g, U - 1)

            def dve_turns(first, last, index_last):
                build_hots(first, 0)
                dve_turn(first, first=True)
                start = loop_start(first, last)
                for g in range(first + 1, start):
                    dve_turn(g)
                with dve.Fori(start, last, TOGETHER) as g:
                    for j in range(TOGETHER):
                        dve_turn(g + j)
                dve_turn(last, last=True, index=index_last)

            dve_turns(1, FAST_TURNS, False)
            n = dve.value_load(count[0:1, 0:1], min_val=0, max_val=ALL_ITEMS)
            with dve.If(n > FAST_ITEMS):
                for half in range(2):
                    lo = half * HALF
                    V.tensor_copy(gidx[:, lo:lo + HALF], t_src[:, FAST_ITEMS + lo:FAST_ITEMS + lo + HALF]).then_inc(next_index[half], 1)
                dve_turns(FAST_TURNS + 1, ALL_TURNS, False)
            dve.wait_ge(edges_done, 1)
            V.tensor_copy(q_sb[0:NP, 0, :], ps[0:NP, 0, :]).then_inc(s_copied_v, 1)
            for b in (2, 4):
                V.tensor_copy(q_sb[0:NP, b, :], ps[0:NP, b, :]).then_inc(s_copied_v, 1)
                dve.wait_ge(sT_done, b)
                V.tensor_copy(sT[:, b - 1, :], ps[:, sT_bank(b - 1), 0:4 * NP]).then_inc(sT_copied_v, 1)
            for b in range(NT):
                dve.wait_ge(conv_done, b + 1)
                step(V.scalar_tensor_tensor(tmp[0:NP, b, :], ps[0:NP, b, 0:D], rdeg2[0:NP, b:b + 1], x2_b2[0:NP, b, :],
                                            ALU.mult, ALU.add))
                settle()
                step(V.bn_stats(stats[0:NP, b, :], tmp[0:NP, b, :]))
            layer_norm(x1, tmp, x_ready, begun=True)

            copy_xT(3)
            for b in range(NT):
                dve.wait_ge(xt_rounded, b + 1)
                V.tensor_tensor(xt_low[0:NP, b, :], ps[0:NP, 3 + b, 0:WX], xt_high[0:NP, b, :].bitcast(f32),
                                ALU.subtract).then_inc(xt_split, 1)
            dve.wait_ge(al_gathered, 16 * NT)
            dve.wait_ge(xt_spread, NT)
            al = lg[0:NP, :, :]
            step(V.tensor_tensor(al, al_g[0:NP, :, :], ps[0:NP, 1:1 + NT, D + H:D + 2 * H], ALU.add))
            settle()
            step(V.scalar_tensor_tensor(al, al, 0.01, al, ALU.mult, ALU.max))
            settle()
            step(V.tensor_reduce(lmax[0:NP, :], al, AX.X, ALU.max))
            settle()
            V.tensor_tensor(al, al, lmax[0:NP, :].unsqueeze(2).to_broadcast([NP, NT, H]), ALU.subtract).then_inc(lg_ready, 1)
            dve.wait_ge(l_exped, 1)
            step(V.tensor_reduce(lsum[0:NP, :], al, AX.X, ALU.add))
            settle()
            step(V.reciprocal(lsum[0:NP, :], lsum[0:NP, :]))
            settle()
            step(V.tensor_tensor(al, al, lsum[0:NP, :].unsqueeze(2).to_broadcast([NP, NT, H]), ALU.mult))
            settle()
            by_head = tmp[0:NP, :, :].rearrange("p b (h f) -> p b h f", h=H)
            step(V.tensor_tensor(by_head, ps[0:NP, 1:1 + NT, 0:D].rearrange("p b (h f) -> p b h f", h=H),
                                 lg[0:NP, :, :].unsqueeze(3).to_broadcast([NP, NT, H, F]), ALU.mult))
            settle()
            step(V.tensor_reduce(x2[0:NP, :, 0:F], tmp[0:NP, :, :].rearrange("p b (h f) -> p b f h", h=H), AX.X, ALU.add))
            settle()
            for b in range(NT):
                step(V.tensor_tensor(tmp[0:NP, b, :].rearrange("p (h f) -> p h f", h=H),
                                     x1[0:NP, b, :].rearrange("p (h f) -> p h f", h=H),
                                     x2[0:NP, b, 0:F].unsqueeze(1).to_broadcast([NP, H, F]), ALU.add))
            settle()
            layer_norm(x0, tmp, result_ready)

        @block.tensor
        def _(pe):
            def mm(o, a, b, start, stop):
                return nc.tensor.matmul(o, a, b, start=start, stop=stop, skip_group_check=True)

            def keep_busy(products, bank):
                for k in range(products):
                    mm(ps[:, bank, :], zeros[:, 0:128], zeros[:, :], True, True)

            def turn(n, xs):
                for b in range(NT - 1):
                    if n:
                        pe.wait_ge(x_ready, NT * (n - 1) + b + 1)
                    for c in range(DC):
                        last = nc.tensor.transpose(ps[:, c, b * NP:(b + 1) * NP], xs[0:NP, b, c * 128:(c + 1) * 128],
                                                   ident[0:NP, 0:NP])
                        if b == NT - 2:
                            last.then_inc(xT_done, 1)
                if n:
                    pe.wait_ge(x_ready, NT * n)
                for c in range(DC):
                    last = nc.tensor.transpose(ps[:, 2, c * NP:(c + 1) * NP], xs[0:NP, NT - 1, c * 128:(c + 1) * 128],
                                               ident[0:NP, 0:NP])
                last.then_inc(xT_done, 1)

            def turned(n):
                pe.wait_ge(xT_copied_a, 2 * n + 2)
                pe.wait_ge(xT_copied_v, n + 1)

            def make_list(w, sem_in, base, done):
                pe.wait_ge(sem_in, base)
                for q in range(2 * NT):
                    b, kt = q // 2, q % 2
                    one = pick[:, q, 0:w]
                    mm(ps[:, 0, 0:w], src16[:, kt, :], one, q == 0, q == 2 * NT - 1)
                    mm(ps[:, 1, 0:w], dst_loc[:, b, kt * ET:(kt + 1) * ET], one, q == 0, q == 2 * NT - 1)
                    last = mm(ps[0:1, 2, 0:w], tile_no[:, b:b + 1], one, q == 0, q == 2 * NT - 1)
                last.then_inc(done, 1)

            def linear(b):
                for c in range(DC):
                    last = mm(ps[0:NP, min(4 + b, 7), :], xT[:, c, b * NP:(b + 1) * NP], w_lrT[:, c, :], c == 0, c == DC - 1)
                last.then_inc(lin_done, 1)

            pe.wait_ge(consts, 1)
            keep_busy(10, 7)
            pe.wait_ge(x_loaded, 16)
            turn(0, x0)
            pe.wait_ge(lr_loaded, 32)
            for n in range(2):
                for c in range(DC):
                    for o in range(DC):
                        at = c * D + o * 128
                        last = nc.tensor.transpose(ps[:, 3 + n, at:at + 128], w_lr[:, n, o, c * 128:(c + 1) * 128], ident[:, :])
                last.then_inc(wT_done, 1)
            pe.wait_ge(has_ready, 1)
            mm(ps[:, 7, 0:2 * NT], upto[:, :], has[:, :], True, False)
            mm(ps[:, 7, 0:2 * NT], ones[:, :], has_before[:, :], False, True)
            mm(ps[:, 7, 2 * NT:2 * NT + 1], ones[:, :], has_sum[:, 2 * NT - 1:2 * NT], True, True).then_inc(pos_done, 1)
            turned(0)
            pe.wait_ge(wT_copied, 2)
            linear(0)
            pe.wait_ge(casts_done, 1)
            make_list(FAST_ITEMS, picked, 2 * NT, listed)
            linear(1)
            linear(2)
            linear(3)
            pe.wait_ge(list_read, 1)
            n_items = pe.value_load(count[0:1, 0:1], min_val=0, max_val=ALL_ITEMS)
            with pe.If(n_items > FAST_ITEMS):
                for r in range(2):
                    make_list(REST_CHUNK, rest_picked, 2 * NT * (r + 1), rest_listed)
                    pe.wait_ge(rest_read, r + 1)
            pe.wait_ge(lin_read, 2 * NT - 4)
            for k in range(7):
                mm(ps[:, k, :], zeros[:, 0:128], zeros[:, :], True, True)

            def tiles_at(at, width):
                _, values = nc.values_load_multi_w_load_instructions(
                    t_tile[0:1, bass.ds(at, width)], engines=[mybir.EngineType.PE], min_val=0, max_val=NT - 1,
                    skip_runtime_bounds_check_because="a node tile's number: one of 0 to NT - 1, or 0 where no item is")
                return values

            def adjacency(g):
                tiles = tiles_at(WIDE * g + (PAD - WIDE), WIDE)
                for j in range(GROUPS):
                    pe.wait_ge(src_built[j], g)
                    pe.wait_ge(dst_built[j], g)
                    for k in range(GROUP * j, GROUP * (j + 1)):
                        mm(ps[:, bass.ds(tiles[k], 1), :], hot_dst[:, k, :], hot_src[:, k, 0:512], False, True)
                        last = mm(flat[:, bass.ds(tiles[k] * 128 + 2560, 128)], hot_dst[:, k, :], hot_src[:, k, 512:NW],
                                  False, True)
                    last.then_inc(hots_used[j], 1)

            with pe.Fori(1, FAST_WIDE + 1) as g:
                adjacency(g)
            with pe.If(n_items > FAST_ITEMS):
                with pe.Fori(FAST_WIDE + 1, ALL_WIDE + 1) as g:
                    adjacency(g)
            mm(ps[:, 6, :], zeros[:, 0:128], zeros[:, :], False, True).then_inc(adj_done, 1)
            pe.wait_ge(lin_read, 2 * NT - 2)
            linear(NT - 1)
            pe.wait_ge(adj_copied_v, 3)
            pe.wait_ge(adj_copied_a, 3)
            for n in range(NT * NT):
                s, d = n // NT, n % NT
                last = nc.tensor.transpose(ps[0:NP, n // 4, (n % 4) * NP:(n % 4 + 1) * NP], adj[0:NP, d, s * NP:(s + 1) * NP],
                                           ident[0:NP, 0:NP])
                if n % 4 == 3 or n == NT * NT - 1:
                    last.then_inc(adjT_done, 1)
            pe.wait_ge(lin_read, 2 * NT)
            pe.wait_ge(adjT_copied_v, 4)
            pe.wait_ge(adjT_copied_a, 3)
            for b in range(NT):
                for s in range(NT):
                    at = (s * NT + b) * NP
                    last = mm(ps[0:NP, b, 0:D + 1], adjT[0:NP, at:at + NP], xl[0:NP, s, :], s == 0, s == NT - 1)
                last.then_inc(agg_done, 1)
            keep_busy(14, 7)
            turn(1, x1)
            pe.wait_ge(folded, 4)
            turned(1)

            for b in range(NT):
                for c in range(DC):
                    last = mm(ps[0:NP, 3 + b, 0:WX], xT[:, c, b * NP:(b + 1) * NP], g1[:, c, :], c == 0, c == DC - 1)
                last.then_inc(h_done, 1)


            def spread_row(r, columns):
                for b in range(NT):
                    at = row_bank(r) + 128 * b
                    last = mm(flat[0:NP, at:at + NP], columns[0:NP, b, r % H:r % H + 1].to_broadcast([NP, NP]),
                              ident[0:NP, 0:NP], True, True)
                last.then_inc(row_done, 1)

            pe.wait_ge(h_copied, 2 * NT)
            for r in range(H):
                spread_row(r, h_sb[:, :, D:D + H])
            for r in range(H, 2 * H):
                pe.wait_ge(row_copied, r - H + 1)
                spread_row(r, h_sb[:, :, D + H:D + 2 * H])

            def spread_down(h):
                pe.wait_ge(down_ready, h + 1)
                pe.wait_ge(row_copied, 2 * H + h)
                spread_row(2 * H + h, down)

            def turn_sums(h):
                pe.wait_ge(sumT_copied, h + 1)
                if h >= 2:
                    pe.wait_ge(sum_read, h - 1)
                for b in range(NT):
                    last = nc.tensor.transpose(ps[0:NP, sum_bank(h), b * (F + 1):(b + 1) * (F + 1)],
                                               xT[0:F + 1, h % 2, b * NP:(b + 1) * NP], ident[0:F + 1, 0:F + 1])
                last.then_inc(sum_turned, 1)

            spread_down(0)
            for i in range(HEADS):
                h, s = i // NT, i % NT
                if s == 0 and h + 1 < H:
                    spread_down(h + 1)
                if s == 0 and h >= 2:
                    pe.wait_ge(sumT_copied, h - 1)
                if s == 3 and h >= 1:
                    turn_sums(h - 1)
                pe.wait_ge(weighted, i + 1)
                for lo, hi in ((0, 512), (512, N)):
                    at = 1024 * (h % 2)
                    last = mm(flat[0:F + 1, at + lo:at + hi], h_ones[0:NP, s, h, :], score[i % SLOTS][:, lo:hi],
                              s == 0, s == NT - 1)
                last.then_inc(mixed, 1)
            turn_sums(H - 1)
            pe.wait_ge(var_ready, 2)
            keep_busy(24, 6)
            turn(2, x2)
            turned(2)
            pe.wait_ge(w1_loaded, 16)
            for b in range(NT):
                for c in range(DC):
                    last = mm(ps[0:NP, 3 + b, :], xT[:, c, b * NP:(b + 1) * NP], w1_sb[:, DC + c, :], c == 0, c == DC - 1)
                last.then_inc(q_done, 1)
            pe.wait_ge(dif_ready, 1)
            for b in range(NT):
                if b >= 2:
                    pe.wait_ge(p_added, b - 1)
                for c in range(DC):
                    last = mm(ps[0:NP, (b + 1) % 2, :], xT[:, c, b * NP:(b + 1) * NP], w1_dif[:, c, :], c == 0, c == DC - 1)
                last.then_inc(p_done, 1)
            pe.wait_ge(p_added, NT)
            pe.wait_ge(q_copied, NT)
            for k in range(NT):
                mm(ps[:, k, :], zeros[:, 0:128], zeros[:, :], True, True)
            pe.wait_ge(parts_ready, NT)

            def turn_hot(g, k):
                k, g = k % U, g + k // U
                if k % 2 == 0:
                    pe.wait_ge(hot_built[k // 2], g)
                if not (isinstance(g, int) and g - (k < 1) < 1):
                    pe.wait_ge(hotT_ready[(k - 1) % U], g - (1 if k < 1 else 0))
                nc.tensor.transpose(ps[:, 7, 0:128].bitcast(f32r), hot[:, k, :], ident_r[:, :]).then_inc(hot_turned[k], 1)

            def spread_p(g, k, tile):
                k, g = k % U, g + k // U
                pe.wait_ge(hotT_ready[k], g)
                if not (isinstance(g, int) and g - (k < 2) < 1):
                    pe.wait_ge(summed[(k - 2) % U], g - (1 if k < 2 else 0))
                for r in range(2):
                    last = mm(ps[:, 5 + k % 2, :], hotT[0:NP, k % 2, :], parts[0:NP, r, bass.ds(tile, 1), :], r == 0, r == 1)
                last.then_inc(p_spread[k], 1)

            def scatter(g, k, tile):
                k, g = k % U, g + k // U
                pe.wait_ge(relued[k], g)
                mm(flat[:, bass.ds(tile * 512 + SPLIT, HID - SPLIT)], hot[:, k, :].bitcast(f32), whole[:, k % 3, :], False, True)
                pe.wait_ge(low_ready[k], g)
                mm(flat[:, bass.ds(tile * 512, SPLIT)], hot[:, k, :], high[:, k % 3, :], False, True)
                mm(flat[:, bass.ds(tile * 512, SPLIT)], hot[:, k, :], low[:, k % 3, :], False, True).then_inc(scattered[k], 1)

            def pe_turn(g, first=False, last=False, tiles=None):
                tiles = tiles or tiles_at(U * g - U, PAD + U + 1)
                if first:
                    spread_p(g, 0, tiles[PAD])
                for k in range(U):
                    if not (first and k < 2):
                        scatter(g, k - 2, tiles[k])
                    if not (last and k + 1 >= U):
                        spread_p(g, k + 1, tiles[PAD + k + 1])
                    if not (last and k + 2 >= U):
                        turn_hot(g, k + 2)
                if last:
                    scatter(g, U - 2, tiles[U])
                    scatter(g, U - 1, tiles[U + 1])

            def pe_turns(first, last):
                turn_hot(first, 0)
                turn_hot(first, 1)
                pe_turn(first, first=True)
                start = loop_start(first, last)
                for g in range(first + 1, start):
                    pe_turn(g)
                with pe.Fori(start, last, TOGETHER) as g:
                    tiles = tiles_at(U * g - U, PAD + TOGETHER * U + 1)
                    for j in range(TOGETHER):
                        pe_turn(g + j, tiles=tiles[U * j:])
                pe_turn(last, last=True)

            pe_turns(1, FAST_TURNS)
            with pe.If(n_items > FAST_ITEMS):
                pe_turns(FAST_TURNS + 1, ALL_TURNS)
            mm(ps[:, 4, :], zeros[:, 0:128], zeros[:, :], False, True).then_inc(edges_done, 1)
            def turn_edge_sums(b):
                if b % 2:
                    pe.wait_ge(s_copied_a, b // 2 + 1)
                else:
                    pe.wait_ge(s_copied_v, b // 2 + 1)
                if b == 3:
                    pe.wait_ge(sT_copied_a, 1)
                elif b == 4:
                    pe.wait_ge(sT_copied_v, 1)
                for c in range(4):
                    last = nc.tensor.transpose(ps[:, sT_bank(b), c * NP:(c + 1) * NP], q_sb[0:NP, b, c * 128:(c + 1) * 128],
                                               ident[0:NP, 0:NP])
                last.then_inc(sT_done, 1)

            def edge_product(b):
                if b % 2:
                    pe.wait_ge(sT_copied_v, b // 2 + 1)
                else:
                    pe.wait_ge(sT_copied_a, b // 2 + 1)
                for c in range(4):
                    last = mm(ps[0:NP, b, 0:D], sT[:, b, c * NP:(c + 1) * NP], w2_sb[:, c, :], c == 0, c == 3)
                last.then_inc(conv_done, 1)

            pe.wait_ge(w2_loaded, 16)
            turn_edge_sums(0)
            turn_edge_sums(1)
            for b in range(NT):
                edge_product(b)
                if b + 2 < NT:
                    turn_edge_sums(b + 2)
            keep_busy(10, 7)
            turn(3, x1)
            turned(3)
            for b in range(NT):
                for c in range(DC):
                    last = mm(ps[0:NP, 3 + b, 0:WX], xT[:, c, b * NP:(b + 1) * NP], g3[:, c, :], c == 0, c == DC - 1)
                last.then_inc(xt_done, 1)
            pe.wait_ge(pool_step, 3 + NT)
            pe.wait_ge(al_copied, NT)
            pe.wait_ge(xt_split, NT)
            for b in range(NT):
                for n in range(NT):
                    for part in (xt_high, xt_low):
                        last = mm(ps[0:NP, 1 + b, 0:WX], e_hot[0:NP, n, b * NP:(b + 1) * NP], part[0:NP, n, :],
                                  n == 0 and part is xt_high, n == NT - 1 and part is xt_low)
                last.then_inc(xt_spread, 1)


_INS = ['x', 'src', 'dst', 'L0_gnn_W_l', 'L0_gnn_W_r', 'L0_gnn_b_r', 'L1_gnn_W', 'L1_gnn_att_src', 'L1_gnn_att_dst',
        'L1_gnn_bias', 'L1_gnn_ln_gamma', 'L1_gnn_ln_beta', 'L2_gnn_W1', 'L2_gnn_b1', 'L2_gnn_W2', 'L2_gnn_b2',
        'L3_gnn_weight', 'L3_gnn_attn_l', 'L3_gnn_attn_r']


def kernel(**inputs):
    import numpy as _np
    import concourse.bacc as _bacc
    from concourse import mybir as _mybir
    from concourse.bass_utils import run_bass_kernel_spmd as _run

    nc = _bacc.Bacc("TRN2", target_bir_lowering=False, num_devices=1)
    arrays, args = {}, []
    for name in _INS:
        a = _np.ascontiguousarray(inputs[name])
        arrays[f"in_{name}"] = a
        args.append(nc.dram_tensor(f"in_{name}", a.shape, _mybir.dt.from_np(a.dtype), kind="ExternalInput").ap())
    args.append(nc.dram_tensor("out_0", (N, D), _mybir.dt.float32, kind="ExternalOutput").ap())
    program(nc, *args)
    r = _run(nc, [arrays], core_ids=[0])
    return r.results[0]["out_0"]
```
